# Optimizing a Trainium2 kernel written in Bass

```python
import numpy as np
import jax
import jax.numpy as jnp

def _softmax(x, axis=-1):
    return jax.nn.softmax(x, axis=axis)

def _gelu(x):
    return jax.nn.gelu(x, approximate=True)

def _silu(x):
    return jax.nn.silu(x)

def _sigmoid(x):
    return jax.nn.sigmoid(x)

def _layernorm(x, axis=-1, eps=1e-05):
    m = jnp.mean(x, axis=axis, keepdims=True)
    v = jnp.var(x, axis=axis, keepdims=True)
    return (x - m) / jnp.sqrt(v + eps)

def _scatter_add(tgt, idx, src, axis=0):
    return tgt.at[idx].add(src)

def _segment_sum(src, seg, n):
    return jax.ops.segment_sum(src, seg, n)
kernel_name = 'mk_seq_preln_d2_jaxref_r4_c1d18b'

def setup_inputs(seed: int=0):
    np.random.seed(seed)
    _w = jnp.asarray

    def _L0_attn_setup():
        import jax, jax.numpy as jnp
        import numpy as np
        B, T, C, H = (2, 512, 256, 16)
        D = C // H

        def _alibi_slopes(n_heads):
            return 2.0 ** (-(8.0 / n_heads) * jnp.arange(1, n_heads + 1, dtype=jnp.float32))
        key = jax.random.key(seed)
        k1, k2, k3 = jax.random.split(key, 3)
        return {'x': jax.random.normal(k1, (B, T, C), dtype=jnp.float32), 'w_attn': jax.random.normal(k2, (C, 3 * C), dtype=jnp.float32) * 0.02, 'b_attn': jnp.zeros((3 * C,), dtype=jnp.float32), 'w_proj': jax.random.normal(k3, (C, C), dtype=jnp.float32) * 0.02, 'b_proj': jnp.zeros((C,), dtype=jnp.float32)}
    _L0_attn_in = _L0_attn_setup()

    def _L0_ffn_setup():
        import jax, jax.numpy as jnp
        import numpy as np
        B, S, D, H, E = (4, 512, 256, 16, 4)
        key = jax.random.key(seed)
        ks = jax.random.split(key, 8)
        w = lambda k, shape: jax.random.normal(k, shape, jnp.float32) * 0.02
        return {'x': jax.random.normal(ks[0], (B, S, D), jnp.float32), 'router_w': w(ks[1], (D, E)), 'router_b': jnp.zeros((E,), jnp.float32), 'wq': w(ks[2], (E, D, D)), 'bq': jnp.zeros((E, D), jnp.float32), 'wk': w(ks[3], (E, D, D)), 'bk': jnp.zeros((E, D), jnp.float32), 'wv': w(ks[4], (E, D, D)), 'bv': jnp.zeros((E, D), jnp.float32), 'wo': w(ks[5], (E, D, D)), 'bo': jnp.zeros((E, D), jnp.float32)}
    _L0_ffn_in = _L0_ffn_setup()

    def _L1_attn_setup():
        import jax, jax.numpy as jnp
        import numpy as np
        D_MODEL = 256
        N_HEADS = 16
        D_K = D_MODEL // N_HEADS
        THETA = 10000.0

        def _rope(x, pos):
            half = D_K // 2
            inv_freq = THETA ** (-jnp.arange(0, half, dtype=jnp.float32) * 2.0 / D_K)
            ang = pos[:, None].astype(jnp.float32) * inv_freq[None, :]
            cos, sin = (jnp.cos(ang), jnp.sin(ang))
            x1, x2 = (x[..., 0::2], x[..., 1::2])
            r1 = x1 * cos - x2 * sin
            r2 = x1 * sin + x2 * cos
            out = jnp.stack([r1, r2], axis=-1).reshape(x.shape)
            return out
        key = jax.random.key(seed)
        ks = jax.random.split(key, 5)
        b, s = (4, 512)
        sc = 1.0 / np.sqrt(D_MODEL)
        return {'x': jax.random.normal(ks[0], (b, s, D_MODEL), dtype=jnp.float32), 'Wq': jax.random.normal(ks[1], (D_MODEL, D_MODEL), dtype=jnp.float32) * sc, 'Wk': jax.random.normal(ks[2], (D_MODEL, D_MODEL), dtype=jnp.float32) * sc, 'Wv': jax.random.normal(ks[3], (D_MODEL, D_MODEL), dtype=jnp.float32) * sc, 'Wo': jax.random.normal(ks[4], (D_MODEL, D_MODEL), dtype=jnp.float32) * sc}
    _L1_attn_in = _L1_attn_setup()

    def _L1_ffn_setup():
        import jax, jax.numpy as jnp
        import numpy as np
        TOP_K = 8
        CAPACITY = 128

        def _silu(x):
            return x * jax.nn.sigmoid(x)
        key = jax.random.key(seed)
        ks = jax.random.split(key, 7)
        B, S, H, E, I, Is = (2, 256, 256, 64, 128, 512)
        s = 0.05
        return {'hidden_states': jax.random.normal(ks[0], (B, S, H), jnp.float32), 'gate_w': jax.random.normal(ks[1], (H, E), jnp.float32) * s, 'shared_gate_w': jax.random.normal(ks[2], (H, 1), jnp.float32) * s, 'shared_gate_up_w': jax.random.normal(ks[3], (H, 2 * Is), jnp.float32) * s, 'shared_down_w': jax.random.normal(ks[4], (Is, H), jnp.float32) * s, 'expert_gate_up_w': jax.random.normal(ks[5], (E, H, 2 * I), jnp.float32) * s, 'expert_down_w': jax.random.normal(ks[6], (E, I, H), jnp.float32) * s}
    _L1_ffn_in = _L1_ffn_setup()
    _d = {'L0_attn_x': _L0_attn_in['x'], 'L0_attn_w_attn': _L0_attn_in['w_attn'], 'L0_attn_b_attn': _L0_attn_in['b_attn'], 'L0_attn_w_proj': _L0_attn_in['w_proj'], 'L0_attn_b_proj': _L0_attn_in['b_proj'], 'L0_ffn_router_w': _L0_ffn_in['router_w'], 'L0_ffn_router_b': _L0_ffn_in['router_b'], 'L0_ffn_wq': _L0_ffn_in['wq'], 'L0_ffn_bq': _L0_ffn_in['bq'], 'L0_ffn_wk': _L0_ffn_in['wk'], 'L0_ffn_bk': _L0_ffn_in['bk'], 'L0_ffn_wv': _L0_ffn_in['wv'], 'L0_ffn_bv': _L0_ffn_in['bv'], 'L0_ffn_wo': _L0_ffn_in['wo'], 'L0_ffn_bo': _L0_ffn_in['bo'], 'L1_attn_Wq': _L1_attn_in['Wq'], 'L1_attn_Wk': _L1_attn_in['Wk'], 'L1_attn_Wv': _L1_attn_in['Wv'], 'L1_attn_Wo': _L1_attn_in['Wo'], 'L1_ffn_gate_w': _L1_ffn_in['gate_w'], 'L1_ffn_shared_gate_w': _L1_ffn_in['shared_gate_w'], 'L1_ffn_shared_gate_up_w': _L1_ffn_in['shared_gate_up_w'], 'L1_ffn_shared_down_w': _L1_ffn_in['shared_down_w'], 'L1_ffn_expert_gate_up_w': _L1_ffn_in['expert_gate_up_w'], 'L1_ffn_expert_down_w': _L1_ffn_in['expert_down_w']}
    _x0 = _d['L0_attn_x']
    _d['L0_attn_x'] = jax.random.normal(jax.random.fold_in(jax.random.key(seed), 1), (4, 1024, 256), dtype=_x0.dtype)
    del _x0
    return _d

def reference(L0_attn_x, L0_attn_w_attn, L0_attn_b_attn, L0_attn_w_proj, L0_attn_b_proj, L0_ffn_router_w, L0_ffn_router_b, L0_ffn_wq, L0_ffn_bq, L0_ffn_wk, L0_ffn_bk, L0_ffn_wv, L0_ffn_bv, L0_ffn_wo, L0_ffn_bo, L1_attn_Wq, L1_attn_Wk, L1_attn_Wv, L1_attn_Wo, L1_ffn_gate_w, L1_ffn_shared_gate_w, L1_ffn_shared_gate_up_w, L1_ffn_shared_down_w, L1_ffn_expert_gate_up_w, L1_ffn_expert_down_w):

    def _L0_attn_ref(x, w_attn, b_attn, w_proj, b_proj):
        import jax, jax.numpy as jnp
        import numpy as np
        B, T, C, H = (2, 512, 256, 16)
        D = C // H

        def _alibi_slopes(n_heads):
            return 2.0 ** (-(8.0 / n_heads) * jnp.arange(1, n_heads + 1, dtype=jnp.float32))
        b, t, c = x.shape
        qkv = (x @ w_attn + b_attn).reshape(b, t, 3, H, D).transpose(2, 0, 3, 1, 4)
        q, k, v = (qkv[0], qkv[1], qkv[2])
        scores = jnp.einsum('bhtd,bhsd->bhts', q, k) / jnp.sqrt(jnp.float32(D))
        slopes = _alibi_slopes(H)
        pos = jnp.arange(t, dtype=scores.dtype)
        scores = scores + slopes[None, :, None, None] * pos[None, None, None, :]
        causal = jnp.tril(jnp.ones((t, t), dtype=bool))
        scores = jnp.where(causal[None, None], scores, -jnp.inf)
        attn = jax.nn.softmax(scores, axis=-1)
        y = jnp.einsum('bhts,bhsd->bhtd', attn, v)
        y = y.transpose(0, 2, 1, 3).reshape(b, t, c)
        return y @ w_proj + b_proj

    def _L0_ffn_ref(x, router_w, router_b, wq, bq, wk, bk, wv, bv, wo, bo):
        import jax, jax.numpy as jnp
        import numpy as np
        B, S, D, H, E = (4, 512, 256, 16, 4)
        b, s, d = x.shape
        e_total = router_w.shape[-1]
        h = H
        hd = d // h
        sm_scale = 0.5
        logits = x @ router_w + router_b
        probs = jax.nn.softmax(logits, axis=-1)
        _, top2 = jax.lax.top_k(probs, 2)
        out = jnp.zeros_like(x)
        bidx = jnp.arange(b)[:, None]
        for e in range(e_total):
            member = (top2 == e).any(-1)
            w_tok = jnp.where(member, probs[..., e], 0.0)
            order = jnp.argsort((~member).astype(jnp.int32), axis=-1, stable=True)
            xg = jnp.take_along_axis(x, order[..., None], axis=1)
            validg = jnp.take_along_axis(member, order, axis=1)
            wg = jnp.take_along_axis(w_tok, order, axis=1)
            q = (xg @ wq[e] + bq[e]).reshape(b, s, h, hd)
            k = (xg @ wk[e] + bk[e]).reshape(b, s, h, hd)
            v = (xg @ wv[e] + bv[e]).reshape(b, s, h, hd)
            att = jnp.einsum('bqhd,bkhd->bhqk', q, k) * sm_scale
            att = jnp.where(validg[:, None, None, :], att, -1000000000.0)
            att = jax.nn.softmax(att, axis=-1)
            y = jnp.einsum('bhqk,bkhd->bqhd', att, v).reshape(b, s, d)
            y = y @ wo[e] + bo[e]
            out = out.at[bidx, order].add(wg[..., None] * y)
        return out

    def _L1_attn_ref(x, Wq, Wk, Wv, Wo):
        import jax, jax.numpy as jnp
        import numpy as np
        D_MODEL = 256
        N_HEADS = 16
        D_K = D_MODEL // N_HEADS
        THETA = 10000.0

        def _rope(x, pos):
            half = D_K // 2
            inv_freq = THETA ** (-jnp.arange(0, half, dtype=jnp.float32) * 2.0 / D_K)
            ang = pos[:, None].astype(jnp.float32) * inv_freq[None, :]
            cos, sin = (jnp.cos(ang), jnp.sin(ang))
            x1, x2 = (x[..., 0::2], x[..., 1::2])
            r1 = x1 * cos - x2 * sin
            r2 = x1 * sin + x2 * cos
            out = jnp.stack([r1, r2], axis=-1).reshape(x.shape)
            return out
        b, s, _ = x.shape
        pos = jnp.arange(s)

        def split_heads(t):
            return t.reshape(b, s, N_HEADS, D_K).transpose(0, 2, 1, 3).reshape(b * N_HEADS, s, D_K)
        q = split_heads(x @ Wq.T)
        k = split_heads(x @ Wk.T)
        v = split_heads(x @ Wv.T)
        q = _rope(q, pos)
        k = _rope(k, pos)
        score = jnp.einsum('bqd,bkd->bqk', q, k)
        causal = jnp.tril(jnp.ones((s, s), dtype=bool))
        score = jnp.where(causal[None], score, -jnp.inf)
        attn = jax.nn.softmax(score / jnp.sqrt(jnp.float32(D_K)), axis=-1)
        out = jnp.einsum('bqk,bkd->bqd', attn, v)
        out = out.reshape(b, N_HEADS, s, D_K).transpose(0, 2, 1, 3).reshape(b, s, D_MODEL)
        return out @ Wo.T

    def _L1_ffn_ref(hidden_states, gate_w, shared_gate_w, shared_gate_up_w, shared_down_w, expert_gate_up_w, expert_down_w):
        import jax, jax.numpy as jnp
        import numpy as np
        TOP_K = 8
        CAPACITY = 128

        def _silu(x):
            return x * jax.nn.sigmoid(x)
        B, S, H = hidden_states.shape
        x = hidden_states.reshape(-1, H)
        T = x.shape[0]
        E = gate_w.shape[1]
        Is = shared_gate_up_w.shape[1] // 2
        I = expert_gate_up_w.shape[2] // 2
        gu = x @ shared_gate_up_w
        shared = _silu(gu[:, :Is]) * gu[:, Is:] @ shared_down_w
        shared = shared * jax.nn.sigmoid(x @ shared_gate_w)
        logits = x @ gate_w
        probs = jax.nn.softmax(logits.astype(jnp.float32), axis=-1)
        w, idx = jax.lax.top_k(probs, TOP_K)
        w = (w / jnp.sum(w, axis=-1, keepdims=True)).astype(x.dtype)
        e_flat = idx.reshape(-1)
        w_flat = w.reshape(-1)
        A = e_flat.shape[0]
        tok = jnp.arange(A) // TOP_K
        onehot = jax.nn.one_hot(e_flat, E, dtype=jnp.int32)
        pos = jnp.take_along_axis(jnp.cumsum(onehot, axis=0) - 1, e_flat[:, None], axis=1)[:, 0]
        slot = jnp.minimum(pos, CAPACITY)
        buf = jnp.zeros((E, CAPACITY + 1, H), x.dtype).at[e_flat, slot].set(x[tok])
        gu_e = jnp.einsum('ech,ehf->ecf', buf, expert_gate_up_w)
        act = _silu(gu_e[..., :I]) * gu_e[..., I:]
        out_e = jnp.einsum('eci,eih->ech', act, expert_down_w)
        y = out_e[e_flat, slot] * w_flat[:, None]
        y = jnp.where((pos < CAPACITY)[:, None], y, jnp.zeros_like(y))
        y = y.reshape(T, TOP_K, H).sum(axis=1)
        return (y + shared).reshape(B, S, H)
    x = L0_attn_x
    x = x + _L0_attn_ref(_layernorm(x, axis=-1), L0_attn_w_attn, L0_attn_b_attn, L0_attn_w_proj, L0_attn_b_proj)
    x = x + _L0_ffn_ref(_layernorm(x, axis=-1), L0_ffn_router_w, L0_ffn_router_b, L0_ffn_wq, L0_ffn_bq, L0_ffn_wk, L0_ffn_bk, L0_ffn_wv, L0_ffn_bv, L0_ffn_wo, L0_ffn_bo)
    x = x + _L1_attn_ref(_layernorm(x, axis=-1), L1_attn_Wq, L1_attn_Wk, L1_attn_Wv, L1_attn_Wo)
    x = x + _L1_ffn_ref(_layernorm(x, axis=-1), L1_ffn_gate_w, L1_ffn_shared_gate_w, L1_ffn_shared_gate_up_w, L1_ffn_shared_down_w, L1_ffn_expert_gate_up_w, L1_ffn_expert_down_w)
    return x

_drawn_inputs = setup_inputs


def setup_inputs(seed=0):
    import zlib

    import numpy as np

    out = dict(_drawn_inputs(seed))
    spreads = {'L0_attn_b_attn': (0.0, 0.1),
     'L0_attn_b_proj': (0.0, 0.1),
     'L0_ffn_router_b': (0.0, 0.661),
     'L0_ffn_bq': (0.0, 0.8),
     'L0_ffn_bk': (0.0, 0.8),
     'L0_ffn_bv': (0.0, 0.444),
     'L0_ffn_bo': (0.0, 0.1)}
    factors = {'L0_ffn_wq': 8.0, 'L0_ffn_wk': 8.0, 'L0_ffn_wv': 6.811, 'L0_ffn_wo': 3.067}
    for name, (base, spread) in spreads.items():
        noise = np.random.default_rng([zlib.crc32(name.encode()), seed]).standard_normal(out[name].shape)
        drawn = base * np.exp(spread * noise) if base else spread * noise
        out[name] = jnp.asarray(drawn.astype(out[name].dtype))
    for name, factor in factors.items():
        out[name] = (out[name] * factor).astype(out[name].dtype)
    return out
```

```python
from contextlib import ExitStack

import numpy as np

import concourse.bass as bass
from concourse import mybir

ALU = mybir.AluOpType
ACT = mybir.ActivationFunctionType
AX = mybir.AxisListType
F32 = mybir.dt.float32
BF16 = mybir.dt.bfloat16
I32 = mybir.dt.int32

B, T, C, H, D = 4, 1024, 256, 16, 16
NT = T // 128
E0 = 4
UROWS = 1152
E1, I1, IS, CAP = 64, 128, 512, 128
NTOK = B * T
EPS = 1e-5
NEG = -1e30
ENGINES = ("pe", "act", "dve", "pool", "sp")
KA = 99
KB = 101


class Section:

    def __init__(self, sems, dma_sems):
        self.q = {k: [] for k in ENGINES}
        self.sems = sems
        self.count = {k: 0 for k in ENGINES}
        self.seen = {k: {} for k in ENGINES}
        self.dma_sems = dma_sems
        self.dma_n = {k: 0 for k in dma_sems}
        self.dma_val = {k: [0] * len(v) for k, v in dma_sems.items()}

    def wait(self, eng, *tokens):
        for tok in tokens:
            if tok is None:
                continue
            if not (isinstance(tok, tuple) and len(tok) == 2 and isinstance(tok[1], int)):
                self.wait(eng, *tok)
                continue
            sem, val = tok
            if self.seen[eng].get(sem.name, 0) >= val:
                continue
            self.seen[eng][sem.name] = val
            self.q[eng].append(lambda e, env, s=sem, v=val: e.wait_ge(s, v))

    def op(self, eng, fn, *waits, sig=True):
        self.wait(eng, *waits)
        if not sig:
            self.q[eng].append(fn)
            return None
        self.count[eng] += 1
        sem = self.sems[eng]
        self.q[eng].append(lambda e, env: fn(e, env).then_inc(sem, 1))
        return (sem, self.count[eng])

    def dma(self, eng, fn, *waits):
        pool = self.dma_sems[eng]
        i = self.dma_n[eng] % len(pool)
        self.dma_n[eng] += 1
        if self.dma_val[eng][i]:
            self.wait(eng, (pool[i], self.dma_val[eng][i]))
        self.wait(eng, *waits)
        self.dma_val[eng][i] += 16
        sem = pool[i]
        self.q[eng].append(lambda e, env: fn(e, env).then_inc(sem, 16))
        return (sem, self.dma_val[eng][i])

    def close(self):
        for eng, pool in self.dma_sems.items():
            for i, sem in enumerate(pool):
                if self.dma_val[eng][i]:
                    self.wait(eng, (sem, self.dma_val[eng][i]))
        return self


def chunks(a, b, step=512):
    out = []
    while a < b:
        c = min(b, (a // step + 1) * step)
        out.append((a, c))
        a = c
    return out


def build(nc, d, out):
    ctx = ExitStack()
    with ctx:
        def sb(name, shape, dt=F32):
            return ctx.enter_context(nc.sbuf_tensor(name, shape, dt))

        def sem(name):
            return ctx.enter_context(nc.semaphore(name))

        def dram(name, shape, dt=F32):
            return nc.dram_tensor(name, shape, dt, kind="Internal").ap()

        x1_d = dram("x1_d", (NTOK, C))
        xg_d = dram("xg_d", (B * E0 * UROWS, C))
        yg_d = dram("yg_d", (B * E0 * UROWS, C))
        rt_d = dram("rt_d", (B, 128, NT * 4))
        mk_d = dram("mk_d", (B * E0, T), BF16)
        cnt_d = dram("cnt_d", (B * E0, 1), I32)
        qk_d = [dram(f"qk_d{i}", (3, C, T), BF16) for i in range(2)]
        x3_d = dram("x3_d", (NTOK, C))
        xw_d = dram("xw_d", (NTOK + 128, C + E1))
        list_d = dram("list_d", (E1 * CAP, 1), I32)
        ye_d = [dram(f"ye_d{i}", (NTOK + 128, C)) for i in range(4)]

        ident = sb("ident", [128, 128])
        identb = sb("identb", [128, 128], BF16)
        ones = sb("ones", [128, 128])
        upper = sb("upper", [128, 128])
        maskA = sb("maskA", [128, 128], BF16)
        maskB = sb("maskB", [128, 128], BF16)
        iota = sb("iota", [1, T])
        e4 = sb("e4", [128, NT, E0])
        eoff = sb("eoff", [128, NT, E0])
        eoff1 = sb("eoff1", [128, NT, E1])
        tokid = sb("tokid", [128, NT])
        carry = sb("carry", [128, E1])
        base = sb("base", [128, 1])
        cnt = sb("cnt", [1, B * E0], I32)
        XR = sb("XR", [128, NT, C])
        XN = sb("XN", [128, NT, C])
        XT = sb("XT", [128, 2, T])
        W = sb("W", [128, 6, 2, C])
        bq = sb("bq", [128, 2, 2])
        bv = sb("bv", [128, C])
        bo = sb("bo", [128, C])
        rw = sb("rw", [128, 2, E1])
        rb = sb("rb", [128, E0])
        QF = sb("QF", [128, 2, T])
        PH = sb("PH", [128, 3, 2, T], BF16)
        QS = sb("QS", [KB, H, T], BF16)
        KS = sb("KS", [KB, H, T], BF16)
        VA = sb("VA", [128, NT, H, 32])
        PB = [sb(f"PB{i}", [128, T]) for i in range(8)]
        M1 = sb("M1", [128, 2, NT, 4])
        MHL = sb("MHL", [128, 2, NT, 8], BF16)
        MR = sb("MR", [8, T], BF16)
        RD = sb("RD", [128, NT, 4])
        bst = sb("bst", [128, NT, 6])
        mv = sb("mv", [128, NT, 2])
        rstd = sb("rstd", [128, NT])
        mhalf = sb("mhalf", [128, NT])
        Z = sb("Z", [128, C])
        ON = XN
        OT = QF[:, 0, :]
        cosT = PB[0]
        sinT = PB[1]
        sm = sb("sm", [128, 24, 32])
        smi = sb("smi", [128, 8, 32], I32)

        PA = ctx.enter_context(nc.psum_tensor("PA", [128, 1024], F32))
        PS = [ctx.enter_context(nc.psum_tensor(f"PS{i}", [128, 1024], F32)) for i in range(2)]
        PO = ctx.enter_context(nc.psum_tensor("PO", [128, 1024], F32))
        BANKS = [PA[:, 0:512], PA[:, 512:1024], PS[0][:, 0:512], PS[0][:, 512:1024],
                 PS[1][:, 0:512], PS[1][:, 512:1024], PO[:, 0:512], PO[:, 512:1024]]

        sems = {k: sem("s_" + k) for k in ENGINES}
        dma_sems = {"sp": [sem(f"d_sp{i}") for i in range(32)],
                    "pool": [sem(f"d_pool{i}") for i in range(16)]}
        A1, A2, B1, B2 = [sem(f"bar{i}") for i in range(4)]
        work = list(sems.values()) + dma_sems["sp"] + dma_sems["pool"]

        def new():
            return Section(sems, dma_sems)


        def load_w(S, i, ap, *waits):
            return S.dma("sp", lambda e, v: e.dma_start(
                W[:, i, :, :], ap(v).rearrange("(k p) n -> p k n", p=128)), *waits)

        def bcast_load(S, dst, ap, n, *waits):
            return S.dma("sp", lambda e, v: e.dma_start(dst, ap(v).to_broadcast([128, n])), *waits)

        def layernorm(S, src, tsrc, dst, nt, *free):
            t = []
            for i in range(nt):
                a = S.op("dve", lambda e, v, i=i: e.bn_stats(bst[:, i, :], src[:, i, :]), tsrc[i])
            for i in range(nt):
                a = S.op("dve", lambda e, v, i=i: e.bn_aggr(mv[:, i, :], bst[:, i, :]), a)
            a = S.op("dve", lambda e, v: e.tensor_scalar(rstd[:, 0:nt], mv[:, 0:nt, 1], EPS, None, ALU.add), a)
            p = S.op("pool", lambda e, v: e.tensor_tensor(
                rstd[:, 0:nt], rstd[:, 0:nt], mhalf[:, 0:nt], ALU.pow), a)
            for i in range(nt):
                t.append(S.op("dve", lambda e, v, i=i: e.tensor_scalar(
                    dst[:, i, :], src[:, i, :], mv[:, i, 0:1], rstd[:, i:i + 1],
                    ALU.subtract, ALU.mult), a, p, *free))
            return t

        def transposes(S, src, tsrc, nt, *free):
            toks = []
            n = 0
            users = [None] * 4
            for c0 in range(0, nt, 4):
                w = min(4, nt - c0)
                for k in range(2):
                    bank = BANKS[n % 4]
                    for i in range(w):
                        a = S.op("pe", lambda e, v, i=i, k=k, c0=c0, bank=bank: e.transpose(
                            bank[:, 128 * i:128 * i + 128], src[:, c0 + i, 128 * k:128 * k + 128],
                            ident[:, :]), tsrc[c0 + i], users[n % 4], sig=(i == w - 1))
                    eng = "dve" if n % 2 else "act"

                    def ev(e, v, k=k, c0=c0, w=w, bank=bank, eng=eng):
                        o = XT[:, k, 128 * c0:128 * (c0 + w)]
                        return (e.tensor_copy(o, bank[:, 0:128 * w]) if eng == "dve"
                                else e.activation(o, bank[:, 0:128 * w], ACT.Copy))
                    users[n % 4] = S.op(eng, ev, a, *free)
                    toks.append(users[n % 4])
                    n += 1
            return toks

        def project_qk(S, nt, txt, wtok, bias, rope, kadd):
            n = 128 * nt
            done = []
            last_ph = None
            last_qf = None
            users = [None] * 8
            nb = 0
            stores = []
            for qk in range(2):
                for g in range(2):
                    evs = []
                    for (a, b) in chunks(0, n):
                        m = b - a
                        if not rope:
                            bank = BANKS[nb % 8]
                            for k in range(2):
                                mm = S.op("pe", lambda e, v, k=k, g=g, qk=qk, a=a, b=b, bank=bank: e.matmul(
                                    bank[:, 0:b - a], W[:, qk, k, 128 * g:128 * g + 128],
                                    XT[:, k, a:b], start=(k == 0), stop=(k == 1)),
                                    txt, wtok, users[nb % 8], sig=(k == 1))
                            def f1(e, v, o=QF[:, g, a:b], i=bank[:, 0:m], g=g, qk=qk):
                                if bias:
                                    return e.activation(o, i, ACT.Identity, bias=bq[:, qk, g:g + 1])
                                return e.activation(o, i, ACT.Copy)
                            t1 = S.op("act", f1, mm, last_qf)
                            users[nb % 8] = t1
                            nb += 1
                        else:
                            b0, b1 = BANKS[nb % 8], BANKS[(nb + 1) % 8]
                            for bank, wi in ((b0, qk), (b1, qk + 4)):
                                for k in range(2):
                                    mm = S.op("pe", lambda e, v, k=k, g=g, wi=wi, a=a, b=b, bank=bank: e.matmul(
                                        bank[:, 0:b - a], W[:, wi, k, 128 * g:128 * g + 128],
                                        XT[:, k, a:b], start=(k == 0), stop=(k == 1)),
                                        txt, wtok, users[nb % 8], users[(nb + 1) % 8], sig=(k == 1))
                            t1 = S.op("dve", lambda e, v, o=QF[:, g, a:b], i=b0[:, 0:m], c=cosT[:, a:b]:
                                      e.tensor_tensor(o, i, c, ALU.mult), mm, last_qf, rope)
                            t2 = S.op("dve", lambda e, v, o=PB[2][:, a:b], i=b1[:, 0:m], c=sinT[:, a:b]:
                                      e.tensor_tensor(o, i, c, ALU.mult), mm, rope)
                            t1 = S.op("dve", lambda e, v, o=QF[:, g, a:b], i=PB[2][:, a:b]:
                                      e.tensor_tensor(o, o, i, ALU.add), t2)
                            users[nb % 8] = users[(nb + 1) % 8] = t2
                            nb += 2
                        evs.append(t1)
                    f = QF[:, g, 0:n]
                    ph = [PH[:, p, g, 0:n] for p in range(3)]
                    th = S.op("act", lambda e, v, o=ph[0], i=f: e.activation(o, i, ACT.Copy), evs, last_ph)
                    tr = S.op("dve", lambda e, v, o=f, i=ph[0]: e.tensor_tensor(o, o, i, ALU.subtract), evs, th)
                    tm = S.op("dve", lambda e, v, o=ph[1], i=f: e.tensor_copy(o, i), tr, last_ph)
                    tl = S.op("dve", lambda e, v, o=ph[2], i=f, j=ph[1]: e.tensor_tensor(o, i, j, ALU.subtract), tm)
                    for p, tt in ((0, th), (1, tm), (2, tl)):
                        stores.append(S.dma("sp", lambda e, v, p=p, g=g, qk=qk: e.dma_start(
                            qk_d[qk][p, 128 * g:128 * g + 128, 0:n], PH[:, p, g, 0:n]), tt))
                last_ph = stores[-6:]
                last_qf = tl
                parts = (0, 1, 2, 0, 1, 0) if qk == 0 else (0, 0, 0, 1, 1, 2)
                dst = QS if qk == 0 else KS
                for s, p in enumerate(parts):
                    done.append(S.dma("sp", lambda e, v, s=s, p=p, dst=dst, qk=qk: e.dma_start(
                        dst[16 * s:16 * s + 16, :, 0:n],
                        qk_d[qk][p, :, 0:n].rearrange("(h d) n -> d h n", d=16)), stores[-6:]))
            done.append(kadd(S))
            return done

        def project_v(S, nt, txt, wtok, bias, *free):
            toks = []
            for t in range(nt):
                bank = BANKS[t % 8]
                for k in range(2):
                    mm = S.op("pe", lambda e, v, k=k, t=t, bank=bank: e.matmul(
                        bank[:, 0:C], XT[:, k, 128 * t:128 * t + 128], W[:, 2, k, :],
                        start=(k == 0), stop=(k == 1)), txt, wtok, free, sig=(k == 1))
                def ev(e, v, t=t, bank=bank):
                    o = VA[:, t, :, 0:16]
                    i = bank[:, 0:C].rearrange("p (h d) -> p h d", d=16)
                    if bias:
                        return e.tensor_tensor(o, i, bv[:, :].rearrange("p (h d) -> p h d", d=16), ALU.add)
                    return e.tensor_copy(o, i)
                toks.append(S.op("dve", ev, mm))
            return toks

        def attend(S, nt, causal, scale, tqk, tv, *free):
            n = 128 * nt
            nsl = 4 * nt
            total = 4 * nsl
            lead = min(nsl + 6, total)
            st = {"pa": free[0], "po": free[0], "ps": [free[0], free[0]], "pb": [free[0]] * 8,
                  "m1": {}, "mr": None, "pv": None, "qsm": {}, "ot": None}

            def krange(qt):
                return 128 * (qt + 1) if causal else n

            def pass1(i):
                g, r = divmod(i, nsl)
                qt, j = divmod(r, 4)
                h = 4 * g + j
                kn = krange(qt)
                cs = chunks(0, kn)
                for (a, b) in cs:
                    diag = causal and b == kn
                    mm = S.op("pe", lambda e, v, a=a, b=b, h=h, qt=qt, diag=diag: e.matmul(
                        PA[:, a:b], QS[0:KA, h, 128 * qt:128 * qt + 128], KS[0:KA, h, a:b],
                        start=True, stop=not diag, skip_group_check=diag), tqk, st["pa"],
                        sig=(b == kn and not diag))
                if causal:
                    mm = S.op("pe", lambda e, v, kn=kn: e.matmul(
                        PA[:, kn - 128:kn], identb[:, :], maskA[:, :], start=False, stop=True,
                        skip_group_check=True))
                st["pa"] = S.op("dve", lambda e, v, g=g, qt=qt, j=j, kn=kn: e.tensor_reduce(
                    M1[:, g % 2, qt, j:j + 1], PA[:, 0:kn], AX.X, ALU.max), mm)
                if r == nsl - 1:
                    m_rows(g)

            def m_rows(g):
                m1 = M1[:, g % 2, 0:nt, :]
                hi = MHL[:, g % 2, 0:nt, 0:4]
                lo = MHL[:, g % 2, 0:nt, 4:8]
                a = S.op("dve", lambda e, v: e.tensor_scalar(hi, m1, -1.0, None, ALU.mult), st["pa"],
                         st["m1"].get(g - 2))
                a = S.op("dve", lambda e, v: e.scalar_tensor_tensor(
                    lo, m1, -1.0, hi, ALU.mult, ALU.subtract), a)
                for t in range(nt):
                    mm = S.op("pe", lambda e, v, t=t: e.matmul(
                        PA[0:8, 128 * t:128 * t + 128], MHL[:, g % 2, t, :], identb[:, :],
                        start=True, stop=True), a, sig=(t == nt - 1))
                st["m1"][g] = mm
                c = S.op("dve", lambda e, v: e.tensor_copy(MR[:, 0:n], PA[0:8, 0:n]), mm, st["mr"])
                st["pa"] = c
                ds = []
                for r in range(2):
                    ds.append(S.dma("sp", lambda e, v, r=r: e.dma_start(
                        QS[KA + r:KA + r + 1, 4 * g:4 * g + 4, 0:n], MR[4 * r:4 * r + 4, 0:n]), c))
                st["mr"] = ds
                st["qsm"][g] = ds

            def pass2(i):
                g, r = divmod(i, nsl)
                kt, j = divmod(r, 4)
                h = 4 * g + j
                q0 = 128 * kt if causal else 0
                s = PS[i % 2]
                cs = chunks(q0, n)
                for (a, b) in cs:
                    fin = b == n
                    diag = causal and a == q0
                    mm = S.op("pe", lambda e, v, a=a, b=b, h=h, kt=kt, diag=diag: e.matmul(
                        s[:, a:b], KS[0:KB, h, 128 * kt:128 * kt + 128], QS[0:KB, h, a:b],
                        start=True, stop=not diag, skip_group_check=diag), tqk, st["qsm"][g],
                        st["ps"][i % 2], sig=(fin and not causal))
                if causal:
                    mm = S.op("pe", lambda e, v: e.matmul(
                        s[:, q0:q0 + 128], identb[:, :], maskB[:, :], start=False, stop=True,
                        skip_group_check=True))
                pb = ((g * nt + kt) % 2) * 4 + j
                t = S.op("act", lambda e, v: e.activation(
                    PB[pb][:, q0:n], s[:, q0:n], ACT.Exp, scale=scale), mm, st["pb"][pb])
                st["ps"][i % 2] = t
                st[("p", g, kt, j)] = t

            def pv(g, kt):
                q0 = 128 * kt if causal else 0
                for (a, b) in chunks(q0, n):
                    for j in range(4):
                        pb = ((g * nt + kt) % 2) * 4 + j
                        fin = b == n and j == 3
                        mm = S.op("pe", lambda e, v, a=a, b=b, j=j, pb=pb: e.matmul(
                            PO[32 * j:32 * j + 32, a:b], VA[:, kt, 4 * g + j, :], PB[pb][:, a:b],
                            start=(kt == 0), stop=(kt == nt - 1), skip_group_check=True),
                            st[("p", g, kt, j)], tv, st["po"] if kt == 0 else None, sig=fin)
                for j in range(4):
                    st["pb"][((g * nt + kt) % 2) * 4 + j] = mm
                if kt == nt - 1:
                    c = S.op("act", lambda e, v: e.activation(OT[:, 0:n], PO[:, 0:n], ACT.Copy),
                             mm, st["ot"])
                    st["po"] = c
                    st[("norm", g)] = c

            def norm(g):
                for t in range(nt):
                    mm = S.op("pe", lambda e, v, t=t: e.transpose(
                        PA[:, 128 * t:128 * t + 128], OT[:, 128 * t:128 * t + 128], ident[:, :]),
                        st[("norm", g)], st["pa"], sig=(t == nt - 1))
                st["ot"] = mm
                view = PA[:, 0:n].rearrange("p (t j d) -> p t j d", j=4, d=32)
                r = S.op("dve", lambda e, v: e.reciprocal(RD[:, 0:nt, :], view[:, :, :, 16]), mm,
                         st.get("rd"))
                for j in range(4):
                    m = S.op("dve", lambda e, v, j=j: e.tensor_tensor(
                        ON[:, 0:nt, 64 * g + 16 * j:64 * g + 16 * j + 16], view[:, :, j, 0:16],
                        RD[:, 0:nt, j:j + 1].to_broadcast([128, nt, 16]), ALU.mult), r, mm)
                st["pa"] = m
                st["rd"] = m
                return m

            pending = []
            for i in range(-lead, total + 8):
                if 0 <= i + lead < total:
                    pass1(i + lead)
                if 0 <= i < total:
                    pass2(i)
                for item in list(pending):
                    if item[0] <= i:
                        pending.remove(item)
                        if item[1] == "pv":
                            pv(item[2], item[3])
                            if item[3] == nt - 1:
                                pending.append((i + 2, "norm", item[2]))
                        else:
                            last = norm(item[2])
                if 0 <= i < total and i % 4 == 3:
                    g, r = divmod(i, nsl)
                    pending.append((i + 2, "pv", g, r // 4))
            while pending:
                item = pending.pop(0)
                if item[1] == "pv":
                    pv(item[2], item[3])
                    if item[3] == nt - 1:
                        pending.append((0, "norm", item[2]))
                else:
                    last = norm(item[2])
            return last

        def project_out(S, nt, txt, wtok, write, *free):
            toks = []
            users = [None] * 8
            for t in range(nt):
                bank = BANKS[t % 8]
                for k in range(2):
                    mm = S.op("pe", lambda e, v, k=k, t=t, bank=bank: e.matmul(
                        bank[:, 0:C], XT[:, k, 128 * t:128 * t + 128], W[:, 3, k, :],
                        start=(k == 0), stop=(k == 1)), txt, wtok, free, users[t % 8], sig=(k == 1))
                users[t % 8] = write(S, t, bank[:, 0:C], mm)
                toks.append(users[t % 8])
            return toks

        def row(v):
            return bass.ds(v, 1)


        def constants():
            S = new()
            for dst, name in ((ident, "c_ident"), (ones, "c_ones"), (upper, "c_upper"), (iota, "c_iota"),
                              (identb, "c_identb"), (maskA, "c_maskA"), (maskB, "c_maskB")):
                S.dma("sp", lambda e, v, dst=dst, name=name: e.dma_start(dst[:, :], d[name]))
            for dst, name in ((e4, "c_e4"), (eoff, "c_eoff"), (eoff1, "c_eoff1")):
                S.dma("sp", lambda e, v, dst=dst, name=name: e.dma_start(
                    dst[:, :, :], d[name].rearrange("p (t e) -> p t e", t=NT)))
            S.dma("sp", lambda e, v: e.dma_start(tokid[:, :], d["c_tokid"]))
            S.dma("sp", lambda e, v: e.dma_start(list_d, d["c_list"]))
            S.op("dve", lambda e, v: e.memset(carry[:, :], 0.0))
            S.op("dve", lambda e, v: e.memset(base[:, :], 0.0))
            S.op("dve", lambda e, v: e.memset(mhalf[:, :], -0.5))
            S.op("dve", lambda e, v: e.memset(Z[:, :], 0.0))
            S.op("dve", lambda e, v: e.memset(QS[96:KB, :, :], 1.0))
            S.op("dve", lambda e, v: e.memset(KS[96:KB, :, :], 1.0))
            S.op("pool", lambda e, v: e.memset(VA[:, :, :, :], 1.0))
            z = S.op("dve", lambda e, v: e.memset(XR[:, :, :], 0.0))
            for i in range(4):
                for b in range(4):
                    S.dma("sp", lambda e, v, i=i, b=b: e.dma_start(
                        ye_d[i][1024 * b:1024 * b + 1024, :].rearrange("(t p) c -> p t c", p=128),
                        XR[:, :, :]), z)
                S.dma("sp", lambda e, v, i=i: e.dma_start(ye_d[i][NTOK:NTOK + 128, :], XR[:, 0, :]), z)
            S.dma("sp", lambda e, v: e.dma_start(
                xw_d[NTOK:NTOK + 128, :], XR[:, 0:2, :].rearrange("p t c -> p (t c)")[:, 0:C + E1]), z)
            for i in range(3):
                load_w(S, i, lambda v, i=i: d["L0_attn_w_attn"][:, 256 * i:256 * i + 256])
            load_w(S, 3, lambda v: d["L0_attn_w_proj"])
            ba = d["L0_attn_b_attn"]
            for qk in range(2):
                S.dma("sp", lambda e, v, qk=qk: e.dma_start(
                    bq[:, qk, :], ba[256 * qk:256 * qk + 256].rearrange("(g p) -> p g", p=128),
                    allow_slow_non_contiguous=True))
            S.dma("sp", lambda e, v: e.dma_start(bv[:, :], ba[512:768].partition_broadcast(128)))
            S.dma("sp", lambda e, v: e.dma_start(bo[:, :], d["L0_attn_b_proj"].partition_broadcast(128)))
            S.dma("sp", lambda e, v: e.dma_start(rb[:, :], d["L0_ffn_router_b"].partition_broadcast(128)))
            S.dma("sp", lambda e, v: e.dma_start(
                rw[:, :, 0:E0], d["L0_ffn_router_w"].rearrange("(k p) n -> p k n", p=128)))
            return S.close()

        def tokens3(ap, b):
            return ap.rearrange("(b t p) c -> b p t c", b=B, p=128)[row(b), :, :, :].rearrange(
                "o p t c -> (o p) t c")

        def l0_attn():
            S = new()
            ld = S.dma("sp", lambda e, v: e.dma_start(XR[:, :, :], tokens3(d["L0_attn_x"], v["b"])))
            for ex in range(E0):
                S.dma("sp", lambda e, v, ex=ex: e.dma_start(
                    yg_d.rearrange("(u s p) c -> u p s c", u=B * E0, p=128)[
                        row(v["b"] * E0 + ex), :, :, :].rearrange("o p s c -> (o p) s c"),
                    Z[:, :].rearrange("p (o c) -> p o c", o=1).to_broadcast([128, UROWS // 128, C])))
            tln = layernorm(S, XR, [ld] * NT, XN, NT)
            txt = transposes(S, XN, tln, NT)
            tqk = project_qk(S, NT, txt, None, True, None, lambda S: S.dma(
                "sp", lambda e, v: e.dma_start(KS[96:99, :, :], d["c_alibi"])))
            tv = project_v(S, NT, txt, None, True, tqk)
            last = attend(S, NT, True, 0.25, tqk, tv, tv)
            txt = transposes(S, ON, [last] * NT, NT)

            def write(S, t, ps, mm):
                a = S.op("dve", lambda e, v: e.tensor_tensor(XR[:, t, :], ps, XR[:, t, :], ALU.add), mm)
                return S.op("dve", lambda e, v: e.tensor_tensor(XR[:, t, :], XR[:, t, :], bo[:, :], ALU.add), a)
            to = project_out(S, NT, txt, None, write)
            S.dma("sp", lambda e, v: e.dma_start(tokens3(x1_d, v["b"]), XR[:, :, :]), to)
            tln = layernorm(S, XR, to, XN, NT, txt)
            txt = transposes(S, XN, tln, NT, to)
            route0(S, tln, txt)
            return S.close()

        def route0(S, tln, txt):
            lg = PA[:, 0:32].rearrange("p (t e) -> p t e", e=E0)
            for t in range(NT):
                for k in range(2):
                    mm = S.op("pe", lambda e, v, t=t, k=k: e.matmul(
                        PA[:, 4 * t:4 * t + 4], XT[:, k, 128 * t:128 * t + 128], rw[:, k, 0:E0],
                        start=(k == 0), stop=(k == 1)), txt, sig=(t == NT - 1 and k == 1))
            names = ["L", "t1", "oh1", "L2", "t2", "oh2", "ex", "mask", "pre", "pos", "tmp", "tot"]
            R = {nm: sm[:, i, :].rearrange("p (t e) -> p t e", e=E0) for i, nm in enumerate(names)}
            V = {nm: sm[:, 12 + i, 0:NT] for i, nm in enumerate(["m1", "x1", "m2", "x2", "s", "w1", "w2", "d1", "d2"])}
            out4 = sm[:, 22, :].rearrange("p (t e) -> p t e", e=4)

            def bc(ap):
                return ap.rearrange("p (t o) -> p t o", o=1).to_broadcast([128, NT, E0])

            def dv(fn, *w):
                dv.t = S.op("dve", fn, dv.t, *w)
                return dv.t
            dv.t = None
            dv(lambda e, v: e.tensor_tensor(R["L"], lg, rb[:, :].rearrange("p (o e) -> p o e", o=1).to_broadcast([128, NT, E0]), ALU.add), mm)
            lt = dv.t
            dv(lambda e, v: e.tensor_reduce(V["m1"], R["L"], AX.X, ALU.max))
            dv(lambda e, v: e.tensor_tensor(R["t1"], R["L"], bc(V["m1"]), ALU.is_equal))
            dv(lambda e, v: e.tensor_tensor(R["t1"], R["t1"], e4[:, :, :], ALU.mult))
            dv(lambda e, v: e.tensor_reduce(V["x1"], R["t1"], AX.X, ALU.max))
            dv(lambda e, v: e.tensor_tensor(R["oh1"], R["t1"], bc(V["x1"]), ALU.is_equal))
            dv(lambda e, v: e.scalar_tensor_tensor(R["L2"], R["oh1"], NEG, R["L"], ALU.mult, ALU.add))
            dv(lambda e, v: e.tensor_reduce(V["m2"], R["L2"], AX.X, ALU.max))
            dv(lambda e, v: e.tensor_tensor(R["t2"], R["L2"], bc(V["m2"]), ALU.is_equal))
            dv(lambda e, v: e.tensor_tensor(R["t2"], R["t2"], e4[:, :, :], ALU.mult))
            dv(lambda e, v: e.tensor_reduce(V["x2"], R["t2"], AX.X, ALU.max))
            dv(lambda e, v: e.tensor_tensor(R["oh2"], R["t2"], bc(V["x2"]), ALU.is_equal))
            dv(lambda e, v: e.tensor_tensor(R["mask"], R["oh1"], R["oh2"], ALU.add))
            tm = dv.t
            dv(lambda e, v: e.tensor_tensor(R["ex"], R["L"], bc(V["m1"]), ALU.subtract))
            ta = S.op("act", lambda e, v: e.activation(R["ex"], R["ex"], ACT.Exp), dv.t)
            dv(lambda e, v: e.tensor_reduce(V["s"], R["ex"], AX.X, ALU.add), ta)
            dv(lambda e, v: e.reciprocal(V["s"], V["s"]))
            dv(lambda e, v: e.tensor_tensor(R["ex"], R["ex"], bc(V["s"]), ALU.mult))
            dv(lambda e, v: e.tensor_tensor(R["tmp"], R["ex"], R["oh1"], ALU.mult))
            dv(lambda e, v: e.tensor_reduce(out4[:, :, 2], R["tmp"], AX.X, ALU.add))
            dv(lambda e, v: e.tensor_tensor(R["tmp"], R["ex"], R["oh2"], ALU.mult))
            dv(lambda e, v: e.tensor_reduce(out4[:, :, 3], R["tmp"], AX.X, ALU.add))
            p0, p1 = PS[0][:, 0:32], PS[1][:, 0:32]
            S.op("pe", lambda e, v: e.matmul(p0, upper[:, :], sm[:, 7, :], start=True, stop=True), tm, sig=False)
            mm = S.op("pe", lambda e, v: e.matmul(p1, ones[:, :], sm[:, 7, :], start=True, stop=True))
            dv(lambda e, v: e.tensor_copy(sm[:, 11, :], p1), mm)
            dv(lambda e, v: e.memset(R["pre"][:, 0, :], 0.0))
            for t in range(1, NT):
                dv(lambda e, v, t=t: e.tensor_tensor(
                    R["pre"][:, t, :], R["pre"][:, t - 1, :], R["tot"][:, t - 1, :], ALU.add))
            nf = sm[:, 21, 0:E0]
            dv(lambda e, v: e.tensor_tensor(nf, R["pre"][:, NT - 1, :], R["tot"][:, NT - 1, :], ALU.add))
            tn = dv.t
            dv(lambda e, v: e.tensor_tensor(sm[:, 9, :], p0, sm[:, 8, :], ALU.add))
            dv(lambda e, v: e.tensor_tensor(R["pos"], R["pos"], eoff[:, :, :], ALU.add))
            di = smi[:, 0, 0:16].rearrange("p (t k) -> p t k", k=2)
            for k, oh in ((0, "oh1"), (1, "oh2")):
                dd = V["d1"] if k == 0 else V["d2"]
                dv(lambda e, v, oh=oh: e.tensor_tensor(R["tmp"], R["pos"], R[oh], ALU.mult))
                dv(lambda e, v, dd=dd: e.tensor_reduce(dd, R["tmp"], AX.X, ALU.add))
                dv(lambda e, v, dd=dd: e.tensor_scalar(dd, dd, base[:, 0:1], None, ALU.add))
                dv(lambda e, v, dd=dd, k=k: e.tensor_copy(di[:, :, k], dd))
                dv(lambda e, v, k=k: e.tensor_copy(out4.bitcast(I32)[:, :, k], di[:, :, k]))
            ti = dv.t
            dv(lambda e, v: e.tensor_scalar(base[:, :], base[:, :], float(E0 * UROWS), None, ALU.add))
            ni = smi[0:1, 2, 0:E0]
            tcn = smi[0:1, 3, 0:E0]
            dv(lambda e, v: e.tensor_copy(ni, nf[0:1, :]))
            dv(lambda e, v: e.tensor_scalar(sm[0:1, 23, 0:E0], nf[0:1, :], 127.0, None, ALU.add))
            dv(lambda e, v: e.tensor_copy(tcn, sm[0:1, 23, 0:E0]))
            dv(lambda e, v: e.tensor_scalar(tcn, tcn, 7, None, ALU.logical_shift_right))
            tc_ = dv.t
            mkb = PH[0:1, :, :, :].rearrange("p a b n -> p (a b) n")
            for ex in range(E0):
                dv(lambda e, v, ex=ex: e.tensor_scalar(
                    mkb[:, ex, :], iota[0:1, :], nf[0:1, ex:ex + 1], NEG, ALU.is_ge, ALU.mult))
            for ex in range(E0):
                S.dma("sp", lambda e, v, ex=ex: e.dma_start(mk_d[row(v["b"] * E0 + ex), :], mkb[:, ex, :]), dv.t)
                S.dma("sp", lambda e, v, ex=ex: e.dma_start(cnt_d[row(v["b"] * E0 + ex), :], tcn[:, ex:ex + 1]), tc_)
            S.dma("sp", lambda e, v: e.dma_start(rt_d[row(v["b"]), :, :].rearrange("o p n -> (o p) n"), sm[:, 22, :]), ti)
            for t in range(NT):
                for k in range(2):
                    S.dma("pool", lambda e, v, t=t, k=k: e.indirect_dma_start(
                        out=xg_d, out_offset=bass.IndirectOffsetOnAxis(ap=di[:, t, k:k + 1], axis=0),
                        in_=XN[:, t, :], in_offset=None), ti, tln)
            zt = S.op("dve", lambda e, v: e.memset(PB[0][:, 0:C], 0.0))
            for ex in range(E0):
                def pad(e, v, ex=ex):
                    r = e.value_load(ni[0:1, ex:ex + 1], min_val=0, max_val=T)
                    return e.dma_start(xg_d[bass.ds(r + (v["b"] * E0 + ex) * UROWS, 128), :], PB[0][:, 0:C])
                S.dma("sp", pad, zt, tc_)

        def pre_ffn():
            S = new()
            z = S.op("dve", lambda e, v: e.memset(KS[96:99, :, :], 0.0))
            S.dma("sp", lambda e, v: e.dma_start(cnt[:, :], cnt_d.rearrange("a o -> o a"),
                                                 allow_slow_non_contiguous=True))
            return S.close()

        def ffn_unit(nt):
            S = new()
            n = 128 * nt
            lds = []
            for t in range(nt):
                lds.append(S.dma("sp", lambda e, v, t=t: e.dma_start(
                    XN[:, t, :], xg_d[bass.ds(v["u"] * UROWS + 128 * t, 128), :])))
            wt = []
            for i, nm in enumerate(("wq", "wk", "wv", "wo")):
                wt.append(load_w(S, i, lambda v, nm=nm: d["L0_ffn_" + nm][row(v["ex"]), :, :].rearrange("o a b -> (o a) b")))
            for qk, nm in enumerate(("bq", "bk")):
                wt.append(S.dma("sp", lambda e, v, qk=qk, nm=nm: e.dma_start(
                    bq[:, qk, :], d["L0_ffn_" + nm][row(v["ex"]), :].rearrange("o (g p) -> p (o g)", p=128),
                    allow_slow_non_contiguous=True)))
            for dst, nm in ((bv, "bv"), (bo, "bo")):
                wt.append(S.dma("sp", lambda e, v, dst=dst, nm=nm: e.dma_start(
                    dst[:, :], d["L0_ffn_" + nm][row(v["ex"]), :].to_broadcast([128, C]))))
            txt = transposes(S, XN, lds, nt)
            tqk = project_qk(S, nt, txt, wt, True, None, lambda S: S.dma(
                "sp", lambda e, v: e.dma_start(
                    KS[96:97, :, 0:n],
                    mk_d[row(v["u"]), 0:n].rearrange("o (h n) -> o h n", h=1).to_broadcast([1, H, n]))))
            tv = project_v(S, nt, txt, wt, True, tqk)
            last = attend(S, nt, False, 0.5, tqk, tv, tv)
            txt = transposes(S, ON, [last] * nt, nt)

            def write(S, t, ps, mm):
                return S.op("dve", lambda e, v: e.tensor_tensor(XR[:, t, :], ps, bo[:, :], ALU.add), mm)
            to = project_out(S, nt, txt, wt, write)
            for t in range(nt):
                S.dma("sp", lambda e, v, t=t: e.dma_start(
                    yg_d[bass.ds(v["u"] * UROWS + 128 * t, 128), :], XR[:, t, :]), to[t])
            return S.close()

        def pre_l1():
            S = new()
            z = S.op("dve", lambda e, v: e.memset(KS[96:99, :, :], 0.0))
            for i, nm in enumerate(("w1_q", "w1_k", "w1_v", "w1_o", "w1_qs", "w1_ks")):
                load_w(S, i, lambda v, nm=nm: d[nm])
            S.dma("sp", lambda e, v: e.dma_start(rw[:, :, :], d["L1_ffn_gate_w"].rearrange("(k p) n -> p k n", p=128)))
            return S.close()

        def l1_attn():
            S = new()
            ld = S.dma("sp", lambda e, v: e.dma_start(XR[:, :, :], tokens3(x1_d, v["b"])))
            lr = S.dma("sp", lambda e, v: e.dma_start(
                sm[:, 22, :], rt_d[row(v["b"]), :, :].rearrange("o p n -> (o p) n")))
            out4 = sm[:, 22, :].rearrange("p (t e) -> p t e", e=4)
            di = smi[:, 0, 0:16].rearrange("p (t k) -> p t k", k=2)
            ti = S.op("dve", lambda e, v: e.tensor_copy(di, out4.bitcast(I32)[:, :, 0:2]), lr)
            gs, tx = [], []
            for t in range(NT):
                for k in range(2):
                    g = S.dma("pool", lambda e, v, t=t, k=k: e.indirect_dma_start(
                        out=PB[t][:, 256 * k:256 * k + 256], out_offset=None, in_=yg_d,
                        in_offset=bass.IndirectOffsetOnAxis(ap=di[:, t, k:k + 1], axis=0)), ti)
                    gs.append(g)
            for t in range(NT):
                a = None
                for k in range(2):
                    a = S.op("dve", lambda e, v, t=t, k=k: e.scalar_tensor_tensor(
                        XR[:, t, :], PB[t][:, 256 * k:256 * k + 256], out4[:, t, 2 + k:3 + k], XR[:, t, :],
                        ALU.mult, ALU.add), gs[2 * t + k], ld, lr, a)
                tx.append(a)
            tln = layernorm(S, XR, tx, XN, NT)
            tc = [S.dma("sp", lambda e, v: e.dma_start(cosT[:, :], d["c_cos"]), tx),
                  S.dma("sp", lambda e, v: e.dma_start(sinT[:, :], d["c_sin"]), tx)]
            txt = transposes(S, XN, tln, NT)
            tqk = project_qk(S, NT, txt, None, False, tc, lambda S: None)
            tv = project_v(S, NT, txt, None, False, tqk)
            last = attend(S, NT, True, 0.25, tqk, tv, tv)
            txt = transposes(S, ON, [last] * NT, NT)

            def write(S, t, ps, mm):
                return S.op("dve", lambda e, v: e.tensor_tensor(XR[:, t, :], ps, XR[:, t, :], ALU.add), mm)
            to = project_out(S, NT, txt, None, write)
            S.dma("sp", lambda e, v: e.dma_start(tokens3(x3_d, v["b"]), XR[:, :, :]), to)
            tln = layernorm(S, XR, to, XN, NT, txt)
            txt = transposes(S, XN, tln, NT, to)
            S.dma("sp", lambda e, v: e.dma_start(tokens3(xw_d[0:NTOK, :], v["b"])[:, :, 0:C], XN[:, :, :]), tln)
            route1(S, txt)
            return S.close()

        def route1(S, txt):
            R = {nm: PB[i][:, 0:512].rearrange("p (t e) -> p t e", e=E1)
                 for i, nm in enumerate(["L", "rep", "mask", "ex", "pre", "pos", "w"])}
            sml = PB[7]
            top = sml[:, 0:64].rearrange("p (t k) -> p t k", k=8)
            v8 = sml[:, 64:128].rearrange("p (t k) -> p t k", k=8)
            s1 = sml[:, 128:136]
            s2 = sml[:, 136:144]
            di = smi[:, 0:2, :].rearrange("p a b -> p (a b)")
            ti_ = smi[:, 2, 0:NT]

            def bc(ap):
                return ap.rearrange("p (t o) -> p t o", o=1).to_broadcast([128, NT, E1])
            for t in range(NT):
                for k in range(2):
                    mm = S.op("pe", lambda e, v, t=t, k=k: e.matmul(
                        PA[:, E1 * t:E1 * t + E1], XT[:, k, 128 * t:128 * t + 128], rw[:, k, :],
                        start=(k == 0), stop=(k == 1)), txt, sig=(t == NT - 1 and k == 1))

            def dv(fn, *w):
                dv.t = S.op("dve", fn, dv.t, *w)
                return dv.t
            dv.t = None
            dv(lambda e, v: e.tensor_copy(PB[0][:, 0:512], PA[:, 0:512]), mm)
            for t in range(NT):
                tt = S.op("dve", lambda e, v, t=t: e.max(top[:, t, :], R["L"][:, t, :]), dv.t)
            for t in range(NT):
                t2 = S.op("dve", lambda e, v, t=t: e.match_replace(R["rep"][:, t, :], top[:, t, :], R["L"][:, t, :], NEG), tt)
            dv.t = t2
            dv(lambda e, v: e.tensor_tensor(R["mask"], R["rep"], R["L"], ALU.not_equal))
            tm = dv.t
            dv(lambda e, v: e.tensor_tensor(R["ex"], R["L"], bc(top[:, :, 0:1].rearrange("p t o -> p (t o)")), ALU.subtract))
            ta = S.op("act", lambda e, v: e.activation(R["ex"], R["ex"], ACT.Exp), dv.t)
            dv(lambda e, v: e.tensor_copy(R["pre"][:, 0, :], carry[:, :]))
            for t in range(1, NT):
                dv(lambda e, v, t=t: e.tensor_tensor(
                    R["pre"][:, t, :], R["pre"][:, t - 1, :], R["mask"][:, t - 1, :], ALU.add))
            tp = dv.t
            dv(lambda e, v: e.tensor_tensor(carry[:, :], R["pre"][:, NT - 1, :], R["mask"][:, NT - 1, :], ALU.add))
            S.op("pe", lambda e, v: e.matmul(PS[0][:, 0:512], upper[:, :], PB[2][:, 0:512], start=True, stop=False), tm, sig=False)
            mm = S.op("pe", lambda e, v: e.matmul(PS[0][:, 0:512], ones[:, :], PB[4][:, 0:512], start=False, stop=True), tp)
            dv(lambda e, v: e.tensor_reduce(s1, R["ex"], AX.X, ALU.add), ta)
            dv(lambda e, v: e.reciprocal(s1, s1))
            dv(lambda e, v: e.tensor_tensor(R["ex"], R["ex"], bc(s1), ALU.mult))
            dv(lambda e, v: e.tensor_tensor(R["ex"], R["ex"], R["mask"], ALU.mult))
            dv(lambda e, v: e.tensor_reduce(s2, R["ex"], AX.X, ALU.add))
            dv(lambda e, v: e.reciprocal(s2, s2))
            dv(lambda e, v: e.tensor_tensor(R["w"], R["ex"], bc(s2), ALU.mult))
            S.dma("sp", lambda e, v: e.dma_start(tokens3(xw_d[0:NTOK, :], v["b"])[:, :, C:C + E1], R["w"]), dv.t)
            dv(lambda e, v: e.tensor_copy(PB[5][:, 0:512], PS[0][:, 0:512]), mm)
            dv(lambda e, v: e.scalar_tensor_tensor(R["mask"], R["pos"], float(CAP), R["mask"], ALU.is_lt, ALU.mult))
            dv(lambda e, v: e.tensor_tensor(R["pos"], eoff1[:, :, :], R["pos"], ALU.subtract))
            dv(lambda e, v: e.tensor_tensor(R["pos"], R["pos"], R["mask"], ALU.mult))
            for t in range(NT):
                tt = S.op("dve", lambda e, v, t=t: e.max(v8[:, t, :], R["pos"][:, t, :]), dv.t)
            dv.t = tt
            dv(lambda e, v: e.tensor_scalar(sml[:, 192:256], sml[:, 64:128], -1.0, 16384.0, ALU.mult, ALU.add))
            dv(lambda e, v: e.tensor_copy(di, sml[:, 192:256]))
            dv(lambda e, v: e.tensor_copy(ti_, tokid[:, :]))
            t3 = dv.t
            dv(lambda e, v: e.tensor_scalar(tokid[:, :], tokid[:, :], float(T), None, ALU.add))
            for t in range(NT):
                for k in range(8):
                    S.dma("pool", lambda e, v, t=t, k=k: e.indirect_dma_start(
                        out=list_d, out_offset=bass.IndirectOffsetOnAxis(ap=di[:, 8 * t + k:8 * t + k + 1], axis=0),
                        in_=ti_[:, t:t + 1], in_offset=None, bounds_check=E1 * CAP - 1, oob_is_err=False), t3)

        NX = 4

        def experts():
            S = new()
            li = smi[:, 4, 0:NX]
            ll = S.dma("sp", lambda e, v: e.dma_start(
                li, list_d.rearrange("(g e s) o -> g s (e o)", s=CAP, e=NX)[row(v["g"]), :, :].rearrange("o s e -> (o s) e"),
                allow_slow_non_contiguous=True))
            XE = [PB[x][:, 0:C + E1] for x in range(NX)]
            WG = [QF[:, x // 2, 512 * (x % 2):512 * (x % 2) + 512].rearrange("p (k n) -> p k n", k=2) for x in range(NX)]
            WD = [W[:, x, 0, :] for x in range(NX)]
            for x in range(NX):
                lw = S.dma("sp", lambda e, v, x=x: e.dma_start(
                    WG[x], d["L1_ffn_expert_gate_up_w"].rearrange("g (k p) n -> g p k n", p=128)[
                        row(v["g"] * NX + x), :, :, :].rearrange("o p k n -> (o p) k n")))
                lw2 = S.dma("sp", lambda e, v, x=x: e.dma_start(
                    WD[x], d["L1_ffn_expert_down_w"][row(v["g"] * NX + x), :, :].rearrange("o p n -> (o p) n")))
                g = S.dma("pool", lambda e, v, x=x: e.indirect_dma_start(
                    out=XE[x], out_offset=None, in_=xw_d,
                    in_offset=bass.IndirectOffsetOnAxis(ap=li[:, x:x + 1], axis=0)), ll)
                pt, pg, py = BANKS[2 * x], BANKS[2 * x + 1], BANKS[2 * x]
                xt = XT[:, x // 2, 512 * (x % 2):512 * (x % 2) + 256]
                at = XT[:, x // 2, 512 * (x % 2) + 256:512 * (x % 2) + 512]
                for k in range(2):
                    mm = S.op("pe", lambda e, v, x=x, k=k, pt=pt: e.transpose(
                        pt[:, 128 * k:128 * k + 128], XE[x][:, 128 * k:128 * k + 128], ident[:, :]), g, sig=(k == 1))
                c = S.op("act", lambda e, v, xt=xt, pt=pt: e.activation(xt, pt[:, 0:256], ACT.Copy), mm)
                for m in range(2):
                    for k in range(2):
                        mm = S.op("pe", lambda e, v, x=x, k=k, m=m, pg=pg, xt=xt: e.matmul(
                            pg[:, 128 * m:128 * m + 128], WG[x][:, k, 128 * m:128 * m + 128],
                            xt[:, 128 * k:128 * k + 128], start=(k == 0), stop=(k == 1)), c, lw,
                            sig=(k == 1 and m == 1))
                s = S.op("act", lambda e, v, at=at, pg=pg: e.activation(at[:, 0:128], pg[:, 0:128], ACT.Sigmoid), mm)
                s2 = S.op("dve", lambda e, v, at=at, pg=pg: e.tensor_tensor(at[:, 0:128], at[:, 0:128], pg[:, 0:128], ALU.mult), s)
                s3 = S.op("dve", lambda e, v, at=at, pg=pg: e.tensor_tensor(at[:, 0:128], at[:, 0:128], pg[:, 128:256], ALU.mult), s2)
                mm = S.op("pe", lambda e, v, x=x, at=at, py=py: e.matmul(
                    py[:, 0:C], at[:, 0:128], WD[x], start=True, stop=True), s3, lw2)

                def wmul(e, v, x=x, py=py):
                    return e.tensor_scalar(PB[4 + x][:, 0:C], py[:, 0:C],
                                           XE[x][:, bass.ds(v["g"] * NX + (C + x), 1)], None, ALU.mult)
                y = S.op("dve", wmul, mm)
                S.dma("pool", lambda e, v, x=x: e.indirect_dma_start(
                    out=ye_d[x], out_offset=bass.IndirectOffsetOnAxis(ap=li[:, x:x + 1], axis=0),
                    in_=PB[4 + x][:, 0:C], in_offset=None, compute_op=ALU.add), y)
            return S.close()

        WGU = [PB[i] for i in range(2)]

        def pre_shared():
            S = new()
            for k in range(2):
                S.dma("sp", lambda e, v, k=k: e.dma_start(PB[k][:, :], d["L1_ffn_shared_gate_up_w"][128 * k:128 * k + 128, :]))
            S.dma("sp", lambda e, v: e.dma_start(PB[2][:, :].rearrange("p (k n) -> p k n", k=4),
                                                 d["L1_ffn_shared_down_w"].rearrange("(k p) n -> p k n", p=128)))
            S.dma("sp", lambda e, v: e.dma_start(rw[:, :, 0:1], d["L1_ffn_shared_gate_w"].rearrange("(k p) n -> p k n", p=128),
                                                 allow_slow_non_contiguous=True))
            return S.close()

        def shared():
            S = new()
            l3 = S.dma("sp", lambda e, v: e.dma_start(XR[:, :, :], tokens3(x3_d, v["b"])))
            ln = S.dma("sp", lambda e, v: e.dma_start(XN[:, :, :], tokens3(xw_d[0:NTOK, :], v["b"])[:, :, 0:C]))
            YE = [QF[:, :, :].rearrange("p a n -> p (a n)").rearrange("p (t c) -> p t c", c=C)] + \
                 [VA[:, 4 * i:4 * i + 4, :, :].rearrange("p a h d -> p (a h d)").rearrange("p (t c) -> p t c", c=C) for i in range(2)]
            acc = [l3]
            for i in range(4):
                y = YE[i % 2]
                l = S.dma("sp", lambda e, v, i=i, y=y: e.dma_start(y, tokens3(ye_d[i][0:NTOK, :], v["b"])), acc[-2] if i >= 2 else None)
                acc.append(S.op("dve", lambda e, v, y=y: e.tensor_tensor(XR[:, :, :], XR[:, :, :], y, ALU.add), l, acc[-1]))
            txt = transposes(S, XN, [ln] * NT, NT)
            for t in range(NT):
                for k in range(2):
                    mm = S.op("pe", lambda e, v, t=t, k=k: e.matmul(
                        PO[:, t:t + 1], XT[:, k, 128 * t:128 * t + 128], rw[:, k, 0:1],
                        start=(k == 0), stop=(k == 1)), txt, sig=(k == 1 and t == NT - 1))
            sg = S.op("act", lambda e, v: e.activation(rstd[:, :], PO[:, 0:NT], ACT.Sigmoid), mm)
            AT = [PB[3 + m][:, 0:512] for m in range(4)]
            free = [None] * 4
            pos_ = sg
            for c in range(2):
                ats = []
                for m in range(4):
                    pg, pu = (PA, PS[0])[m % 2][:, 0:512], (PA, PS[0])[m % 2][:, 512:1024]
                    for dst, off in ((pg, 128 * m), (pu, IS + 128 * m)):
                        for k in range(2):
                            mm = S.op("pe", lambda e, v, dst=dst, off=off, k=k, c=c: e.matmul(
                                dst, PB[k][:, off:off + 128], XT[:, k, 512 * c:512 * c + 512],
                                start=(k == 0), stop=(k == 1)), free[m % 2], txt, sig=(k == 1 and dst is pu))
                    s = S.op("act", lambda e, v, m=m, pg=pg: e.activation(AT[m], pg, ACT.Sigmoid), mm, free[2 + c % 2 - 0] if c else None)
                    s2 = S.op("dve", lambda e, v, m=m, pg=pg: e.tensor_tensor(AT[m], AT[m], pg, ALU.mult), s)
                    s3 = S.op("dve", lambda e, v, m=m, pu=pu: e.tensor_tensor(AT[m], AT[m], pu, ALU.mult), s2)
                    free[m % 2] = s3
                    ats.append(s3)
                for t in range(4):
                    py = (PS[1][:, 0:C], PS[1][:, 512:512 + C], PO[:, 0:C], PO[:, 512:512 + C])[t]
                    for k in range(4):
                        mm = S.op("pe", lambda e, v, t=t, k=k, py=py: e.matmul(
                            py, AT[k][:, 128 * t:128 * t + 128], PB[2][:, 256 * k:256 * k + 256],
                            start=(k == 0), stop=(k == 3)), ats, pos_, sig=(k == 3))
                    pl = S.op("dve", lambda e, v, t=t, c=c, py=py: e.scalar_tensor_tensor(
                        XR[:, 4 * c + t, :], py, rstd[:, 4 * c + t:4 * c + t + 1], XR[:, 4 * c + t, :],
                        ALU.mult, ALU.add), mm, sg, acc[-1])
                pos_ = [sg, pl]
                free[2] = free[3] = pl
            S.dma("sp", lambda e, v: e.dma_start(tokens3(out.rearrange("b t c -> (b t) c"), v["b"]), XR[:, :, :]), pl)
            return S.close()


        secs = {"constants": constants(), "l0_attn": l0_attn(), "pre_ffn": pre_ffn(),
                "pre_l1": pre_l1(), "l1_attn": l1_attn(), "experts": experts(),
                "pre_shared": pre_shared(), "shared": shared()}
        for nt in range(1, NT + 1):
            secs[f"ffn{nt}"] = ffn_unit(nt)

        def emit(key, e):
            def barrier():
                if key == "sp":
                    e.wait_ge(A1, 4)
                    for s in work:
                        e.sem_clear(s)
                    e.sem_clear(A1)
                    e.sem_clear(B2)
                    e.sem_inc(A2, 1)
                    e.wait_ge(B1, 4)
                    e.sem_clear(A2)
                    e.sem_clear(B1)
                    e.sem_inc(B2, 1)
                else:
                    if key == "pool":
                        e.dma_reset()
                    e.drain().then_inc(A1, 1)
                    e.wait_ge(A2, 1)
                    e.drain().then_inc(B1, 1)
                    e.wait_ge(B2, 1)

            def run(name, env):
                for f in secs[name].q[key]:
                    f(e, env)

            run("constants", {})
            barrier()
            with e.Fori(0, B) as b:
                run("l0_attn", {"b": b})
                barrier()
            run("pre_ffn", {})
            barrier()
            with e.Fori(0, B) as b:
                with e.Fori(0, E0) as ex:
                    u = b * E0 + ex
                    tiles = e.value_load(cnt[0:1, bass.ds(u, 1)], min_val=0, max_val=NT)
                    for nt in range(1, NT + 1):
                        with e.If(tiles == nt):
                            run(f"ffn{nt}", {"b": b, "ex": ex, "u": u})
                    barrier()
            run("pre_l1", {})
            barrier()
            with e.Fori(0, B) as b:
                run("l1_attn", {"b": b})
                barrier()
            with e.Fori(0, E1 // NX) as g:
                run("experts", {"g": g})
                barrier()
            run("pre_shared", {})
            barrier()
            with e.Fori(0, B) as b:
                run("shared", {"b": b})
                barrier()

        block = ctx.enter_context(nc.Block())

        @block.sync
        def _(e):
            emit("sp", e)

        @block.tensor
        def _(e):
            emit("pe", e)

        @block.scalar
        def _(e):
            emit("act", e)

        @block.vector
        def _(e):
            emit("dve", e)

        @block.gpsimd
        def _(e):
            emit("pool", e)


def shape_constants():
    bf = mybir.dt.np(BF16)
    f = np.float32
    k = {}
    k["c_ident"] = np.eye(128, dtype=f)
    k["c_identb"] = np.eye(128, dtype=f).astype(bf)
    k["c_ones"] = np.ones((128, 128), f)
    k["c_upper"] = np.triu(np.ones((128, 128), f), 1)
    k["c_iota"] = np.arange(T, dtype=f)[None, :]
    mask = np.where(np.triu(np.ones((128, 128)), 1) > 0, f(NEG), f(0)).astype(f)
    k["c_maskA"] = mask.astype(bf)
    k["c_maskB"] = np.ascontiguousarray(mask.T).astype(bf)
    k["c_e4"] = np.tile(np.arange(E0, 0, -1, dtype=f), (128, NT))
    k["c_eoff"] = np.tile(np.arange(E0, dtype=f) * UROWS, (128, NT))
    k["c_eoff1"] = np.tile(f(16384) - np.arange(E1, dtype=f) * CAP, (128, NT))
    k["c_tokid"] = (np.arange(NT)[None, :] * 128 + np.arange(128)[:, None]).astype(f)
    k["c_list"] = (NTOK + np.arange(E1 * CAP) % CAP).astype(np.int32)[:, None]
    slopes = (f(2.0) ** (f(-0.5) * np.arange(1, H + 1, dtype=f))).astype(f)
    al = (slopes[:, None] * np.arange(T, dtype=f)[None, :]).astype(f) * f(4.0)
    parts = []
    r = al
    for _ in range(3):
        p = r.astype(bf)
        parts.append(p)
        r = (r - p.astype(f)).astype(f)
    k["c_alibi"] = np.stack(parts)
    half = D // 2
    inv = (f(10000.0) ** (-np.arange(0, half, dtype=f) * f(2.0) / f(D))).astype(f)
    ang = np.arange(T, dtype=f)[:, None] * inv[None, :]
    cos, sin = np.cos(ang).astype(f), np.sin(ang).astype(f)
    ct = np.repeat(cos.T, 2, axis=0)
    sn = np.repeat(sin.T, 2, axis=0)
    sn[0::2] *= f(-1)
    k["c_cos"] = np.ascontiguousarray(np.tile(ct, (8, 1)))
    k["c_sin"] = np.ascontiguousarray(np.tile(sn, (8, 1)))
    return k


def kernel(**inputs):
    import concourse.bacc as bacc
    from concourse.bass_utils import run_bass_kernel_spmd

    nc = bacc.Bacc("TRN2", target_bir_lowering=False, num_devices=1)
    a = {n: np.ascontiguousarray(inputs[n]) for n in inputs}
    a["L0_attn_x"] = a["L0_attn_x"].reshape(NTOK, C)
    swap = np.arange(C).reshape(-1, 2)[:, ::-1].reshape(-1)
    for nm, src in (("q", "Wq"), ("k", "Wk"), ("v", "Wv"), ("o", "Wo")):
        a["w1_" + nm] = np.ascontiguousarray(a.pop("L1_attn_" + src).T)
    for nm in ("q", "k"):
        a[f"w1_{nm}s"] = np.ascontiguousarray(a["w1_" + nm][:, swap])
    a.update(shape_constants())
    arrays, d = {}, {}
    for n, x in a.items():
        arrays["in_" + n] = x
        d[n] = nc.dram_tensor("in_" + n, x.shape, mybir.dt.from_np(x.dtype), kind="ExternalInput").ap()
    out = nc.dram_tensor("out_0", (B, T, C), F32, kind="ExternalOutput").ap()
    build(nc, d, out)
    r = run_bass_kernel_spmd(nc, [arrays], core_ids=[0])
    return r.results[0]["out_0"]
```

```python
from contextlib import ExitStack

import numpy as np

import concourse.bass as bass
from concourse import mybir

ALU = mybir.AluOpType
ACT = mybir.ActivationFunctionType
AX = mybir.AxisListType
F32 = mybir.dt.float32
BF16 = mybir.dt.bfloat16
I32 = mybir.dt.int32

B, T, C, H, D = 4, 1024, 256, 16, 16
NT = T // 128
E0 = 4
UROWS = 1152
E1, I1, IS, CAP = 64, 128, 512, 128
NTOK = B * T
EPS = 1e-5
NEG = -1e30
ENGINES = ("pe", "act", "dve", "pool", "sp")
KA = 99
KB = 101


class Section:

    def __init__(self, sems, dma_sems):
        self.q = {k: [] for k in ENGINES}
        self.sems = sems
        self.count = {k: 0 for k in ENGINES}
        self.seen = {k: {} for k in ENGINES}
        self.dma_sems = dma_sems
        self.dma_n = {k: 0 for k in dma_sems}
        self.dma_val = {k: [0] * len(v) for k, v in dma_sems.items()}

    def wait(self, eng, *tokens):
        for tok in tokens:
            if tok is None:
                continue
            if not (isinstance(tok, tuple) and len(tok) == 2 and isinstance(tok[1], int)):
                self.wait(eng, *tok)
                continue
            sem, val = tok
            if self.seen[eng].get(sem.name, 0) >= val:
                continue
            self.seen[eng][sem.name] = val
            self.q[eng].append(lambda e, env, s=sem, v=val: e.wait_ge(s, v))

    def op(self, eng, fn, *waits, sig=True):
        self.wait(eng, *waits)
        if not sig:
            self.q[eng].append(fn)
            return None
        self.count[eng] += 1
        sem = self.sems[eng]
        self.q[eng].append(lambda e, env: fn(e, env).then_inc(sem, 1))
        return (sem, self.count[eng])

    def dma(self, eng, fn, *waits):
        pool = self.dma_sems[eng]
        i = self.dma_n[eng] % len(pool)
        self.dma_n[eng] += 1
        if self.dma_val[eng][i]:
            self.wait(eng, (pool[i], self.dma_val[eng][i]))
        self.wait(eng, *waits)
        self.dma_val[eng][i] += 16
        sem = pool[i]
        self.q[eng].append(lambda e, env: fn(e, env).then_inc(sem, 16))
        return (sem, self.dma_val[eng][i])

    def close(self):
        for eng, pool in self.dma_sems.items():
            for i, sem in enumerate(pool):
                if self.dma_val[eng][i]:
                    self.wait(eng, (sem, self.dma_val[eng][i]))
        return self


def chunks(a, b, step=512):
    out = []
    while a < b:
        c = min(b, (a // step + 1) * step)
        out.append((a, c))
        a = c
    return out


def build(nc, d, out):
    ctx = ExitStack()
    with ctx:
        def sb(name, shape, dt=F32):
            return ctx.enter_context(nc.sbuf_tensor(name, shape, dt))

        def sem(name):
            return ctx.enter_context(nc.semaphore(name))

        def dram(name, shape, dt=F32):
            return nc.dram_tensor(name, shape, dt, kind="Internal").ap()

        x1_d = dram("x1_d", (NTOK, C))
        xg_d = dram("xg_d", (B * E0 * UROWS, C))
        yg_d = dram("yg_d", (B * E0 * UROWS, C))
        rt_d = dram("rt_d", (B, 128, NT * 4))
        mk_d = dram("mk_d", (B * E0, T), BF16)
        cnt_d = dram("cnt_d", (B * E0, 1), I32)
        qk_d = [dram(f"qk_d{i}", (3, C, T), BF16) for i in range(2)]
        x3_d = dram("x3_d", (NTOK, C))
        xw_d = dram("xw_d", (NTOK + 128, C + E1))
        list_d = dram("list_d", (E1 * CAP, 1), I32)
        ye_d = dram("ye_d", (NTOK + 128, C))

        ident = sb("ident", [128, 128])
        identb = sb("identb", [128, 128], BF16)
        ones = sb("ones", [128, 128])
        upper = sb("upper", [128, 128])
        maskA = sb("maskA", [128, 128], BF16)
        maskB = sb("maskB", [128, 128], BF16)
        iota = sb("iota", [1, T])
        e4 = sb("e4", [128, NT, E0])
        eoff = sb("eoff", [128, NT, E0])
        eoff1 = sb("eoff1", [128, NT, E1])
        tokid = sb("tokid", [128, NT])
        carry = sb("carry", [128, E1])
        base = sb("base", [128, 1])
        cnt = sb("cnt", [1, B * E0], I32)
        XR = sb("XR", [128, NT, C])
        XN = sb("XN", [128, NT, C])
        XT = sb("XT", [128, 2, T])
        W = sb("W", [128, 6, 2, C])
        bq = sb("bq", [128, 2, 2])
        bv = sb("bv", [1, C])
        bo = sb("bo", [128, C])
        rw = sb("rw", [128, 2, E1])
        rb = sb("rb", [128, E0])
        QF = sb("QF", [128, 2, T])
        PH = sb("PH", [128, 3, 2, T], BF16)
        QS = sb("QS", [KB, H, T], BF16)
        KS = sb("KS", [KB, H, T], BF16)
        VA = sb("VA", [128, NT, H, 32])
        PB = [sb(f"PB{i}", [128, T]) for i in range(8)]
        M1 = sb("M1", [128, 4, NT, 4])
        MHL = sb("MHL", [128, 4, NT, 8], BF16)
        MR = sb("MR", [8, 2, T], BF16)
        RD = sb("RD", [128, NT, 4])
        bst = sb("bst", [128, NT, 6])
        mv = sb("mv", [128, NT, 2])
        rstd = sb("rstd", [128, NT])
        mhalf = sb("mhalf", [128, NT])
        Z = sb("Z", [128, C])
        ON = XN
        OT = [QF[:, 0, 0:512], QF[:, 0, 512:1024]]
        cosT = PB[0]
        sinT = PB[1]
        sm = sb("sm", [128, 24, 32])
        smi = sb("smi", [128, 8, 32], I32)
        dlist = sb("dlist", [128, 64], I32)
        tlist = sb("tlist", [128, NT], I32)
        lists = sb("lists", [128, E1], I32)

        PSUM = ctx.enter_context(nc.psum_tensor("PSUM", [128, 8, 512], F32))
        BANKS = [PSUM[:, i, :] for i in range(8)]
        PR = [PSUM[:, 2 * i:2 * i + 2, :].rearrange("p a n -> p (a n)") for i in range(2)]
        PX = [BANKS[i] for i in (4, 5, 6)]
        PO = BANKS[7]

        sems = {k: sem("s_" + k) for k in ENGINES}
        dma_sems = {"sp": [sem(f"d_sp{i}") for i in range(32)],
                    "pool": [sem(f"d_pool{i}") for i in range(16)]}
        A1, A2, B1, B2 = [sem(f"bar{i}") for i in range(4)]
        work = list(sems.values()) + dma_sems["sp"] + dma_sems["pool"]

        def new():
            return Section(sems, dma_sems)


        def load_w(S, i, ap, *waits):
            return S.dma("sp", lambda e, v: e.dma_start(
                W[:, i, :, :], ap(v).rearrange("(k p) n -> p k n", p=128)), *waits)

        def bcast_load(S, dst, ap, n, *waits):
            return S.dma("sp", lambda e, v: e.dma_start(dst, ap(v).to_broadcast([128, n])), *waits)

        def layernorm(S, src, tsrc, dst, nt, *free):
            t = []
            for i in range(nt):
                a = S.op("dve", lambda e, v, i=i: e.bn_stats(bst[:, i, :], src[:, i, :]), tsrc[i])
            for i in range(nt):
                a = S.op("dve", lambda e, v, i=i: e.bn_aggr(mv[:, i, :], bst[:, i, :]), a)
            a = S.op("dve", lambda e, v: e.tensor_scalar(rstd[:, 0:nt], mv[:, 0:nt, 1], EPS, None, ALU.add), a)
            p = S.op("pool", lambda e, v: e.tensor_tensor(
                rstd[:, 0:nt], rstd[:, 0:nt], mhalf[:, 0:nt], ALU.pow), a)
            for i in range(nt):
                t.append(S.op("dve", lambda e, v, i=i: e.tensor_scalar(
                    dst[:, i, :], src[:, i, :], mv[:, i, 0:1], rstd[:, i:i + 1],
                    ALU.subtract, ALU.mult), a, p, *free))
            return t

        def transposes(S, src, tsrc, nt, *free):
            toks = []
            n = 0
            users = [None] * 4
            for c0 in range(0, nt, 4):
                w = min(4, nt - c0)
                for k in range(2):
                    bank = BANKS[n % 4]
                    for i in range(w):
                        a = S.op("pe", lambda e, v, i=i, k=k, c0=c0, bank=bank: e.transpose(
                            bank[:, 128 * i:128 * i + 128], src[:, c0 + i, 128 * k:128 * k + 128],
                            ident[:, :]), tsrc[c0 + i], users[n % 4], sig=(i == w - 1))
                    eng = "dve" if n % 2 else "act"

                    def ev(e, v, k=k, c0=c0, w=w, bank=bank, eng=eng):
                        o = XT[:, k, 128 * c0:128 * (c0 + w)]
                        return (e.tensor_copy(o, bank[:, 0:128 * w]) if eng == "dve"
                                else e.activation(o, bank[:, 0:128 * w], ACT.Copy))
                    users[n % 4] = S.op(eng, ev, a, *free)
                    toks.append(users[n % 4])
                    n += 1
            return toks

        def project_qk(S, nt, txt, wtok, bias, rope, kadd):
            n = 128 * nt
            users = [None] * 8
            nb = 0
            add = kadd(S)
            ready = []
            last_st = [None, None]
            for g in range(2):
                done = [add]
                for qk in range(2):
                    evs = []
                    for (a, b) in chunks(0, n):
                        m = b - a
                        mats = [(BANKS[nb % 8], qk)]
                        if rope:
                            mats.append((BANKS[(nb + 1) % 8], qk + 4))
                        for bank, wi in mats:
                            for k in range(2):
                                mm = S.op("pe", lambda e, v, k=k, g=g, wi=wi, a=a, b=b, bank=bank: e.matmul(
                                    bank[:, 0:b - a], W[:, wi, k, 128 * g:128 * g + 128],
                                    XT[:, k, a:b], start=(k == 0), stop=(k == 1)),
                                    txt, wtok, users[nb % 8], users[(nb + 1) % 8] if rope else None,
                                    sig=(k == 1))
                        o = QF[:, qk, a:b]
                        if not rope:
                            def f1(e, v, o=o, i=mats[0][0][:, 0:m], g=g, qk=qk):
                                if bias:
                                    return e.activation(o, i, ACT.Identity, bias=bq[:, qk, g:g + 1])
                                return e.activation(o, i, ACT.Copy)
                            t1 = S.op("act", f1, mm, last_st[qk])
                            users[nb % 8] = t1
                            nb += 1
                        else:
                            t1 = S.op("dve", lambda e, v, o=o, i=mats[0][0][:, 0:m], c=cosT[:, a:b]:
                                      e.tensor_tensor(o, i, c, ALU.mult), mm, last_st[qk], rope)
                            t2 = S.op("dve", lambda e, v, o=PB[2][:, a:b], i=mats[1][0][:, 0:m], c=sinT[:, a:b]:
                                      e.tensor_tensor(o, i, c, ALU.mult), mm, rope)
                            t1 = S.op("dve", lambda e, v, o=o, i=PB[2][:, a:b]:
                                      e.tensor_tensor(o, o, i, ALU.add), t1, t2)
                            users[nb % 8] = users[(nb + 1) % 8] = t2
                            nb += 2
                        evs.append(t1)
                    f = QF[:, qk, 0:n]
                    ph = [PH[:, p, qk, 0:n] for p in range(3)]
                    th = S.op("act", lambda e, v, o=ph[0], i=f: e.activation(o, i, ACT.Copy), evs, last_st[qk])
                    tr = S.op("dve", lambda e, v, o=f, i=ph[0]: e.tensor_tensor(o, o, i, ALU.subtract), evs, th)
                    tm = S.op("dve", lambda e, v, o=ph[1], i=f: e.tensor_copy(o, i), tr, last_st[qk])
                    tl = S.op("dve", lambda e, v, o=ph[2], i=f, j=ph[1]: e.tensor_tensor(o, i, j, ALU.subtract), tm)
                    stores = []
                    for p, tt in ((0, th), (1, tm), (2, tl)):
                        stores.append(S.dma("sp", lambda e, v, p=p, g=g, qk=qk: e.dma_start(
                            qk_d[qk][p, 128 * g:128 * g + 128, 0:n], PH[:, p, qk, 0:n]), tt))
                    last_st[qk] = stores + [tl]
                    parts = (0, 1, 2, 0, 1, 0) if qk == 0 else (0, 0, 0, 1, 1, 2)
                    dst = QS if qk == 0 else KS
                    for s, p in enumerate(parts):
                        done.append(S.dma("sp", lambda e, v, s=s, p=p, dst=dst, qk=qk, g=g: e.dma_start(
                            dst[16 * s:16 * s + 16, 8 * g:8 * g + 8, 0:n],
                            qk_d[qk][p, 128 * g:128 * g + 128, 0:n].rearrange("(h d) n -> d h n", d=16)),
                            stores[p]))
                ready.append(done)
            return ready, users

        def project_v(S, nt, txt, wtok, bias, bank, before):
            toks = {}

            def tile(t):
                i = t % len(bank)
                if bias:
                    S.op("pe", lambda e, v, t=t, i=i: e.matmul(
                        bank[i][:, 0:C], ones[0:1, :], bv[0:1, :], start=True, stop=False),
                        txt, wtok, before[i], sig=False)
                for k in range(2):
                    mm = S.op("pe", lambda e, v, k=k, t=t, i=i: e.matmul(
                        bank[i][:, 0:C], XT[:, k, 128 * t:128 * t + 128], W[:, 2, k, :],
                        start=(k == 0 and not bias), stop=(k == 1)), txt, wtok, before[i], sig=(k == 1))
                before[i] = S.op("act", lambda e, v, t=t, i=i: e.activation(
                    VA[:, t, :, 0:16], bank[i][:, 0:C].rearrange("p (h d) -> p h d", d=16), ACT.Copy), mm)
                toks[t] = before[i]
            return toks, [lambda t=t: tile(t) for t in range(nt)]

        def attend(S, nt, causal, scale, ready, users, vproj):
            n = 128 * nt
            before = [users[4], users[5], users[6]]
            tv, fillers = vproj(PX, before)
            st = {"pr": [[users[0], users[1]], [users[2], users[3]]], "po": users[7],
                  "pb": [None] * 16, "mr": [None, None], "qsm": {}, "ot": [None, None], "m1": {},
                  "npr": 0, "nps": 0, "step": 0, "rd": None}
            p1 = [[(qt, j) for qt in range(nt) for j in range(4)] for _ in range(4)]
            steps = [(qc, kt) for qc in range((n + 511) // 512)
                     for kt in range(nt) if not causal or 128 * kt < min(n, 512 * qc + 512)]

            def pass1(g, qt, j):
                h = 4 * g + j
                kn = 128 * (qt + 1) if causal else n
                r = st["npr"] % 2
                st["npr"] += 1
                buf = PR[r]
                for (a, b) in chunks(0, kn):
                    diag = causal and b == kn
                    mm = S.op("pe", lambda e, v, a=a, b=b, diag=diag: e.matmul(
                        buf[:, a:b], QS[0:KA, h, 128 * qt:128 * qt + 128], KS[0:KA, h, a:b],
                        start=True, stop=not diag, skip_group_check=diag), ready[g // 2], st["pr"][r],
                        sig=(b == kn and not diag))
                if causal:
                    mm = S.op("pe", lambda e, v: e.matmul(
                        buf[:, kn - 128:kn], identb[:, :], maskA[:, :], start=False, stop=True,
                        skip_group_check=True))
                st["pr"][r] = S.op("dve", lambda e, v: e.tensor_reduce(
                    M1[:, g, qt, j:j + 1], buf[:, 0:kn], AX.X, ALU.max), mm)
                st["m1"][g] = st["pr"][r]

            def m_rows(g):
                m1 = M1[:, g, 0:nt, :]
                hi = MHL[:, g, 0:nt, 0:4]
                lo = MHL[:, g, 0:nt, 4:8]
                a = S.op("dve", lambda e, v: e.tensor_scalar(hi, m1, -1.0, None, ALU.mult), st["m1"][g])
                a = S.op("dve", lambda e, v: e.scalar_tensor_tensor(
                    lo, m1, -1.0, hi, ALU.mult, ALU.subtract), a)
                r = st["npr"] % 2
                st["npr"] += 1
                buf = PR[r]
                for t in range(nt):
                    mm = S.op("pe", lambda e, v, t=t: e.matmul(
                        buf[0:8, 128 * t:128 * t + 128], MHL[:, g, t, :], identb[:, :],
                        start=True, stop=True), a, st["pr"][r], sig=(t == nt - 1))
                c = S.op("act", lambda e, v: e.activation(MR[:, g % 2, 0:n], buf[0:8, 0:n], ACT.Copy),
                         mm, st["mr"][g % 2])
                st["pr"][r] = c
                ds = []
                for r in range(2):
                    ds.append(S.dma("sp", lambda e, v, r=r: e.dma_start(
                        QS[KA + r:KA + r + 1, 4 * g:4 * g + 4, 0:n], MR[4 * r:4 * r + 4, g % 2, 0:n]), c))
                st["mr"][g % 2] = ds
                st["qsm"][g] = ds

            def span(qc, kt):
                return max(512 * qc, 128 * kt if causal else 0), min(n, 512 * qc + 512)

            def pbuf(i, j):
                i = 4 * (i % 4) + j
                return PB[i // 2][:, 512 * (i % 2):512 * (i % 2) + 512]

            def pass2(g, qc, kt, j, step):
                h = 4 * g + j
                q0, q1 = span(qc, kt)
                w = q1 - q0
                diag = causal and q0 == 128 * kt
                x = st["nps"] % 3
                st["nps"] += 1
                ps = PX[x]
                mm = S.op("pe", lambda e, v: e.matmul(
                    ps[:, 0:w], KS[0:KB, h, 128 * kt:128 * kt + 128], QS[0:KB, h, q0:q1],
                    start=True, stop=not diag, skip_group_check=diag), ready[g // 2], st["qsm"][g],
                    before[x], sig=not diag)
                if diag:
                    mm = S.op("pe", lambda e, v: e.matmul(
                        ps[:, 0:128], identb[:, :], maskB[:, :], start=False, stop=True,
                        skip_group_check=True))
                t = S.op("act", lambda e, v: e.activation(
                    pbuf(step, j)[:, 0:w], ps[:, 0:w], ACT.Exp, scale=scale), mm,
                    st["pb"][4 * (step % 4) + j])
                before[x] = t
                st[("p", step, j)] = t

            def pv(g, qc, kt, step):
                q0, q1 = span(qc, kt)
                o = q0 - 512 * qc
                w = q1 - q0
                lastk = nt - 1 if not causal else min(nt, 4 * qc + 4) - 1
                for j in range(4):
                    mm = S.op("pe", lambda e, v, j=j: e.matmul(
                        PO[32 * j:32 * j + 32, o:o + w], VA[:, kt, 4 * g + j, :], pbuf(step, j)[:, 0:w],
                        start=(kt == 0), stop=(kt == lastk), skip_group_check=True),
                        st[("p", step, j)], tv[kt], st["po"], sig=(j == 3))
                for j in range(4):
                    st["pb"][4 * (step % 4) + j] = mm
                if kt == lastk:
                    full = q1 - 512 * qc
                    st["po"] = S.op("act", lambda e, v: e.activation(OT[qc][:, 0:full], PO[:, 0:full], ACT.Copy),
                                    mm, st["ot"][qc])
                    return True

            def norm(g, qc, tok):
                tiles = min(nt, 4 * qc + 4) - 4 * qc
                r = st["npr"] % 2
                st["npr"] += 1
                buf = PR[r]
                for t in range(tiles):
                    mm = S.op("pe", lambda e, v, t=t: e.transpose(
                        buf[:, 128 * t:128 * t + 128], OT[qc][:, 128 * t:128 * t + 128], ident[:, :]),
                        tok, st["pr"][r], sig=(t == tiles - 1))
                st["ot"][qc] = mm
                view = buf[:, 0:128 * tiles].rearrange("p (t j d) -> p t j d", j=4, d=32)
                t0 = 4 * qc
                c = S.op("dve", lambda e, v: e.reciprocal(RD[:, 0:tiles, :], view[:, :, :, 16]), mm,
                         st["rd"])
                for t in range(tiles):
                    m = S.op("dve", lambda e, v, t=t: e.tensor_tensor(
                        ON[:, t0 + t, 64 * g:64 * g + 64].rearrange("p (j d) -> p j d", d=16),
                        view[:, t, :, 0:16],
                        RD[:, t, :].rearrange("p (j o) -> p j o", o=1).to_broadcast([128, 4, 16]),
                        ALU.mult), c, mm)
                st["pr"][r] = m
                st["rd"] = m
                return m

            ahead = 4 if nt <= 2 else 1
            for g in range(ahead):
                for i, (qt, j) in enumerate(p1[g]):
                    pass1(g, qt, j)
                    if fillers and i % 3 == 1:
                        fillers.pop(0)()
                while fillers and g == 0:
                    fillers.pop(0)()
                m_rows(g)
            late = []
            last = None
            nstep = 0
            for g in range(4):
                nxt = list(p1[g + 1]) if g + 1 < 4 and g + 1 >= ahead else []
                n1 = len(nxt)
                need_m = bool(nxt)
                n2 = 4 * len(steps)
                i2 = 0
                for (qc, kt) in steps:
                    for j in range(4):
                        pass2(g, qc, kt, j, nstep)
                        i2 += 1
                        while late and late[0][0] <= 4 * nstep + j:
                            _, f = late.pop(0)
                            f()
                        while nxt and (n1 - len(nxt)) < n1 * i2 / (0.82 * n2):
                            pass1(g + 1, *nxt.pop(0))
                        if need_m and not nxt:
                            need_m = False
                            late.append((4 * nstep + j + 2, lambda g=g: m_rows(g + 1)))

                    def fpv(g=g, qc=qc, kt=kt, step=nstep):
                        nonlocal last
                        if pv(g, qc, kt, step):
                            def fn(tok=st["po"]):
                                nonlocal last
                                last = norm(g, qc, tok)
                            late.append((4 * step + 3 + 6, fn))
                            late.sort(key=lambda x: x[0])
                    late.append((4 * nstep + 3 + 2, fpv))
                    late.sort(key=lambda x: x[0])
                    nstep += 1
                while need_m:
                    while nxt:
                        pass1(g + 1, *nxt.pop(0))
                    if any(x[0] > 4 * nstep for x in late):
                        pass
                    need_m = False
                    m_rows(g + 1)
                if g + 1 < 4 and g + 1 not in st["qsm"]:
                    for x in [x for x in late]:
                        late.remove(x)
                        x[1]()
            while late:
                late.pop(0)[1]()
            return last

        def project_out(S, nt, txt, wtok, write, *free):
            toks = []
            users = [None] * 8
            for t in range(nt):
                bank = BANKS[t % 8]
                for k in range(2):
                    mm = S.op("pe", lambda e, v, k=k, t=t, bank=bank: e.matmul(
                        bank[:, 0:C], XT[:, k, 128 * t:128 * t + 128], W[:, 3, k, :],
                        start=(k == 0), stop=(k == 1)), txt, wtok, free, users[t % 8], sig=(k == 1))
                users[t % 8] = write(S, t, bank[:, 0:C], mm)
                toks.append(users[t % 8])
            return toks

        def row(v):
            return bass.ds(v, 1)


        def constants():
            S = new()
            for dst, name in ((ident, "c_ident"), (ones, "c_ones"), (upper, "c_upper"), (iota, "c_iota"),
                              (identb, "c_identb"), (maskA, "c_maskA"), (maskB, "c_maskB")):
                S.dma("sp", lambda e, v, dst=dst, name=name: e.dma_start(dst[:, :], d[name]))
            for dst, name in ((e4, "c_e4"), (eoff, "c_eoff"), (eoff1, "c_eoff1")):
                S.dma("sp", lambda e, v, dst=dst, name=name: e.dma_start(
                    dst[:, :, :], d[name].rearrange("p (t e) -> p t e", t=NT)))
            S.dma("sp", lambda e, v: e.dma_start(tokid[:, :], d["c_tokid"]))
            S.dma("sp", lambda e, v: e.dma_start(list_d, d["c_list"]))
            S.op("dve", lambda e, v: e.memset(carry[:, :], 0.0))
            S.op("dve", lambda e, v: e.memset(base[:, :], 0.0))
            S.op("dve", lambda e, v: e.memset(mhalf[:, :], -0.5))
            for dst in (QS, KS):
                S.dma("sp", lambda e, v, dst=dst: e.dma_start(dst[96:KB, :, :].rearrange("p h n -> p (h n)"), d["c_rows"]))
            S.op("pool", lambda e, v: e.memset(VA[:, :, :, :], 1.0))
            z = S.op("dve", lambda e, v: e.memset(Z[:, :], 0.0))
            S.dma("sp", lambda e, v: e.dma_start(ye_d[NTOK:NTOK + 128, :], Z[:, :]), z)
            S.dma("sp", lambda e, v: e.dma_start(xw_d[NTOK:NTOK + 128, 0:C], Z[:, :]), z)
            S.dma("sp", lambda e, v: e.dma_start(xw_d[NTOK:NTOK + 128, C:C + E1], Z[:, 0:E1]), z)
            for i in range(3):
                load_w(S, i, lambda v, i=i: d["L0_attn_w_attn"][:, 256 * i:256 * i + 256])
            load_w(S, 3, lambda v: d["L0_attn_w_proj"])
            ba = d["L0_attn_b_attn"]
            for qk in range(2):
                S.dma("sp", lambda e, v, qk=qk: e.dma_start(
                    bq[:, qk, :], ba[256 * qk:256 * qk + 256].rearrange("(g p) -> p g", p=128),
                    allow_slow_non_contiguous=True))
            S.dma("sp", lambda e, v: e.dma_start(bv[0:1, :], ba[512:768].partition_broadcast(1)))
            S.dma("sp", lambda e, v: e.dma_start(bo[:, :], d["L0_attn_b_proj"].partition_broadcast(128)))
            S.dma("sp", lambda e, v: e.dma_start(rb[:, :], d["L0_ffn_router_b"].partition_broadcast(128)))
            S.dma("sp", lambda e, v: e.dma_start(
                rw[:, :, 0:E0], d["L0_ffn_router_w"].rearrange("(k p) n -> p k n", p=128)))
            return S.close()

        def tokens3(ap, b):
            return ap.rearrange("(b t p) c -> b p t c", b=B, p=128)[row(b), :, :, :].rearrange(
                "o p t c -> (o p) t c")

        def l0_attn():
            S = new()
            ld = S.dma("sp", lambda e, v: e.dma_start(XR[:, :, :], tokens3(d["L0_attn_x"], v["b"])))
            tln = layernorm(S, XR, [ld] * NT, XN, NT)
            txt = transposes(S, XN, tln, NT)
            ready, users = project_qk(S, NT, txt, None, True, None, lambda S: S.dma(
                "sp", lambda e, v: e.dma_start(KS[96:99, :, :], d["c_alibi"])))
            for ex in range(E0):
                S.dma("sp", lambda e, v, ex=ex: e.dma_start(
                    yg_d.rearrange("(u s p) c -> u p s c", u=B * E0, p=128)[
                        row(v["b"] * E0 + ex), :, :, :].rearrange("o p s c -> (o p) s c"),
                    Z[:, :].rearrange("p (o c) -> p o c", o=1).to_broadcast([128, UROWS // 128, C])))
            S.dma("sp", lambda e, v: e.dma_start(
                tokens3(ye_d[0:NTOK, :], v["b"]),
                Z[:, :].rearrange("p (o c) -> p o c", o=1).to_broadcast([128, NT, C])))
            last = attend(S, NT, True, 0.25, ready, users,
                          lambda bank, before: project_v(S, NT, txt, None, True, bank, before))
            txt = transposes(S, ON, [last] * NT, NT)

            def write(S, t, ps, mm):
                a = S.op("dve", lambda e, v: e.tensor_tensor(XR[:, t, :], ps, XR[:, t, :], ALU.add), mm)
                return S.op("dve", lambda e, v: e.tensor_tensor(XR[:, t, :], XR[:, t, :], bo[:, :], ALU.add), a)
            to = project_out(S, NT, txt, None, write)
            S.dma("sp", lambda e, v: e.dma_start(tokens3(x1_d, v["b"]), XR[:, :, :]), to)
            tln = layernorm(S, XR, to, XN, NT, txt)
            txt = transposes(S, XN, tln, NT, to)
            route0(S, tln, txt)
            return S.close()

        def route0(S, tln, txt):
            lg = BANKS[0][:, 0:32].rearrange("p (t e) -> p t e", e=E0)
            for t in range(NT):
                for k in range(2):
                    mm = S.op("pe", lambda e, v, t=t, k=k: e.matmul(
                        BANKS[0][:, 4 * t:4 * t + 4], XT[:, k, 128 * t:128 * t + 128], rw[:, k, 0:E0],
                        start=(k == 0), stop=(k == 1)), txt, sig=(t == NT - 1 and k == 1))
            names = ["L", "t1", "oh1", "L2", "t2", "oh2", "ex", "mask", "pre", "pos", "tmp", "tot"]
            R = {nm: sm[:, i, :].rearrange("p (t e) -> p t e", e=E0) for i, nm in enumerate(names)}
            V = {nm: sm[:, 12 + i, 0:NT] for i, nm in enumerate(["m1", "x1", "m2", "x2", "s", "w1", "w2", "d1", "d2"])}
            out4 = sm[:, 22, :].rearrange("p (t e) -> p t e", e=4)

            def bc(ap):
                return ap.rearrange("p (t o) -> p t o", o=1).to_broadcast([128, NT, E0])

            def dv(fn, *w):
                dv.t = S.op("dve", fn, dv.t, *w)
                return dv.t
            dv.t = None
            dv(lambda e, v: e.tensor_tensor(R["L"], lg, rb[:, :].rearrange("p (o e) -> p o e", o=1).to_broadcast([128, NT, E0]), ALU.add), mm)
            lt = dv.t
            dv(lambda e, v: e.tensor_reduce(V["m1"], R["L"], AX.X, ALU.max))
            dv(lambda e, v: e.tensor_tensor(R["t1"], R["L"], bc(V["m1"]), ALU.is_equal))
            dv(lambda e, v: e.tensor_tensor(R["t1"], R["t1"], e4[:, :, :], ALU.mult))
            dv(lambda e, v: e.tensor_reduce(V["x1"], R["t1"], AX.X, ALU.max))
            dv(lambda e, v: e.tensor_tensor(R["oh1"], R["t1"], bc(V["x1"]), ALU.is_equal))
            dv(lambda e, v: e.scalar_tensor_tensor(R["L2"], R["oh1"], NEG, R["L"], ALU.mult, ALU.add))
            dv(lambda e, v: e.tensor_reduce(V["m2"], R["L2"], AX.X, ALU.max))
            dv(lambda e, v: e.tensor_tensor(R["t2"], R["L2"], bc(V["m2"]), ALU.is_equal))
            dv(lambda e, v: e.tensor_tensor(R["t2"], R["t2"], e4[:, :, :], ALU.mult))
            dv(lambda e, v: e.tensor_reduce(V["x2"], R["t2"], AX.X, ALU.max))
            dv(lambda e, v: e.tensor_tensor(R["oh2"], R["t2"], bc(V["x2"]), ALU.is_equal))
            dv(lambda e, v: e.tensor_tensor(R["mask"], R["oh1"], R["oh2"], ALU.add))
            tm = dv.t
            dv(lambda e, v: e.tensor_tensor(R["ex"], R["L"], bc(V["m1"]), ALU.subtract))
            ta = S.op("act", lambda e, v: e.activation(R["ex"], R["ex"], ACT.Exp), dv.t)
            dv(lambda e, v: e.tensor_reduce(V["s"], R["ex"], AX.X, ALU.add), ta)
            dv(lambda e, v: e.reciprocal(V["s"], V["s"]))
            dv(lambda e, v: e.tensor_tensor(R["ex"], R["ex"], bc(V["s"]), ALU.mult))
            dv(lambda e, v: e.tensor_tensor(R["tmp"], R["ex"], R["oh1"], ALU.mult))
            dv(lambda e, v: e.tensor_reduce(out4[:, :, 2], R["tmp"], AX.X, ALU.add))
            dv(lambda e, v: e.tensor_tensor(R["tmp"], R["ex"], R["oh2"], ALU.mult))
            dv(lambda e, v: e.tensor_reduce(out4[:, :, 3], R["tmp"], AX.X, ALU.add))
            p0, p1 = BANKS[4][:, 0:32], BANKS[5][:, 0:32]
            S.op("pe", lambda e, v: e.matmul(p0, upper[:, :], sm[:, 7, :], start=True, stop=True), tm, sig=False)
            mm = S.op("pe", lambda e, v: e.matmul(p1, ones[:, :], sm[:, 7, :], start=True, stop=True))
            dv(lambda e, v: e.tensor_copy(sm[:, 11, :], p1), mm)
            dv(lambda e, v: e.memset(R["pre"][:, 0, :], 0.0))
            for t in range(1, NT):
                dv(lambda e, v, t=t: e.tensor_tensor(
                    R["pre"][:, t, :], R["pre"][:, t - 1, :], R["tot"][:, t - 1, :], ALU.add))
            nf = sm[:, 21, 0:E0]
            dv(lambda e, v: e.tensor_tensor(nf, R["pre"][:, NT - 1, :], R["tot"][:, NT - 1, :], ALU.add))
            tn = dv.t
            dv(lambda e, v: e.tensor_tensor(sm[:, 9, :], p0, sm[:, 8, :], ALU.add))
            dv(lambda e, v: e.tensor_tensor(R["pos"], R["pos"], eoff[:, :, :], ALU.add))
            di = smi[:, 0, 0:16].rearrange("p (t k) -> p t k", k=2)
            for k, oh in ((0, "oh1"), (1, "oh2")):
                dd = V["d1"] if k == 0 else V["d2"]
                dv(lambda e, v, oh=oh: e.tensor_tensor(R["tmp"], R["pos"], R[oh], ALU.mult))
                dv(lambda e, v, dd=dd: e.tensor_reduce(dd, R["tmp"], AX.X, ALU.add))
                dv(lambda e, v, dd=dd: e.tensor_scalar(dd, dd, base[:, 0:1], None, ALU.add))
                dv(lambda e, v, dd=dd, k=k: e.tensor_copy(di[:, :, k], dd))
                dv(lambda e, v, k=k: e.tensor_copy(out4.bitcast(I32)[:, :, k], di[:, :, k]))
            ti = dv.t
            dv(lambda e, v: e.tensor_scalar(base[:, :], base[:, :], float(E0 * UROWS), None, ALU.add))
            ni = smi[0:1, 2, 0:E0]
            tcn = smi[0:1, 3, 0:E0]
            dv(lambda e, v: e.tensor_copy(ni, nf[0:1, :]))
            dv(lambda e, v: e.tensor_scalar(sm[0:1, 23, 0:E0], nf[0:1, :], 127.0, None, ALU.add))
            dv(lambda e, v: e.tensor_copy(tcn, sm[0:1, 23, 0:E0]))
            dv(lambda e, v: e.tensor_scalar(tcn, tcn, 7, None, ALU.logical_shift_right))
            tc_ = dv.t
            mkb = PH[0:1, :, :, :].rearrange("p a b n -> p (a b) n")
            for ex in range(E0):
                dv(lambda e, v, ex=ex: e.tensor_scalar(
                    mkb[:, ex, :], iota[0:1, :], nf[0:1, ex:ex + 1], NEG, ALU.is_ge, ALU.mult))
            for ex in range(E0):
                S.dma("sp", lambda e, v, ex=ex: e.dma_start(mk_d[row(v["b"] * E0 + ex), :], mkb[:, ex, :]), dv.t)
                S.dma("sp", lambda e, v, ex=ex: e.dma_start(cnt_d[row(v["b"] * E0 + ex), :], tcn[:, ex:ex + 1]), tc_)
            S.dma("sp", lambda e, v: e.dma_start(rt_d[row(v["b"]), :, :].rearrange("o p n -> (o p) n"), sm[:, 22, :]), ti)
            for t in range(NT):
                for k in range(2):
                    S.dma("pool", lambda e, v, t=t, k=k: e.indirect_dma_start(
                        out=xg_d, out_offset=bass.IndirectOffsetOnAxis(ap=di[:, t, k:k + 1], axis=0),
                        in_=XN[:, t, :], in_offset=None), ti, tln)
            zt = S.op("dve", lambda e, v: e.memset(PB[0][:, 0:C], 0.0))
            for ex in range(E0):
                def pad(e, v, ex=ex):
                    r = e.value_load(ni[0:1, ex:ex + 1], min_val=0, max_val=T)
                    return e.dma_start(xg_d[bass.ds(r + (v["b"] * E0 + ex) * UROWS, 128), :], PB[0][:, 0:C])
                S.dma("sp", pad, zt, tc_)

        def pre_ffn():
            S = new()
            z = S.op("dve", lambda e, v: e.memset(KS[96:99, :, :], 0.0))
            S.dma("sp", lambda e, v: e.dma_start(cnt[:, :], cnt_d.rearrange("a o -> o a"),
                                                 allow_slow_non_contiguous=True))
            return S.close()

        def ffn_unit(nt):
            S = new()
            n = 128 * nt
            lds = []
            for t in range(nt):
                lds.append(S.dma("sp", lambda e, v, t=t: e.dma_start(
                    XN[:, t, :], xg_d[bass.ds(v["u"] * UROWS + 128 * t, 128), :])))
            wt = []
            for i, nm in enumerate(("wq", "wk", "wv", "wo")):
                wt.append(load_w(S, i, lambda v, nm=nm: d["L0_ffn_" + nm][row(v["ex"]), :, :].rearrange("o a b -> (o a) b")))
            for qk, nm in enumerate(("bq", "bk")):
                wt.append(S.dma("sp", lambda e, v, qk=qk, nm=nm: e.dma_start(
                    bq[:, qk, :], d["L0_ffn_" + nm][row(v["ex"]), :].rearrange("o (g p) -> p (o g)", p=128),
                    allow_slow_non_contiguous=True)))
            for dst, nm, m in ((bv, "bv", 1), (bo, "bo", 128)):
                wt.append(S.dma("sp", lambda e, v, dst=dst, nm=nm, m=m: e.dma_start(
                    dst[:, :], d["L0_ffn_" + nm][row(v["ex"]), :].to_broadcast([m, C]))))
            txt = transposes(S, XN, lds, nt)
            ready, users = project_qk(S, nt, txt, wt, True, None, lambda S: S.dma(
                "sp", lambda e, v: e.dma_start(
                    KS[96:97, :, 0:n],
                    mk_d[row(v["u"]), 0:n].rearrange("o (h n) -> o h n", h=1).to_broadcast([1, H, n]))))
            last = attend(S, nt, False, 0.5, ready, users,
                          lambda bank, before: project_v(S, nt, txt, wt, True, bank, before))
            txt = transposes(S, ON, [last] * nt, nt)

            def write(S, t, ps, mm):
                return S.op("dve", lambda e, v: e.tensor_tensor(XR[:, t, :], ps, bo[:, :], ALU.add), mm)
            to = project_out(S, nt, txt, wt, write)
            for t in range(nt):
                S.dma("sp", lambda e, v, t=t: e.dma_start(
                    yg_d[bass.ds(v["u"] * UROWS + 128 * t, 128), :], XR[:, t, :]), to[t])
            return S.close()

        def pre_l1():
            S = new()
            z = S.op("dve", lambda e, v: e.memset(KS[96:99, :, :], 0.0))
            S.op("dve", lambda e, v: e.memset(tlist[:, :], 0))
            S.op("dve", lambda e, v: e.memset(dlist[:, :], 2 * E1 * CAP))
            for i, nm in enumerate(("w1_q", "w1_k", "w1_v", "w1_o", "w1_qs", "w1_ks")):
                load_w(S, i, lambda v, nm=nm: d[nm])
            S.dma("sp", lambda e, v: e.dma_start(rw[:, :, :], d["L1_ffn_gate_w"].rearrange("(k p) n -> p k n", p=128)))
            return S.close()

        def l1_attn():
            S = new()
            ld = S.dma("sp", lambda e, v: e.dma_start(XR[:, :, :], tokens3(x1_d, v["b"])))
            lr = S.dma("sp", lambda e, v: e.dma_start(
                sm[:, 22, :], rt_d[row(v["b"]), :, :].rearrange("o p n -> (o p) n")))
            out4 = sm[:, 22, :].rearrange("p (t e) -> p t e", e=4)
            di = smi[:, 0, 0:16].rearrange("p (t k) -> p t k", k=2)
            ti = S.op("dve", lambda e, v: e.tensor_copy(di, out4.bitcast(I32)[:, :, 0:2]), lr)
            gs, tx = [], []
            for t in range(NT):
                for k in range(2):
                    g = S.dma("pool", lambda e, v, t=t, k=k: e.indirect_dma_start(
                        out=PB[t][:, 256 * k:256 * k + 256], out_offset=None, in_=yg_d,
                        in_offset=bass.IndirectOffsetOnAxis(ap=di[:, t, k:k + 1], axis=0)), ti)
                    gs.append(g)
            for t in range(NT):
                a = None
                for k in range(2):
                    a = S.op("dve", lambda e, v, t=t, k=k: e.scalar_tensor_tensor(
                        XR[:, t, :], PB[t][:, 256 * k:256 * k + 256], out4[:, t, 2 + k:3 + k], XR[:, t, :],
                        ALU.mult, ALU.add), gs[2 * t + k], ld, lr, a)
                tx.append(a)
            tln = layernorm(S, XR, tx, XN, NT)
            placed = place_tokens(S)
            tc = [S.dma("sp", lambda e, v: e.dma_start(cosT[:, :], d["c_cos"]), tx),
                  S.dma("sp", lambda e, v: e.dma_start(sinT[:, :], d["c_sin"]), tx)]
            txt = transposes(S, XN, tln, NT)
            ready, users = project_qk(S, NT, txt, None, False, tc, lambda S: None)
            last = attend(S, NT, True, 0.25, ready, users,
                          lambda bank, before: project_v(S, NT, txt, None, False, bank, before))
            txt = transposes(S, ON, [last] * NT, NT)

            def write(S, t, ps, mm):
                return S.op("dve", lambda e, v: e.tensor_tensor(XR[:, t, :], ps, XR[:, t, :], ALU.add), mm)
            to = project_out(S, NT, txt, None, write)
            S.dma("sp", lambda e, v: e.dma_start(tokens3(x3_d, v["b"]), XR[:, :, :]), to)
            tln = layernorm(S, XR, to, XN, NT, txt)
            txt = transposes(S, XN, tln, NT, to)
            S.dma("sp", lambda e, v: e.dma_start(tokens3(xw_d[0:NTOK, :], v["b"])[:, :, 0:C], XN[:, :, :]), tln)
            route1(S, txt, placed)
            return S.close()

        def route1(S, txt, free):
            R = {nm: PB[i][:, 0:512].rearrange("p (t e) -> p t e", e=E1)
                 for i, nm in enumerate(["L", "rep", "mask", "ex", "pre", "pos", "w"])}
            sml = PB[7]
            top = sml[:, 0:64].rearrange("p (t k) -> p t k", k=8)
            v8 = sml[:, 64:128].rearrange("p (t k) -> p t k", k=8)
            s1 = sml[:, 128:136]
            s2 = sml[:, 136:144]

            def bc(ap):
                return ap.rearrange("p (t o) -> p t o", o=1).to_broadcast([128, NT, E1])
            for t in range(NT):
                for k in range(2):
                    mm = S.op("pe", lambda e, v, t=t, k=k: e.matmul(
                        BANKS[0][:, E1 * t:E1 * t + E1], XT[:, k, 128 * t:128 * t + 128], rw[:, k, :],
                        start=(k == 0), stop=(k == 1)), txt, sig=(t == NT - 1 and k == 1))

            def dv(fn, *w):
                dv.t = S.op("dve", fn, dv.t, *w)
                return dv.t
            dv.t = None
            dv(lambda e, v: e.tensor_copy(PB[0][:, 0:512], BANKS[0]), mm)
            for t in range(NT):
                tt = S.op("dve", lambda e, v, t=t: e.max(top[:, t, :], R["L"][:, t, :]), dv.t)
            for t in range(NT):
                t2 = S.op("dve", lambda e, v, t=t: e.match_replace(R["rep"][:, t, :], top[:, t, :], R["L"][:, t, :], NEG), tt)
            dv.t = t2
            dv(lambda e, v: e.tensor_tensor(R["mask"], R["rep"], R["L"], ALU.not_equal))
            tm = dv.t
            dv(lambda e, v: e.tensor_tensor(R["ex"], R["L"], bc(top[:, :, 0:1].rearrange("p t o -> p (t o)")), ALU.subtract))
            ta = S.op("act", lambda e, v: e.activation(R["ex"], R["ex"], ACT.Exp), dv.t)
            dv(lambda e, v: e.tensor_copy(R["pre"][:, 0, :], carry[:, :]))
            for t in range(1, NT):
                dv(lambda e, v, t=t: e.tensor_tensor(
                    R["pre"][:, t, :], R["pre"][:, t - 1, :], R["mask"][:, t - 1, :], ALU.add))
            tp = dv.t
            dv(lambda e, v: e.tensor_tensor(carry[:, :], R["pre"][:, NT - 1, :], R["mask"][:, NT - 1, :], ALU.add))
            S.op("pe", lambda e, v: e.matmul(BANKS[4], upper[:, :], PB[2][:, 0:512], start=True, stop=False), tm, sig=False)
            mm = S.op("pe", lambda e, v: e.matmul(BANKS[4], ones[:, :], PB[4][:, 0:512], start=False, stop=True), tp)
            dv(lambda e, v: e.tensor_reduce(s1, R["ex"], AX.X, ALU.add), ta)
            dv(lambda e, v: e.reciprocal(s1, s1))
            dv(lambda e, v: e.tensor_tensor(R["ex"], R["ex"], bc(s1), ALU.mult))
            dv(lambda e, v: e.tensor_tensor(R["ex"], R["ex"], R["mask"], ALU.mult))
            dv(lambda e, v: e.tensor_reduce(s2, R["ex"], AX.X, ALU.add))
            dv(lambda e, v: e.reciprocal(s2, s2))
            dv(lambda e, v: e.tensor_tensor(R["w"], R["ex"], bc(s2), ALU.mult))
            S.dma("sp", lambda e, v: e.dma_start(tokens3(xw_d[0:NTOK, :], v["b"])[:, :, C:C + E1], R["w"]), dv.t)
            dv(lambda e, v: e.tensor_copy(PB[5][:, 0:512], BANKS[4]), mm)
            dv(lambda e, v: e.scalar_tensor_tensor(R["mask"], R["pos"], float(CAP), R["mask"], ALU.is_lt, ALU.mult))
            dv(lambda e, v: e.scalar_tensor_tensor(
                R["pos"], R["pos"], -float(E1), eoff1[:, :, :], ALU.mult, ALU.add))
            dv(lambda e, v: e.tensor_tensor(R["pos"], R["pos"], R["mask"], ALU.mult))
            for t in range(NT):
                tt = S.op("dve", lambda e, v, t=t: e.max(v8[:, t, :], R["pos"][:, t, :]), dv.t)
            dv.t = tt
            dv(lambda e, v: e.tensor_scalar(sml[:, 192:256], sml[:, 64:128], -1.0, 16384.0, ALU.mult, ALU.add))
            dv(lambda e, v: e.tensor_copy(dlist[:, :], sml[:, 192:256]), free)
            dv(lambda e, v: e.tensor_copy(tlist[:, :], tokid[:, :]))
            dv(lambda e, v: e.tensor_scalar(tokid[:, :], tokid[:, :], float(T), None, ALU.add))

        def place_tokens(S):
            return [S.dma("pool", lambda e, v, i=i: e.indirect_dma_start(
                out=list_d, out_offset=bass.IndirectOffsetOnAxis(ap=dlist[:, i:i + 1], axis=0),
                in_=tlist[:, i // 8:i // 8 + 1], in_offset=None, bounds_check=E1 * CAP - 1, oob_is_err=False))
                for i in range(64)]

        def last_layer():
            S = new()
            wgu = QF
            wsd = W[:, 0:2, :, :].rearrange("p a k n -> p (a k) n")
            lw = [S.dma("sp", lambda e, v: e.dma_start(
                wgu[:, :, :], d["L1_ffn_shared_gate_up_w"].rearrange("(k p) n -> p k n", p=128))),
                S.dma("sp", lambda e, v: e.dma_start(
                    wsd, d["L1_ffn_shared_down_w"].rearrange("(k p) n -> p k n", p=128))),
                S.dma("sp", lambda e, v: e.dma_start(
                    rw[:, :, 0:1], d["L1_ffn_shared_gate_w"].rearrange("(k p) n -> p k n", p=128),
                    allow_slow_non_contiguous=True))]
            xw_b = xw_d[0:NTOK, 0:C].rearrange("(b t p) c -> b p t c", b=B, p=128)
            x3_b = x3_d.rearrange("(b t p) c -> b p t c", b=B, p=128)
            ye_b = ye_d[0:NTOK, :].rearrange("(b t p) c -> b p t c", b=B, p=128)
            out_b = out.rearrange("b (t p) c -> b p t c", p=128)
            placed = place_tokens(S)
            AT = [XR[:, 2 * m:2 * m + 2, :].rearrange("p a c -> p (a c)") for m in range(4)]
            VF = VA[:, :, :, :].rearrange("p t h d -> p (t h d)")
            WF = W[:, 2:6, :, :].rearrange("p a k n -> p (a k n)")
            PF = PH[:, :, :, :].rearrange("p a b n -> p (a b n)").bitcast(F32)
            NW, NX = 5, 6
            EW = [(VF[:, 768 * i:768 * i + 512].rearrange("p (k n) -> p k n", k=2),
                   VF[:, 768 * i + 512:768 * i + 768]) for i in range(NW)]
            XE = [WF[:, 320 * i:320 * i + 320] for i in range(NX)]
            YO = [PF[:, 1536 + 256 * i:1792 + 256 * i] for i in range(3)]
            XTe = [PF[:, 256 * i:256 * i + 256] for i in range(4)]
            ATe = [PF[:, 1024 + 128 * i:1152 + 128 * i] for i in range(4)]

            def sh(t):
                return PB[t // 4][:, 256 * (t % 4):256 * (t % 4) + 256]

            st = {"gu": [None, None], "xn": None, "xt": None, "at": None, "down": None, "gate": None}
            sh_done = {}

            def batch_head(b):
                l3 = [S.dma("sp", lambda e, v, h=h: e.dma_start(
                    PB[2 * b + h][:, :].rearrange("p (t c) -> p t c", c=C), x3_b[b, :, 4 * h:4 * h + 4, :]))
                    for h in range(2)]
                ln = S.dma("sp", lambda e, v: e.dma_start(XN[:, :, :], xw_b[b]), st["xn"])
                txt = transposes(S, XN, [ln] * NT, NT, st["gu"], st["down"])
                st["xn"] = txt
                for t in range(NT):
                    for k in range(2):
                        mm = S.op("pe", lambda e, v, t=t, k=k: e.matmul(
                            BANKS[4][:, t:t + 1], XT[:, k, 128 * t:128 * t + 128], rw[:, k, 0:1],
                            start=(k == 0), stop=(k == 1)), txt, lw, st["down"],
                            sig=(k == 1 and t == NT - 1))
                st["gate"] = S.op("act", lambda e, v: e.activation(rstd[:, :], BANKS[4][:, 0:NT], ACT.Sigmoid),
                                  mm, st["down"])
                st["l3"] = l3
                st["txt"] = txt

            def gate_up(b, c, m):
                pg, pu = BANKS[2 * (m % 2)], BANKS[2 * (m % 2) + 1]
                for dst, off in ((pg, 128 * m), (pu, IS + 128 * m)):
                    for k in range(2):
                        mm = S.op("pe", lambda e, v, dst=dst, off=off, k=k: e.matmul(
                            dst, wgu[:, k, off:off + 128], XT[:, k, 512 * c:512 * c + 512],
                            start=(k == 0), stop=(k == 1)), st["gu"][m % 2], st["txt"], lw,
                            sig=(k == 1 and dst is pu))
                s1 = S.op("act", lambda e, v: e.activation(AT[m], pg, ACT.Sigmoid), mm, st["at"])
                s2 = S.op("dve", lambda e, v: e.tensor_tensor(AT[m], AT[m], pg, ALU.mult), s1)
                st["gu"][m % 2] = S.op("dve", lambda e, v: e.tensor_tensor(AT[m], AT[m], pu, ALU.mult), s2)

            def down(b, c, t):
                tile = NT * b + 4 * c + t
                for k in range(4):
                    mm = S.op("pe", lambda e, v, k=k: e.matmul(
                        BANKS[4][:, 0:C], AT[k][:, 128 * t:128 * t + 128], wsd[:, k, :],
                        start=(k == 0), stop=(k == 3)), st["gu"], st["down"], st["gate"], sig=(k == 3))
                st["down"] = S.op("dve", lambda e, v: e.scalar_tensor_tensor(
                    sh(tile), BANKS[4][:, 0:C], rstd[:, 4 * c + t:4 * c + t + 1], sh(tile),
                    ALU.mult, ALU.add), mm, st["gate"], st["l3"])
                if t == 3:
                    st["at"] = mm
                sh_done[b] = st["down"]

            def pieces(b):
                out_ = [lambda: batch_head(b)]
                for c in range(2):
                    out_ += [lambda c=c, m=m: gate_up(b, c, m) for m in range(4)]
                    out_ += [lambda c=c, t=t: down(b, c, t) for t in range(4)]
                return out_

            ex = {}
            ux = {"pt": None, "pg": None, "py": None, "acc": None}

            def weights(x):
                if x >= E1:
                    return
                gu, dn = EW[x % NW]
                old = ex.get(x - NW, {}).get("down")
                ex.setdefault(x, {})["w"] = [
                    S.dma("sp", lambda e, v: e.dma_start(
                        gu, d["L1_ffn_expert_gate_up_w"][x].rearrange("(k p) n -> p k n", p=128)), old),
                    S.dma("sp", lambda e, v: e.dma_start(dn, d["L1_ffn_expert_down_w"][x]), old)]

            def gather(x):
                if x >= E1:
                    return
                old = ex.get(x - NX, {})
                ex.setdefault(x, {})["g"] = S.dma("pool", lambda e, v: e.indirect_dma_start(
                    out=XE[x % NX], out_offset=None, in_=xw_d,
                    in_offset=bass.IndirectOffsetOnAxis(ap=lists[:, x:x + 1], axis=0)), ll,
                    old.get("y"))

            def turn(x):
                q = ex[x]
                for k in range(2):
                    mm = S.op("pe", lambda e, v, k=k: e.transpose(
                        BANKS[6][:, 128 * k:128 * k + 128], XE[x % NX][:, 128 * k:128 * k + 128], ident[:, :]),
                        q["g"], ux["pt"], sig=(k == 1))
                q["xt"] = ux["pt"] = S.op("act", lambda e, v: e.activation(
                    XTe[x % 4], BANKS[6][:, 0:256], ACT.Copy), mm)

            def up(x):
                q = ex[x]
                gu, dn = EW[x % NW]
                for m in range(2):
                    for k in range(2):
                        mm = S.op("pe", lambda e, v, k=k, m=m: e.matmul(
                            BANKS[7][:, 128 * m:128 * m + 128], gu[:, k, 128 * m:128 * m + 128],
                            XTe[x % 4][:, 128 * k:128 * k + 128], start=(k == 0), stop=(k == 1)),
                            q["xt"], q["w"], ux["pg"], sig=(k == 1 and m == 1))
                at = ATe[x % 4]
                s1 = S.op("act", lambda e, v: e.activation(at, BANKS[7][:, 0:128], ACT.Sigmoid), mm)
                s2 = S.op("dve", lambda e, v: e.tensor_tensor(at, at, BANKS[7][:, 0:128], ALU.mult), s1)
                q["at"] = ux["pg"] = S.op("dve", lambda e, v: e.tensor_tensor(
                    at, at, BANKS[7][:, 128:256], ALU.mult), s2)

            def down_x(x):
                q = ex[x]
                gu, dn = EW[x % NW]
                mm = S.op("pe", lambda e, v: e.matmul(
                    BANKS[5][:, 0:C], ATe[x % 4], dn, start=True, stop=True), q["at"], q["w"], ux["py"])
                q["down"] = mm
                q["y"] = ux["py"] = S.op("dve", lambda e, v: e.tensor_scalar(
                    YO[x % 3], BANKS[5][:, 0:C], XE[x % NX][:, C + x:C + x + 1], None, ALU.mult), mm,
                    ex.get(x - 3, {}).get("acc"))

            def add(x):
                ux["acc"] = ex[x]["acc"] = S.dma("pool", lambda e, v: e.indirect_dma_start(
                    out=ye_d, out_offset=bass.IndirectOffsetOnAxis(ap=lists[:, x:x + 1], axis=0),
                    in_=YO[x % 3], in_offset=None, compute_op=ALU.add), ex[x]["y"], ux["acc"])

            for x in range(NW - 1):
                weights(x)
            first = pieces(0) + pieces(1)
            for f in first[:len(first) // 2]:
                f()
            ll = S.dma("sp", lambda e, v: e.dma_start(
                lists[:, :], list_d.rearrange("(s e) o -> s (e o)", e=E1)), placed)
            for x in range(2):
                gather(x)
            for f in first[len(first) // 2:]:
                f()
            rest = pieces(2) + pieces(3)
            n_rest = len(rest)
            for i in range(E1 + 3):
                if i < E1:
                    turn(i)
                    gather(i + 2)
                if 0 <= i - 1 < E1:
                    up(i - 1)
                if 0 <= i - 2 < E1:
                    down_x(i - 2)
                    weights(i - 2 + NW)
                if 0 <= i - 2 < E1:
                    add(i - 2)
                if i == 0:
                    weights(NW - 1)
                while rest and (n_rest - len(rest)) < n_rest * (i + 1) / E1:
                    rest.pop(0)()
            buf = [XN, QF[:, :, :].rearrange("p a n -> p (a n)").rearrange("p (t c) -> p t c", c=C)]
            free = [st["xn"], [st["gu"]]]
            for b in range(B):
                ly = S.dma("sp", lambda e, v, b=b: e.dma_start(buf[b % 2][:, :, :], ye_b[b]), ux["acc"], free[b % 2])
                tk = []
                for h in range(2):
                    tk.append(S.op("dve", lambda e, v, b=b, h=h: e.tensor_tensor(
                        PB[2 * b + h][:, :], PB[2 * b + h][:, :],
                        buf[b % 2][:, 4 * h:4 * h + 4, :].rearrange("p t c -> p (t c)"), ALU.add), ly, sh_done[b]))
                    S.dma("sp", lambda e, v, b=b, h=h: e.dma_start(
                        out_b[b, :, 4 * h:4 * h + 4, :], PB[2 * b + h][:, :].rearrange("p (t c) -> p t c", c=C)), tk[h])
                free[b % 2] = tk
            return S.close()


        secs = {"constants": constants(), "l0_attn": l0_attn(), "pre_ffn": pre_ffn(),
                "pre_l1": pre_l1(), "l1_attn": l1_attn(), "last_layer": last_layer()}
        for nt in range(1, NT + 1):
            secs[f"ffn{nt}"] = ffn_unit(nt)

        def emit(key, e):
            def barrier():
                if key == "sp":
                    e.wait_ge(A1, 4)
                    for s in work:
                        e.sem_clear(s)
                    e.sem_clear(A1)
                    e.sem_clear(B2)
                    e.sem_inc(A2, 1)
                    e.wait_ge(B1, 4)
                    e.sem_clear(A2)
                    e.sem_clear(B1)
                    e.sem_inc(B2, 1)
                else:
                    if key == "pool":
                        e.dma_reset()
                    e.drain().then_inc(A1, 1)
                    e.wait_ge(A2, 1)
                    e.drain().then_inc(B1, 1)
                    e.wait_ge(B2, 1)

            def run(name, env):
                for f in secs[name].q[key]:
                    f(e, env)

            run("constants", {})
            barrier()
            with e.Fori(0, B) as b:
                run("l0_attn", {"b": b})
                barrier()
            run("pre_ffn", {})
            barrier()
            with e.Fori(0, B) as b:
                with e.Fori(0, E0) as ex:
                    u = b * E0 + ex
                    tiles = e.value_load(cnt[0:1, bass.ds(u, 1)], min_val=0, max_val=NT)
                    for nt in range(1, NT + 1):
                        with e.If(tiles == nt):
                            run(f"ffn{nt}", {"b": b, "ex": ex, "u": u})
                    barrier()
            run("pre_l1", {})
            barrier()
            with e.Fori(0, B) as b:
                run("l1_attn", {"b": b})
                barrier()
            run("last_layer", {})
            barrier()

        block = ctx.enter_context(nc.Block())

        @block.sync
        def _(e):
            emit("sp", e)

        @block.tensor
        def _(e):
            emit("pe", e)

        @block.scalar
        def _(e):
            emit("act", e)

        @block.vector
        def _(e):
            emit("dve", e)

        @block.gpsimd
        def _(e):
            emit("pool", e)


def shape_constants():
    bf = mybir.dt.np(BF16)
    f = np.float32
    k = {}
    k["c_ident"] = np.eye(128, dtype=f)
    k["c_identb"] = np.eye(128, dtype=f).astype(bf)
    k["c_ones"] = np.ones((128, 128), f)
    k["c_upper"] = np.triu(np.ones((128, 128), f), 1)
    k["c_iota"] = np.arange(T, dtype=f)[None, :]
    mask = np.where(np.triu(np.ones((128, 128)), 1) > 0, f(NEG), f(0)).astype(f)
    k["c_maskA"] = mask.astype(bf)
    k["c_maskB"] = np.ascontiguousarray(mask.T).astype(bf)
    k["c_e4"] = np.tile(np.arange(E0, 0, -1, dtype=f), (128, NT))
    k["c_eoff"] = np.tile(np.arange(E0, dtype=f) * UROWS, (128, NT))
    k["c_eoff1"] = np.tile(f(16384) - np.arange(E1, dtype=f), (128, NT))
    k["c_tokid"] = (np.arange(NT)[None, :] * 128 + np.arange(128)[:, None]).astype(f)
    k["c_list"] = (NTOK + np.arange(E1 * CAP) // E1).astype(np.int32)[:, None]
    slopes = (f(2.0) ** (f(-0.5) * np.arange(1, H + 1, dtype=f))).astype(f)
    al = (slopes[:, None] * np.arange(T, dtype=f)[None, :]).astype(f) * f(4.0)
    parts = []
    r = al
    for _ in range(3):
        p = r.astype(bf)
        parts.append(p)
        r = (r - p.astype(f)).astype(f)
    k["c_alibi"] = np.stack(parts)
    k["c_rows"] = np.ones((KB - 96, H * T), dtype=bf)
    half = D // 2
    inv = (f(10000.0) ** (-np.arange(0, half, dtype=f) * f(2.0) / f(D))).astype(f)
    ang = np.arange(T, dtype=f)[:, None] * inv[None, :]
    cos, sin = np.cos(ang).astype(f), np.sin(ang).astype(f)
    ct = np.repeat(cos.T, 2, axis=0)
    sn = np.repeat(sin.T, 2, axis=0)
    sn[0::2] *= f(-1)
    k["c_cos"] = np.ascontiguousarray(np.tile(ct, (8, 1)))
    k["c_sin"] = np.ascontiguousarray(np.tile(sn, (8, 1)))
    return k


def kernel(**inputs):
    import concourse.bacc as bacc
    from concourse.bass_utils import run_bass_kernel_spmd

    nc = bacc.Bacc("TRN2", target_bir_lowering=False, num_devices=1)
    a = {n: np.ascontiguousarray(inputs[n]) for n in inputs}
    a["L0_attn_x"] = a["L0_attn_x"].reshape(NTOK, C)
    swap = np.arange(C).reshape(-1, 2)[:, ::-1].reshape(-1)
    for nm, src in (("q", "Wq"), ("k", "Wk"), ("v", "Wv"), ("o", "Wo")):
        a["w1_" + nm] = np.ascontiguousarray(a.pop("L1_attn_" + src).T)
    for nm in ("q", "k"):
        a[f"w1_{nm}s"] = np.ascontiguousarray(a["w1_" + nm][:, swap])
    a.update(shape_constants())
    arrays, d = {}, {}
    for n, x in a.items():
        arrays["in_" + n] = x
        d[n] = nc.dram_tensor("in_" + n, x.shape, mybir.dt.from_np(x.dtype), kind="ExternalInput").ap()
    out = nc.dram_tensor("out_0", (B, T, C), F32, kind="ExternalOutput").ap()
    build(nc, d, out)
    r = run_bass_kernel_spmd(nc, [arrays], core_ids=[0])
    return r.results[0]["out_0"]
```

```python
from contextlib import ExitStack

import numpy as np

import concourse.bass as bass
from concourse import mybir

ALU = mybir.AluOpType
ACT = mybir.ActivationFunctionType
AX = mybir.AxisListType
F32 = mybir.dt.float32
BF16 = mybir.dt.bfloat16
I32 = mybir.dt.int32

B, T, C, H, D = 4, 1024, 256, 16, 16
NT = T // 128
E0 = 4
UROWS = 1152
E1, I1, IS, CAP = 64, 128, 512, 128
NTOK = B * T
EPS = 1e-5
NEG = -1e30
ENGINES = ("pe", "act", "dve", "pool", "sp")
KA = 99
KB = 101


class Section:

    def __init__(self, sems, dma_sems):
        self.q = {k: [] for k in ENGINES}
        self.sems = sems
        self.count = {k: 0 for k in sems}
        self.seen = {k: {} for k in ENGINES}
        self.dma_sems = dma_sems
        self.dma_n = {k: 0 for k in dma_sems}
        self.dma_val = {k: [0] * len(v) for k, v in dma_sems.items()}

    def wait(self, eng, *tokens):
        for tok in tokens:
            if tok is None:
                continue
            if not (isinstance(tok, tuple) and len(tok) == 2 and isinstance(tok[1], int)):
                self.wait(eng, *tok)
                continue
            sem, val = tok
            if self.seen[eng].get(sem.name, 0) >= val:
                continue
            self.seen[eng][sem.name] = val
            self.q[eng].append(lambda e, env, s=sem, v=val: e.wait_ge(s, v))

    def op(self, eng, fn, *waits, sig=True):
        self.wait(eng, *waits)
        if not sig:
            self.q[eng].append(fn)
            return None
        self.count[eng] += 1
        sem = self.sems[eng]
        self.q[eng].append(lambda e, env: fn(e, env).then_inc(sem, 1))
        return (sem, self.count[eng])

    def dma(self, eng, fn, *waits):
        pool = self.dma_sems[eng]
        i = self.dma_n[eng] % len(pool)
        self.dma_n[eng] += 1
        if self.dma_val[eng][i]:
            self.wait(eng, (pool[i], self.dma_val[eng][i]))
        self.wait(eng, *waits)
        self.dma_val[eng][i] += 16
        sem = pool[i]
        self.q[eng].append(lambda e, env: fn(e, env).then_inc(sem, 16))
        return (sem, self.dma_val[eng][i])

    def close(self):
        for eng, pool in self.dma_sems.items():
            for i, sem in enumerate(pool):
                if self.dma_val[eng][i]:
                    self.wait(eng, (sem, self.dma_val[eng][i]))
        return self


class Rows:

    def __init__(self, bufs, per, c):
        self.v = [x[:, 0:per * c].rearrange("p (t c) -> p t c", c=c) for x in bufs]
        self.per = per

    def __getitem__(self, ix):
        p, t, c = ix
        return self.v[t // self.per][p, t % self.per, c]


def chunks(a, b, step=512):
    out = []
    while a < b:
        c = min(b, (a // step + 1) * step)
        out.append((a, c))
        a = c
    return out


def build(nc, d, out):
    ctx = ExitStack()
    with ctx:
        def sb(name, shape, dt=F32):
            return ctx.enter_context(nc.sbuf_tensor(name, shape, dt))

        def sem(name):
            return ctx.enter_context(nc.semaphore(name))

        def dram(name, shape, dt=F32):
            return nc.dram_tensor(name, shape, dt, kind="Internal").ap()

        x1_d = dram("x1_d", (NTOK, C))
        xg_d = dram("xg_d", ((B * E0 + 1) * UROWS, C))
        yg_d = dram("yg_d", (B * E0 * UROWS, C))
        rt_d = dram("rt_d", (B + 1, 128, NT * 4))
        mk_d = dram("mk_d", (B * E0 + 1, T), BF16)
        cnt_d = dram("cnt_d", (B * E0, 1), I32)
        qk_d = [dram(f"qk_d{i}", (3, C, T), BF16) for i in range(2)]
        x3_d = dram("x3_d", (NTOK, C))
        xw_d = dram("xw_d", (NTOK + 128, C + E1))
        list_d = dram("list_d", (E1 * CAP, 1), I32)
        ye_d = dram("ye_d", (NTOK + 128, C))

        ident = sb("ident", [128, 128])
        identb = sb("identb", [128, 128], BF16)
        ones = sb("ones", [128, 128])
        upper = sb("upper", [128, 128])
        maskA = sb("maskA", [128, 128], BF16)
        maskB = sb("maskB", [128, 128], BF16)
        iota = sb("iota", [1, T])
        e4 = sb("e4", [128, NT, E0])
        eoff = sb("eoff", [128, NT, E0])
        eoff1 = sb("eoff1", [128, NT, E1])
        tokid = sb("tokid", [128, NT])
        carry = sb("carry", [128, E1])
        base = sb("base", [128, 1])
        cnt = sb("cnt", [1, B * E0 + 1], I32)
        XR = sb("XR", [128, NT, C])
        XN = sb("XN", [128, NT, C])
        XT = sb("XT", [128, 2, T])
        W = sb("W", [128, 6, 2, C])
        bq = sb("bq", [128, 2, 2])
        bv = sb("bv", [1, C])
        bo = sb("bo", [128, C])
        rw = sb("rw", [128, 2, E1])
        rb = sb("rb", [128, E0])
        QF = sb("QF", [128, 2, T])
        PH = sb("PH", [128, 3, 2, T], BF16)
        QS = sb("QS", [KB, H, T], BF16)
        KS = sb("KS", [KB, H, T], BF16)
        VA = sb("VA", [128, NT, H, 32])
        PB = [sb(f"PB{i}", [128, T]) for i in range(8)]
        M1 = sb("M1", [128, 4, NT, 4])
        MHL = sb("MHL", [128, 4, NT, 8], BF16)
        MR = sb("MR", [8, 2, T], BF16)
        RD = sb("RD", [128, NT, 4])
        bst = sb("bst", [128, NT, 6])
        mv = sb("mv", [128, NT, 2])
        rstd = sb("rstd", [128, NT])
        mhalf = sb("mhalf", [128, NT])
        Z = sb("Z", [128, C])
        ON = XN
        NR = Rows([PB[4], PB[5]], 4, C)
        OT = [PB[6][:, 0:512], PB[6][:, 512:1024]]
        cosT = PB[0]
        sinT = PB[1]
        sm = sb("sm", [128, 24, 32])
        smi = sb("smi", [128, 8, 32], I32)
        dlist = sb("dlist", [128, 64], I32)
        tlist = sb("tlist", [128, NT], I32)
        lists = sb("lists", [128, E1], I32)

        PSUM = ctx.enter_context(nc.psum_tensor("PSUM", [128, 8, 512], F32))
        BANKS = [PSUM[:, i, :] for i in range(8)]
        PR = [PSUM[:, 2 * i:2 * i + 2, :].rearrange("p a n -> p (a n)") for i in range(2)]
        PX = [BANKS[i] for i in (4, 5, 6)]
        PO = BANKS[7]

        sems = {k: sem("s_" + k) for k in ENGINES}
        fsems = {k: sem("f_" + k) for k in ENGINES[:3]}
        fdma = {"sp": [sem(f"fd_sp{i}") for i in range(24)]}
        dma_sems = {"sp": [sem(f"d_sp{i}") for i in range(20)],
                    "pool": [sem(f"d_pool{i}") for i in range(10)]}
        A1, A2, B1, B2 = [sem(f"bar{i}") for i in range(4)]
        attn_sems = [sems[k] for k in ENGINES[:4]] + dma_sems["sp"] + dma_sems["pool"]
        unit_sems = [sems[k] for k in ENGINES[:3]] + dma_sems["sp"] + list(fsems.values()) + fdma["sp"]

        def new():
            return Section(sems, dma_sems)


        def load_w(S, i, ap, *waits):
            return S.dma("sp", lambda e, v: e.dma_start(
                W[:, i, :, :], ap(v).rearrange("(k p) n -> p k n", p=128)), *waits)

        def bcast_load(S, dst, ap, n, *waits):
            return S.dma("sp", lambda e, v: e.dma_start(dst, ap(v).to_broadcast([128, n])), *waits)

        def layernorm(S, src, tsrc, dst, nt, *free):
            t = []
            for i in range(nt):
                a = S.op("dve", lambda e, v, i=i: e.bn_stats(bst[:, i, :], src[:, i, :]), tsrc[i])
            for i in range(nt):
                a = S.op("dve", lambda e, v, i=i: e.bn_aggr(mv[:, i, :], bst[:, i, :]), a)
            a = S.op("dve", lambda e, v: e.tensor_scalar(rstd[:, 0:nt], mv[:, 0:nt, 1], EPS, None, ALU.add), a)
            p = S.op("pool", lambda e, v: e.tensor_tensor(
                rstd[:, 0:nt], rstd[:, 0:nt], mhalf[:, 0:nt], ALU.pow), a)
            for i in range(nt):
                t.append(S.op("dve", lambda e, v, i=i: e.tensor_scalar(
                    dst[:, i, :], src[:, i, :], mv[:, i, 0:1], rstd[:, i:i + 1],
                    ALU.subtract, ALU.mult), a, p, *free))
            return t

        def transposes(S, src, tsrc, nt, *free, dst=XT):
            toks = []
            n = 0
            users = [None] * 4
            for c0 in range(0, nt, 4):
                w = min(4, nt - c0)
                for k in range(2):
                    bank = BANKS[n % 4]
                    for i in range(w):
                        a = S.op("pe", lambda e, v, i=i, k=k, c0=c0, bank=bank: e.transpose(
                            bank[:, 128 * i:128 * i + 128], src[:, c0 + i, 128 * k:128 * k + 128],
                            ident[:, :]), tsrc[c0 + i], users[n % 4], sig=(i == w - 1))
                    eng = "dve" if n % 2 else "act"

                    def ev(e, v, k=k, c0=c0, w=w, bank=bank, eng=eng):
                        o = dst[:, k, 128 * c0:128 * (c0 + w)]
                        return (e.tensor_copy(o, bank[:, 0:128 * w]) if eng == "dve"
                                else e.activation(o, bank[:, 0:128 * w], ACT.Copy))
                    users[n % 4] = S.op(eng, ev, a, *free)
                    toks.append(users[n % 4])
                    n += 1
            return toks

        def load_half(S, qk, g, n, stores, h0=0, h1=8):
            parts = (0, 1, 2, 0, 1, 0) if qk == 0 else (0, 0, 0, 1, 1, 2)
            dst = QS if qk == 0 else KS
            return [S.dma("sp", lambda e, v, s=s, p=p: e.dma_start(
                dst[16 * s:16 * s + 16, 8 * g + h0:8 * g + h1, 0:n],
                qk_d[qk][p, 128 * g + 16 * h0:128 * g + 16 * h1, 0:n].rearrange("(h d) n -> d h n", d=16)),
                stores[p]) for s, p in enumerate(parts)]

        def project_qk(S, nt, txt, wtok, bias, rope, kadd, banks=BANKS, halves=(0, 1)):
            n = 128 * nt
            N = len(banks)
            users = [None] * N
            nb = 0
            add = kadd(S)
            ready = []
            last_st = [None, None]
            for g in range(2):
                first = ready[0] if g == 1 and len(halves) == 2 else None
                done = [[add], [add]]
                for qk in range(2):
                    evs = []
                    for (a, b) in chunks(0, n):
                        m = b - a
                        mats = [(banks[nb % N], qk)]
                        if rope:
                            mats.append((banks[(nb + 1) % N], qk + 4))
                        for bank, wi in mats:
                            for k in range(2):
                                mm = S.op("pe", lambda e, v, k=k, g=g, wi=wi, a=a, b=b, bank=bank: e.matmul(
                                    bank[:, 0:b - a], W[:, wi, k, 128 * g:128 * g + 128],
                                    XT[:, k, a:b], start=(k == 0), stop=(k == 1)),
                                    txt, wtok, users[nb % N], users[(nb + 1) % N] if rope else None,
                                    sig=(k == 1))
                        o = QF[:, qk, a:b]
                        if not rope:
                            def f1(e, v, o=o, i=mats[0][0][:, 0:m], g=g, qk=qk):
                                if bias:
                                    return e.activation(o, i, ACT.Identity, bias=bq[:, qk, g:g + 1])
                                return e.activation(o, i, ACT.Copy)
                            t1 = S.op("act", f1, mm, last_st[qk])
                            users[nb % N] = t1
                            nb += 1
                        else:
                            t1 = S.op("dve", lambda e, v, o=o, i=mats[0][0][:, 0:m], c=cosT[:, a:b]:
                                      e.tensor_tensor(o, i, c, ALU.mult), mm, last_st[qk], rope)
                            t2 = S.op("dve", lambda e, v, o=PB[2][:, a:b], i=mats[1][0][:, 0:m], c=sinT[:, a:b]:
                                      e.tensor_tensor(o, i, c, ALU.mult), mm, rope)
                            t1 = S.op("dve", lambda e, v, o=o, i=PB[2][:, a:b]:
                                      e.tensor_tensor(o, o, i, ALU.add), t1, t2)
                            users[nb % N] = users[(nb + 1) % N] = t2
                            nb += 2
                        evs.append(t1)
                    f = QF[:, qk, 0:n]
                    ph = [PH[:, p, qk, 0:n] for p in range(3)]
                    th = S.op("act", lambda e, v, o=ph[0], i=f: e.activation(o, i, ACT.Copy), evs, last_st[qk])
                    tr = S.op("dve", lambda e, v, o=f, i=ph[0]: e.tensor_tensor(o, o, i, ALU.subtract), evs, th)
                    tm = S.op("dve", lambda e, v, o=ph[1], i=f: e.tensor_copy(o, i), tr, last_st[qk])
                    tl = S.op("dve", lambda e, v, o=ph[2], i=f, j=ph[1]: e.tensor_tensor(o, i, j, ALU.subtract), tm)
                    stores = []
                    for p, tt in ((0, th), (1, tm), (2, tl)):
                        stores.append(S.dma("sp", lambda e, v, p=p, g=g, qk=qk: e.dma_start(
                            qk_d[qk][p, 128 * g:128 * g + 128, 0:n], PH[:, p, qk, 0:n]), tt, first))
                    last_st[qk] = stores + [tl]
                    if g in halves and len(halves) == 2 and g == 0:
                        for i in range(2):
                            done[i] += load_half(S, qk, g, n, stores, 4 * i, 4 * i + 4)
                    elif g in halves:
                        for x in [load_half(S, qk, g, n, stores)]:
                            done[0] += x
                            done[1] += x
                ready += done
            return ready, users

        def project_v(S, nt, txt, wtok, bias, bank, before):
            toks = {}

            def tile(t):
                i = t % len(bank)
                if bias:
                    S.op("pe", lambda e, v, t=t, i=i: e.matmul(
                        bank[i][:, 0:C], ones[0:1, :], bv[0:1, :], start=True, stop=False),
                        txt, wtok, before[i], sig=False)
                for k in range(2):
                    mm = S.op("pe", lambda e, v, k=k, t=t, i=i: e.matmul(
                        bank[i][:, 0:C], XT[:, k, 128 * t:128 * t + 128], W[:, 2, k, :],
                        start=(k == 0 and not bias), stop=(k == 1)), txt, wtok, before[i], sig=(k == 1))
                before[i] = S.op("act", lambda e, v, t=t, i=i: e.activation(
                    VA[:, t, :, 0:16], bank[i][:, 0:C].rearrange("p (h d) -> p h d", d=16), ACT.Copy), mm)
                toks[t] = before[i]
            return toks, [lambda t=t: tile(t) for t in range(nt)]

        def attend(S, nt, causal, scale, ready, users, vproj, inject=None, pfree=None):
            n = 128 * nt
            before = [users[4], users[5], users[6]]
            tv, fillers = vproj(PX, before)
            st = {"pr": [[users[0], users[1]], [users[2], users[3]]], "po": users[7],
                  "pb": [pfree] * 16, "mr": [None, None], "qsm": {}, "ot": [None, None], "m1": {},
                  "npr": 0, "nps": 0, "step": 0, "rd": None}
            hb = 1 if causal or nt > 4 else 2 if nt > 2 else 4
            eb = 1 if causal or nt > 2 else 2
            p1 = [[(qt, j) for qt in range(nt) for j in range(0, 4, hb)] for _ in range(4)]
            steps = [(qc, kt) for qc in range((n + 511) // 512)
                     for kt in range(nt) if not causal or 128 * kt < min(n, 512 * qc + 512)]

            def pass1(g, qt, j):
                h = 4 * g + j
                kn = 128 * (qt + 1) if causal else n
                r = st["npr"] % 2
                st["npr"] += 1
                buf = PR[r]
                w = 1024 // hb
                for x in range(hb):
                    for (a, b) in chunks(0, kn):
                        diag = causal and b == kn
                        mm = S.op("pe", lambda e, v, a=a, b=b, x=x, diag=diag: e.matmul(
                            buf[:, w * x + a:w * x + b], QS[0:KA, h + x, 128 * qt:128 * qt + 128],
                            KS[0:KA, h + x, a:b], start=True, stop=not diag, skip_group_check=diag),
                            ready[g], st["pr"][r], sig=(b == kn and x == hb - 1 and not diag))
                if causal:
                    mm = S.op("pe", lambda e, v: e.matmul(
                        buf[:, kn - 128:kn], identb[:, :], maskA[:, :], start=False, stop=True,
                        skip_group_check=True))
                st["pr"][r] = S.op("dve", lambda e, v: e.tensor_reduce(
                    M1[:, g, qt, j:j + hb], buf.rearrange("p (x w) -> p x w", x=hb)[:, :, 0:kn], AX.X,
                    ALU.max), mm)
                st["m1"][g] = st["pr"][r]

            def m_rows(g):
                m1 = M1[:, g, 0:nt, :]
                hi = MHL[:, g, 0:nt, 0:4]
                lo = MHL[:, g, 0:nt, 4:8]
                a = S.op("dve", lambda e, v: e.tensor_scalar(hi, m1, -1.0, None, ALU.mult), st["m1"][g])
                a = S.op("dve", lambda e, v: e.scalar_tensor_tensor(
                    lo, m1, -1.0, hi, ALU.mult, ALU.subtract), a)
                r = st["npr"] % 2
                st["npr"] += 1
                buf = PR[r]
                for t in range(nt):
                    mm = S.op("pe", lambda e, v, t=t: e.matmul(
                        buf[0:8, 128 * t:128 * t + 128], MHL[:, g, t, :], identb[:, :],
                        start=True, stop=True), a, st["pr"][r], sig=(t == nt - 1))
                c = S.op("act", lambda e, v: e.activation(MR[:, g % 2, 0:n], buf[0:8, 0:n], ACT.Copy),
                         mm, st["mr"][g % 2])
                st["pr"][r] = c
                ds = []
                for r in range(2):
                    ds.append(S.dma("sp", lambda e, v, r=r: e.dma_start(
                        QS[KA + r:KA + r + 1, 4 * g:4 * g + 4, 0:n], MR[4 * r:4 * r + 4, g % 2, 0:n]), c))
                st["mr"][g % 2] = ds
                st["qsm"][g] = ds

            def span(qc, kt):
                return max(512 * qc, 128 * kt if causal else 0), min(n, 512 * qc + 512)

            def pbuf(i, j):
                i = 4 * (i % 3) + j
                return PB[i // 2][:, 512 * (i % 2):512 * (i % 2) + 512]

            def pass2(g, qc, kt, j, step):
                h = 4 * g + j
                q0, q1 = span(qc, kt)
                w = q1 - q0
                diag = causal and q0 == 128 * kt
                x = st["nps"] % 3
                st["nps"] += 1
                ps = PX[x]
                for y in range(eb):
                    mm = S.op("pe", lambda e, v, y=y: e.matmul(
                        ps[:, 256 * y:256 * y + w], KS[0:KB, h + y, 128 * kt:128 * kt + 128],
                        QS[0:KB, h + y, q0:q1], start=True, stop=not diag, skip_group_check=diag),
                        ready[g], st["qsm"][g], before[x], sig=(not diag and y == eb - 1))
                if diag:
                    mm = S.op("pe", lambda e, v: e.matmul(
                        ps[:, 0:128], identb[:, :], maskB[:, :], start=False, stop=True,
                        skip_group_check=True))
                i = 4 * (step % 3) + j
                if eb == 1:
                    po_, pi_ = pbuf(step, j)[:, 0:w], ps[:, 0:w]
                else:
                    po_ = PB[i // 2][:, :].rearrange("p (y n) -> p y n", y=2)[:, :, 0:w]
                    pi_ = ps.rearrange("p (y n) -> p y n", y=2)[:, :, 0:w]
                t = S.op("act", lambda e, v: e.activation(po_, pi_, ACT.Exp, scale=scale), mm,
                         st["pb"][i], st["pb"][i + eb - 1])
                before[x] = t
                if g == 1:
                    fence["heads"] = t
                for y in range(eb):
                    st[("p", step, j + y)] = t

            def pv(g, qc, kt, step):
                q0, q1 = span(qc, kt)
                o = q0 - 512 * qc
                w = q1 - q0
                lastk = nt - 1 if not causal else min(nt, 4 * qc + 4) - 1
                for j in range(4):
                    mm = S.op("pe", lambda e, v, j=j: e.matmul(
                        PO[32 * j:32 * j + 32, o:o + w], VA[:, kt, 4 * g + j, :], pbuf(step, j)[:, 0:w],
                        start=(kt == 0), stop=(kt == lastk), skip_group_check=True),
                        st[("p", step, j)], tv[kt], st["po"], sig=(j == 3))
                for j in range(4):
                    st["pb"][4 * (step % 3) + j] = mm
                if kt == lastk:
                    full = q1 - 512 * qc
                    st["po"] = S.op("act", lambda e, v: e.activation(OT[qc][:, 0:full], PO[:, 0:full], ACT.Copy),
                                    mm, st["ot"][qc])
                    return True

            def norm(g, qc, tok):
                tiles = min(nt, 4 * qc + 4) - 4 * qc
                r = st["npr"] % 2
                st["npr"] += 1
                buf = PR[r]
                for t in range(tiles):
                    mm = S.op("pe", lambda e, v, t=t: e.transpose(
                        buf[:, 128 * t:128 * t + 128], OT[qc][:, 128 * t:128 * t + 128], ident[:, :]),
                        tok, st["pr"][r], sig=(t == tiles - 1))
                st["ot"][qc] = mm
                view = buf[:, 0:128 * tiles].rearrange("p (t j d) -> p t j d", j=4, d=32)
                t0 = 4 * qc
                c = S.op("dve", lambda e, v: e.reciprocal(RD[:, 0:tiles, :], view[:, :, :, 16]), mm,
                         st["rd"])
                for t in range(tiles):
                    m = S.op("dve", lambda e, v, t=t: e.tensor_tensor(
                        ON[:, t0 + t, 64 * g:64 * g + 64].rearrange("p (j d) -> p j d", d=16),
                        view[:, t, :, 0:16],
                        RD[:, t, :].rearrange("p (j o) -> p j o", o=1).to_broadcast([128, 4, 16]),
                        ALU.mult), c, mm)
                st["pr"][r] = m
                st["rd"] = m
                return m

            ahead = 4 if nt <= 2 else 1
            while fillers and causal:
                fillers.pop(0)()
            for g in range(ahead):
                for i, (qt, j) in enumerate(p1[g]):
                    pass1(g, qt, j)
                    if fillers and i % 3 == 1:
                        fillers.pop(0)()
                while fillers and g == 0:
                    fillers.pop(0)()
                m_rows(g)
            late = []
            last = None
            nstep = 0
            fence = {"v": dict(tv)}
            for g in range(4):
                if inject and g == (2 if nt <= 2 else 3):
                    inject(st["pr"], fence)
                nxt = list(p1[g + 1]) if g + 1 < 4 and g + 1 >= ahead else []
                n1 = len(nxt)
                need_m = bool(nxt)
                n2 = 4 * len(steps)
                i2 = 0
                for (qc, kt) in steps:
                    for j in range(0, 4, eb):
                        pass2(g, qc, kt, j, nstep)
                        i2 += eb
                        while late and late[0][0] <= 4 * nstep + j:
                            _, f = late.pop(0)
                            f()
                        while nxt and (n1 - len(nxt)) < n1 * i2 / (0.82 * n2):
                            pass1(g + 1, *nxt.pop(0))
                        if need_m and not nxt:
                            need_m = False
                            late.append((4 * nstep + j + 2, lambda g=g: m_rows(g + 1)))
                            late.sort(key=lambda x: x[0])

                    def fpv(g=g, qc=qc, kt=kt, step=nstep):
                        nonlocal last
                        if pv(g, qc, kt, step):
                            def fn(tok=st["po"]):
                                nonlocal last
                                last = norm(g, qc, tok)
                            late.append((4 * step + 3 + 6, fn))
                            late.sort(key=lambda x: x[0])
                    late.append((4 * nstep + 3 + 2, fpv))
                    late.sort(key=lambda x: x[0])
                    nstep += 1
                if need_m:
                    while nxt:
                        pass1(g + 1, *nxt.pop(0))
                    m_rows(g + 1)
                if g + 1 < 4 and g + 1 not in st["qsm"]:
                    for x in [x for x in late]:
                        late.remove(x)
                        x[1]()
            while late:
                late.pop(0)[1]()
            return last

        def project_out(S, nt, txt, wtok, write, *free, src=XT):
            toks = []
            users = [None] * 8
            for t in range(nt):
                bank = BANKS[t % 8]
                for k in range(2):
                    mm = S.op("pe", lambda e, v, k=k, t=t, bank=bank: e.matmul(
                        bank[:, 0:C], src[:, k, 128 * t:128 * t + 128], W[:, 3, k, :],
                        start=(k == 0), stop=(k == 1)), txt, wtok, free, users[t % 8], sig=(k == 1))
                users[t % 8] = write(S, t, bank[:, 0:C], mm)
                toks.append(users[t % 8])
            return toks

        def row(v):
            return bass.ds(v, 1)


        def constants():
            S = new()
            for dst, name in ((ident, "c_ident"), (ones, "c_ones"), (upper, "c_upper"), (iota, "c_iota"),
                              (identb, "c_identb"), (maskA, "c_maskA"), (maskB, "c_maskB")):
                S.dma("sp", lambda e, v, dst=dst, name=name: e.dma_start(dst[:, :], d[name]))
            for dst, name in ((e4, "c_e4"), (eoff, "c_eoff"), (eoff1, "c_eoff1")):
                S.dma("sp", lambda e, v, dst=dst, name=name: e.dma_start(
                    dst[:, :, :], d[name].rearrange("p (t e) -> p t e", t=NT)))
            S.dma("sp", lambda e, v: e.dma_start(tokid[:, :], d["c_tokid"]))
            S.dma("sp", lambda e, v: e.dma_start(list_d, d["c_list"]))
            S.op("dve", lambda e, v: e.memset(carry[:, :], 0.0))
            S.op("dve", lambda e, v: e.memset(base[:, :], 0.0))
            S.op("dve", lambda e, v: e.memset(mhalf[:, :], -0.5))
            for dst in (QS, KS):
                S.dma("sp", lambda e, v, dst=dst: e.dma_start(dst[96:KB, :, :].rearrange("p h n -> p (h n)"), d["c_rows"]))
            S.op("pool", lambda e, v: e.memset(VA[:, :, :, :], 1.0))
            S.op("dve", lambda e, v: e.memset(smi[:, 0, 0:16], 2 * B * E0 * UROWS))
            for i in (4, 5):
                S.op("dve", lambda e, v, i=i: e.memset(PB[i][:, :], 0.0))
            z = S.op("dve", lambda e, v: e.memset(Z[:, :], 0.0))
            S.dma("sp", lambda e, v: e.dma_start(ye_d[NTOK:NTOK + 128, :], Z[:, :]), z)
            S.dma("sp", lambda e, v: e.dma_start(xw_d[NTOK:NTOK + 128, 0:C], Z[:, :]), z)
            S.dma("sp", lambda e, v: e.dma_start(xw_d[NTOK:NTOK + 128, C:C + E1], Z[:, 0:E1]), z)
            for i in range(3):
                load_w(S, i, lambda v, i=i: d["L0_attn_w_attn"][:, 256 * i:256 * i + 256])
            load_w(S, 3, lambda v: d["L0_attn_w_proj"])
            ba = d["L0_attn_b_attn"]
            for qk in range(2):
                S.dma("sp", lambda e, v, qk=qk: e.dma_start(
                    bq[:, qk, :], ba[256 * qk:256 * qk + 256].rearrange("(g p) -> p g", p=128),
                    allow_slow_non_contiguous=True))
            S.dma("sp", lambda e, v: e.dma_start(bv[0:1, :], ba[512:768].partition_broadcast(1)))
            S.dma("sp", lambda e, v: e.dma_start(bo[:, :], d["L0_attn_b_proj"].partition_broadcast(128)))
            S.dma("sp", lambda e, v: e.dma_start(rb[:, :], d["L0_ffn_router_b"].partition_broadcast(128)))
            S.dma("sp", lambda e, v: e.dma_start(
                rw[:, :, 0:E0], d["L0_ffn_router_w"].rearrange("(k p) n -> p k n", p=128)))
            return S.close()

        def tokens3(ap, b):
            return ap.rearrange("(b t p) c -> b p t c", b=B, p=128)[row(b), :, :, :].rearrange(
                "o p t c -> (o p) t c")

        def l0_attn():
            S = new()
            ld = S.dma("sp", lambda e, v: e.dma_start(XR[:, :, :], tokens3(d["L0_attn_x"], v["b"])))
            tln = layernorm(S, XR, [ld] * NT, XN, NT)
            txt = transposes(S, XN, tln, NT)
            ready, users = project_qk(S, NT, txt, None, True, None, lambda S: S.dma(
                "sp", lambda e, v: e.dma_start(KS[96:99, :, :], d["c_alibi"])))
            placed = place_rows(S)
            for ex in range(E0):
                S.dma("sp", lambda e, v, ex=ex: e.dma_start(
                    yg_d.rearrange("(u s p) c -> u p s c", u=B * E0, p=128)[
                        row(v["b"] * E0 + ex), :, :, :].rearrange("o p s c -> (o p) s c"),
                    Z[:, :].rearrange("p (o c) -> p o c", o=1).to_broadcast([128, UROWS // 128, C])))
            S.dma("sp", lambda e, v: e.dma_start(
                tokens3(ye_d[0:NTOK, :], v["b"]),
                Z[:, :].rearrange("p (o c) -> p o c", o=1).to_broadcast([128, NT, C])))
            last = attend(S, NT, True, 0.25, ready, users,
                          lambda bank, before: project_v(S, NT, txt, None, True, bank, before),
                          pfree=placed)
            txt = transposes(S, ON, [last] * NT, NT)

            def write(S, t, ps, mm):
                a = S.op("dve", lambda e, v: e.tensor_tensor(XR[:, t, :], ps, XR[:, t, :], ALU.add), mm)
                return S.op("dve", lambda e, v: e.tensor_tensor(XR[:, t, :], XR[:, t, :], bo[:, :], ALU.add), a)
            to = project_out(S, NT, txt, None, write)
            S.dma("sp", lambda e, v: e.dma_start(tokens3(x1_d, v["b"]), XR[:, :, :]), to)
            tln = layernorm(S, XR, to, NR, NT, placed)
            txt = transposes(S, NR, tln, NT, to)
            route0(S, txt, placed)
            return S.close()

        def place_rows(S):
            di = smi[:, 0, 0:16]
            return [S.dma("pool", lambda e, v, i=i: e.indirect_dma_start(
                out=xg_d, out_offset=bass.IndirectOffsetOnAxis(ap=di[:, i:i + 1], axis=0),
                in_=NR[:, i // 2, :], in_offset=None,
                bounds_check=B * E0 * UROWS - 1, oob_is_err=False)) for i in range(16)]

        def route0(S, txt, placed):
            lg = BANKS[0][:, 0:32].rearrange("p (t e) -> p t e", e=E0)
            for t in range(NT):
                for k in range(2):
                    mm = S.op("pe", lambda e, v, t=t, k=k: e.matmul(
                        BANKS[0][:, 4 * t:4 * t + 4], XT[:, k, 128 * t:128 * t + 128], rw[:, k, 0:E0],
                        start=(k == 0), stop=(k == 1)), txt, sig=(t == NT - 1 and k == 1))
            names = ["L", "t1", "oh1", "L2", "t2", "oh2", "ex", "mask", "pre", "pos", "tmp", "tot"]
            R = {nm: sm[:, i, :].rearrange("p (t e) -> p t e", e=E0) for i, nm in enumerate(names)}
            V = {nm: sm[:, 12 + i, 0:NT] for i, nm in enumerate(["m1", "x1", "m2", "x2", "s", "w1", "w2", "d1", "d2"])}
            out4 = sm[:, 22, :].rearrange("p (t e) -> p t e", e=4)

            def bc(ap):
                return ap.rearrange("p (t o) -> p t o", o=1).to_broadcast([128, NT, E0])

            def dv(fn, *w):
                dv.t = S.op("dve", fn, dv.t, *w)
                return dv.t
            dv.t = None
            dv(lambda e, v: e.tensor_tensor(R["L"], lg, rb[:, :].rearrange("p (o e) -> p o e", o=1).to_broadcast([128, NT, E0]), ALU.add), mm)
            lt = dv.t
            dv(lambda e, v: e.tensor_reduce(V["m1"], R["L"], AX.X, ALU.max))
            dv(lambda e, v: e.tensor_tensor(R["t1"], R["L"], bc(V["m1"]), ALU.is_equal))
            dv(lambda e, v: e.tensor_tensor(R["t1"], R["t1"], e4[:, :, :], ALU.mult))
            dv(lambda e, v: e.tensor_reduce(V["x1"], R["t1"], AX.X, ALU.max))
            dv(lambda e, v: e.tensor_tensor(R["oh1"], R["t1"], bc(V["x1"]), ALU.is_equal))
            dv(lambda e, v: e.scalar_tensor_tensor(R["L2"], R["oh1"], NEG, R["L"], ALU.mult, ALU.add))
            dv(lambda e, v: e.tensor_reduce(V["m2"], R["L2"], AX.X, ALU.max))
            dv(lambda e, v: e.tensor_tensor(R["t2"], R["L2"], bc(V["m2"]), ALU.is_equal))
            dv(lambda e, v: e.tensor_tensor(R["t2"], R["t2"], e4[:, :, :], ALU.mult))
            dv(lambda e, v: e.tensor_reduce(V["x2"], R["t2"], AX.X, ALU.max))
            dv(lambda e, v: e.tensor_tensor(R["oh2"], R["t2"], bc(V["x2"]), ALU.is_equal))
            dv(lambda e, v: e.tensor_tensor(R["mask"], R["oh1"], R["oh2"], ALU.add))
            tm = dv.t
            dv(lambda e, v: e.tensor_tensor(R["ex"], R["L"], bc(V["m1"]), ALU.subtract))
            ta = S.op("act", lambda e, v: e.activation(R["ex"], R["ex"], ACT.Exp), dv.t)
            dv(lambda e, v: e.tensor_reduce(V["s"], R["ex"], AX.X, ALU.add), ta)
            dv(lambda e, v: e.reciprocal(V["s"], V["s"]))
            dv(lambda e, v: e.tensor_tensor(R["ex"], R["ex"], bc(V["s"]), ALU.mult))
            dv(lambda e, v: e.tensor_tensor(R["tmp"], R["ex"], R["oh1"], ALU.mult))
            dv(lambda e, v: e.tensor_reduce(out4[:, :, 2], R["tmp"], AX.X, ALU.add))
            dv(lambda e, v: e.tensor_tensor(R["tmp"], R["ex"], R["oh2"], ALU.mult))
            dv(lambda e, v: e.tensor_reduce(out4[:, :, 3], R["tmp"], AX.X, ALU.add))
            p0, p1 = BANKS[4][:, 0:32], BANKS[5][:, 0:32]
            S.op("pe", lambda e, v: e.matmul(p0, upper[:, :], sm[:, 7, :], start=True, stop=True), tm, sig=False)
            mm = S.op("pe", lambda e, v: e.matmul(p1, ones[:, :], sm[:, 7, :], start=True, stop=True))
            dv(lambda e, v: e.tensor_copy(sm[:, 11, :], p1), mm)
            dv(lambda e, v: e.memset(R["pre"][:, 0, :], 0.0))
            for t in range(1, NT):
                dv(lambda e, v, t=t: e.tensor_tensor(
                    R["pre"][:, t, :], R["pre"][:, t - 1, :], R["tot"][:, t - 1, :], ALU.add))
            nf = sm[:, 21, 0:E0]
            dv(lambda e, v: e.tensor_tensor(nf, R["pre"][:, NT - 1, :], R["tot"][:, NT - 1, :], ALU.add))
            tn = dv.t
            dv(lambda e, v: e.tensor_tensor(sm[:, 9, :], p0, sm[:, 8, :], ALU.add))
            dv(lambda e, v: e.tensor_tensor(R["pos"], R["pos"], eoff[:, :, :], ALU.add))
            di = smi[:, 0, 0:16].rearrange("p (t k) -> p t k", k=2)
            for k, oh in ((0, "oh1"), (1, "oh2")):
                dd = V["d1"] if k == 0 else V["d2"]
                dv(lambda e, v, oh=oh: e.tensor_tensor(R["tmp"], R["pos"], R[oh], ALU.mult))
                dv(lambda e, v, dd=dd: e.tensor_reduce(dd, R["tmp"], AX.X, ALU.add))
                dv(lambda e, v, dd=dd: e.tensor_scalar(dd, dd, base[:, 0:1], None, ALU.add))
                dv(lambda e, v, dd=dd, k=k: e.tensor_copy(di[:, :, k], dd), placed)
                dv(lambda e, v, k=k: e.tensor_copy(out4.bitcast(I32)[:, :, k], di[:, :, k]))
            ti = dv.t
            dv(lambda e, v: e.tensor_scalar(base[:, :], base[:, :], float(E0 * UROWS), None, ALU.add))
            ni = smi[0:1, 2, 0:E0]
            tcn = smi[0:1, 3, 0:E0]
            dv(lambda e, v: e.tensor_copy(ni, nf[0:1, :]))
            dv(lambda e, v: e.tensor_scalar(sm[0:1, 23, 0:E0], nf[0:1, :], 127.0, None, ALU.add))
            dv(lambda e, v: e.tensor_copy(tcn, sm[0:1, 23, 0:E0]))
            dv(lambda e, v: e.tensor_scalar(tcn, tcn, 7, None, ALU.logical_shift_right))
            tc_ = dv.t
            mkb = PH[0:1, :, :, :].rearrange("p a b n -> p (a b) n")
            for ex in range(E0):
                dv(lambda e, v, ex=ex: e.tensor_scalar(
                    mkb[:, ex, :], iota[0:1, :], nf[0:1, ex:ex + 1], NEG, ALU.is_ge, ALU.mult))
            for ex in range(E0):
                S.dma("sp", lambda e, v, ex=ex: e.dma_start(mk_d[row(v["b"] * E0 + ex), :], mkb[:, ex, :]), dv.t)
                S.dma("sp", lambda e, v, ex=ex: e.dma_start(cnt_d[row(v["b"] * E0 + ex), :], tcn[:, ex:ex + 1]), tc_)
            S.dma("sp", lambda e, v: e.dma_start(rt_d[row(v["b"]), :, :].rearrange("o p n -> (o p) n"), sm[:, 22, :]), ti)
            zt = S.op("dve", lambda e, v: e.memset(PB[0][:, 0:C], 0.0))
            for ex in range(E0):
                def pad(e, v, ex=ex):
                    r = e.value_load(ni[0:1, ex:ex + 1], min_val=0, max_val=T)
                    return e.dma_start(xg_d[bass.ds(r + (v["b"] * E0 + ex) * UROWS, 128), :], PB[0][:, 0:C])
                S.dma("sp", pad, zt, tc_)

        def pre_ffn():
            S = new()
            place_rows(S)
            z = S.op("dve", lambda e, v: e.memset(KS[96:99, :, :], 0.0))
            S.op("dve", lambda e, v: e.memset(cnt[:, B * E0:B * E0 + 1], 0))
            S.dma("sp", lambda e, v: e.dma_start(cnt[:, 0:B * E0], cnt_d.rearrange("a o -> o a"),
                                                 allow_slow_non_contiguous=True))
            return S.close()

        def mask_row(S, g, n, u):
            return S.dma("sp", lambda e, v: e.dma_start(
                KS[96:97, 8 * g:8 * g + 8, 0:n],
                mk_d[row(v[u]), 0:n].rearrange("o (h n) -> o h n", h=1).to_broadcast([1, 8, n])))

        def front(nt):
            F = Section(fsems, fdma)
            n = 128 * nt
            lds = []
            for t in range(nt):
                lds.append(F.dma("sp", lambda e, v, t=t: e.dma_start(
                    XR[:, t, :], xg_d[bass.ds(v["nu"] * UROWS + 128 * t, 128), :])))
            wt = []
            for i, nm in enumerate(("wq", "wk", "wv")):
                wt.append(load_w(F, i, lambda v, nm=nm: d["L0_ffn_" + nm][row(v["nex"]), :, :].rearrange("o a b -> (o a) b")))
            for qk, nm in enumerate(("bq", "bk")):
                wt.append(F.dma("sp", lambda e, v, qk=qk, nm=nm: e.dma_start(
                    bq[:, qk, :], d["L0_ffn_" + nm][row(v["nex"]), :].rearrange("o (g p) -> p (o g)", p=128),
                    allow_slow_non_contiguous=True)))
            F.dma("sp", lambda e, v: e.dma_start(bv[:, :], d["L0_ffn_bv"][row(v["nex"]), :]))
            txt = transposes(F, XR, lds, nt)
            ready, users = project_qk(F, nt, txt, wt, True, None, lambda F: mask_row(F, 0, n, "nu"),
                                      banks=BANKS[0:4], halves=(0,))
            F.wait("pe", users)
            return F.close()

        def place_front(S):
            for eng in ENGINES:
                def put(e, v, eng=eng):
                    for nt in range(1, NT + 1):
                        with e.If(v["next"] == nt):
                            for f in fronts[nt].q[eng]:
                                f(e, v)
                if eng != "pool":
                    S.q[eng].append(put)

        def first_front():
            S = new()
            place_front(S)
            return S.close()

        def ffn_unit(nt):
            S = new()
            n = 128 * nt
            wo = load_w(S, 3, lambda v: d["L0_ffn_wo"][row(v["ex"]), :, :].rearrange("o a b -> (o a) b"))
            lbo = S.dma("sp", lambda e, v: e.dma_start(bo[:, :], d["L0_ffn_bo"][row(v["ex"]), :].to_broadcast([128, C])))
            half = [mask_row(S, 1, n, "u")]
            for qk in range(2):
                half += load_half(S, qk, 1, n, [None] * 3)

            def inject(pr, fence):
                S.wait("pe", pr)
                vt = [fence["v"][t] for t in range(nt)]
                for eng in ("act", "dve", "sp"):
                    S.wait(eng, vt)
                S.wait("sp", fence["heads"])
                place_front(S)

            last = attend(S, nt, False, 0.5, [None, None, half, half], [None] * 8,
                          lambda bank, before: project_v(S, nt, None, None, True, bank, before), inject)
            on_t = transposes(S, ON, [last] * nt, nt, dst=QF)

            def write(S, t, ps, mm):
                return S.op("dve", lambda e, v: e.tensor_tensor(XR[:, t, :], ps, bo[:, :], ALU.add), mm, lbo)
            to = project_out(S, nt, on_t, wo, write, src=QF)
            for t in range(nt):
                S.dma("sp", lambda e, v, t=t: e.dma_start(
                    yg_d[bass.ds(v["u"] * UROWS + 128 * t, 128), :], XR[:, t, :]), to[t])
            return S.close()

        def pre_l1():
            S = new()
            z = S.op("dve", lambda e, v: e.memset(KS[96:99, :, :], 0.0))
            S.op("dve", lambda e, v: e.memset(tlist[:, :], 0))
            S.op("dve", lambda e, v: e.memset(dlist[:, :], 2 * E1 * CAP))
            S.dma("sp", lambda e, v: e.dma_start(rt_d[B:B + 1, :, :], rt_d[B - 1:B, :, :]))
            gather_rows(S, row_indices(S, lambda v: 0))
            for i, nm in enumerate(("w1_q", "w1_k", "w1_v", "w1_o", "w1_qs", "w1_ks")):
                load_w(S, i, lambda v, nm=nm: d[nm])
            S.dma("sp", lambda e, v: e.dma_start(rw[:, :, :], d["L1_ffn_gate_w"].rearrange("(k p) n -> p k n", p=128)))
            return S.close()

        def expert_rows(t, k):
            i = 2 * t + k
            if i < 8:
                return QF[:, i // 4, 256 * (i % 4):256 * (i % 4) + 256]
            return PH[:, :, :, :].rearrange("p a b n -> p (a b n)").bitcast(F32)[:, 256 * (i - 8):256 * (i - 7)]

        def row_indices(S, b):
            lr = S.dma("sp", lambda e, v: e.dma_start(
                sm[:, 23, :], rt_d[row(b(v)), :, :].rearrange("o p n -> (o p) n")))
            di = smi[:, 1, 0:16].rearrange("p (t k) -> p t k", k=2)
            return S.op("dve", lambda e, v: e.tensor_copy(
                di, sm[:, 23, :].rearrange("p (t e) -> p t e", e=4).bitcast(I32)[:, :, 0:2]), lr)

        def gather_rows(S, ti, *free):
            di = smi[:, 1, 0:16].rearrange("p (t k) -> p t k", k=2)
            for t in range(NT):
                for k in range(2):
                    S.dma("pool", lambda e, v, t=t, k=k: e.indirect_dma_start(
                        out=expert_rows(t, k), out_offset=None, in_=yg_d,
                        in_offset=bass.IndirectOffsetOnAxis(ap=di[:, t, k:k + 1], axis=0)), ti, *free)

        def l1_attn():
            S = new()
            lr = S.dma("sp", lambda e, v: e.dma_start(
                sm[:, 22, :], rt_d[row(v["b"]), :, :].rearrange("o p n -> (o p) n")))
            ld = [S.dma("sp", lambda e, v, t=t: e.dma_start(
                XR[:, t:t + 2, :], tokens3(x1_d, v["b"])[:, t:t + 2, :])) for t in range(0, NT, 2)]
            tc = [S.dma("sp", lambda e, v: e.dma_start(cosT[:, :], d["c_cos"])),
                  S.dma("sp", lambda e, v: e.dma_start(sinT[:, :], d["c_sin"]))]
            out4 = sm[:, 22, :].rearrange("p (t e) -> p t e", e=4)
            tx = []
            for t in range(NT):
                a = None
                for k in range(2):
                    a = S.op("dve", lambda e, v, t=t, k=k: e.scalar_tensor_tensor(
                        XR[:, t, :], expert_rows(t, k), out4[:, t, 2 + k:3 + k], XR[:, t, :],
                        ALU.mult, ALU.add), ld[t // 2], lr, a)
                tx.append(a)
            tln = layernorm(S, XR, tx, XN, NT)
            ti = row_indices(S, lambda v: v["b"] + 1)
            placed = place_tokens(S)
            txt = transposes(S, XN, tln, NT)
            ready, users = project_qk(S, NT, txt, None, False, tc, lambda S: None)
            gather_rows(S, ti, ready)
            last = attend(S, NT, True, 0.25, ready, users,
                          lambda bank, before: project_v(S, NT, txt, None, False, bank, before))
            txt = transposes(S, ON, [last] * NT, NT)

            def write(S, t, ps, mm):
                return S.op("dve", lambda e, v: e.tensor_tensor(XR[:, t, :], ps, XR[:, t, :], ALU.add), mm)
            to = project_out(S, NT, txt, None, write)
            S.dma("sp", lambda e, v: e.dma_start(tokens3(x3_d, v["b"]), XR[:, :, :]), to)
            tln = layernorm(S, XR, to, XN, NT, txt)
            txt = transposes(S, XN, tln, NT, to)
            S.dma("sp", lambda e, v: e.dma_start(tokens3(xw_d[0:NTOK, :], v["b"])[:, :, 0:C], XN[:, :, :]), tln)
            route1(S, txt, placed)
            return S.close()

        def route1(S, txt, free):
            R = {nm: PB[i][:, 0:512].rearrange("p (t e) -> p t e", e=E1)
                 for i, nm in enumerate(["L", "rep", "mask", "ex", "pre", "pos", "w"])}
            sml = PB[7]
            top = sml[:, 0:64].rearrange("p (t k) -> p t k", k=8)
            v8 = sml[:, 64:128].rearrange("p (t k) -> p t k", k=8)
            s1 = sml[:, 128:136]
            s2 = sml[:, 136:144]

            def bc(ap):
                return ap.rearrange("p (t o) -> p t o", o=1).to_broadcast([128, NT, E1])
            for t in range(NT):
                for k in range(2):
                    mm = S.op("pe", lambda e, v, t=t, k=k: e.matmul(
                        BANKS[0][:, E1 * t:E1 * t + E1], XT[:, k, 128 * t:128 * t + 128], rw[:, k, :],
                        start=(k == 0), stop=(k == 1)), txt, sig=(t == NT - 1 and k == 1))

            def dv(fn, *w):
                dv.t = S.op("dve", fn, dv.t, *w)
                return dv.t
            dv.t = None
            dv(lambda e, v: e.tensor_copy(PB[0][:, 0:512], BANKS[0]), mm)
            for t in range(NT):
                tt = S.op("dve", lambda e, v, t=t: e.max(top[:, t, :], R["L"][:, t, :]), dv.t)
            for t in range(NT):
                t2 = S.op("dve", lambda e, v, t=t: e.match_replace(R["rep"][:, t, :], top[:, t, :], R["L"][:, t, :], NEG), tt)
            dv.t = t2
            dv(lambda e, v: e.tensor_tensor(R["mask"], R["rep"], R["L"], ALU.not_equal))
            tm = dv.t
            dv(lambda e, v: e.tensor_tensor(R["ex"], R["L"], bc(top[:, :, 0:1].rearrange("p t o -> p (t o)")), ALU.subtract))
            ta = S.op("act", lambda e, v: e.activation(R["ex"], R["ex"], ACT.Exp), dv.t)
            dv(lambda e, v: e.tensor_copy(R["pre"][:, 0, :], carry[:, :]))
            for t in range(1, NT):
                dv(lambda e, v, t=t: e.tensor_tensor(
                    R["pre"][:, t, :], R["pre"][:, t - 1, :], R["mask"][:, t - 1, :], ALU.add))
            tp = dv.t
            dv(lambda e, v: e.tensor_tensor(carry[:, :], R["pre"][:, NT - 1, :], R["mask"][:, NT - 1, :], ALU.add))
            S.op("pe", lambda e, v: e.matmul(BANKS[4], upper[:, :], PB[2][:, 0:512], start=True, stop=False), tm, sig=False)
            mm = S.op("pe", lambda e, v: e.matmul(BANKS[4], ones[:, :], PB[4][:, 0:512], start=False, stop=True), tp)
            dv(lambda e, v: e.tensor_reduce(s1, R["ex"], AX.X, ALU.add), ta)
            dv(lambda e, v: e.reciprocal(s1, s1))
            dv(lambda e, v: e.tensor_tensor(R["ex"], R["ex"], bc(s1), ALU.mult))
            dv(lambda e, v: e.tensor_tensor(R["ex"], R["ex"], R["mask"], ALU.mult))
            dv(lambda e, v: e.tensor_reduce(s2, R["ex"], AX.X, ALU.add))
            dv(lambda e, v: e.reciprocal(s2, s2))
            dv(lambda e, v: e.tensor_tensor(R["w"], R["ex"], bc(s2), ALU.mult))
            S.dma("sp", lambda e, v: e.dma_start(tokens3(xw_d[0:NTOK, :], v["b"])[:, :, C:C + E1], R["w"]), dv.t)
            dv(lambda e, v: e.tensor_copy(PB[5][:, 0:512], BANKS[4]), mm)
            dv(lambda e, v: e.scalar_tensor_tensor(R["mask"], R["pos"], float(CAP), R["mask"], ALU.is_lt, ALU.mult))
            dv(lambda e, v: e.scalar_tensor_tensor(
                R["pos"], R["pos"], -float(E1), eoff1[:, :, :], ALU.mult, ALU.add))
            dv(lambda e, v: e.tensor_tensor(R["pos"], R["pos"], R["mask"], ALU.mult))
            for t in range(NT):
                tt = S.op("dve", lambda e, v, t=t: e.max(v8[:, t, :], R["pos"][:, t, :]), dv.t)
            dv.t = tt
            dv(lambda e, v: e.tensor_scalar(sml[:, 192:256], sml[:, 64:128], -1.0, 16384.0, ALU.mult, ALU.add))
            dv(lambda e, v: e.tensor_copy(dlist[:, :], sml[:, 192:256]), free)
            dv(lambda e, v: e.tensor_copy(tlist[:, :], tokid[:, :]))
            dv(lambda e, v: e.tensor_scalar(tokid[:, :], tokid[:, :], float(T), None, ALU.add))

        def place_tokens(S):
            return [S.dma("pool", lambda e, v, i=i: e.indirect_dma_start(
                out=list_d, out_offset=bass.IndirectOffsetOnAxis(ap=dlist[:, i:i + 1], axis=0),
                in_=tlist[:, i // 8:i // 8 + 1], in_offset=None, bounds_check=E1 * CAP - 1, oob_is_err=False))
                for i in range(64)]

        def last_layer():
            S = new()
            wgu = QF
            wsd = W[:, 0:2, :, :].rearrange("p a k n -> p (a k) n")
            lw = [S.dma("sp", lambda e, v: e.dma_start(
                wgu[:, :, :], d["L1_ffn_shared_gate_up_w"].rearrange("(k p) n -> p k n", p=128))),
                S.dma("sp", lambda e, v: e.dma_start(
                    wsd, d["L1_ffn_shared_down_w"].rearrange("(k p) n -> p k n", p=128))),
                S.dma("sp", lambda e, v: e.dma_start(
                    rw[:, :, 0:1], d["L1_ffn_shared_gate_w"].rearrange("(k p) n -> p k n", p=128),
                    allow_slow_non_contiguous=True))]
            xw_b = xw_d[0:NTOK, 0:C].rearrange("(b t p) c -> b p t c", b=B, p=128)
            x3_b = x3_d.rearrange("(b t p) c -> b p t c", b=B, p=128)
            ye_b = ye_d[0:NTOK, :].rearrange("(b t p) c -> b p t c", b=B, p=128)
            out_b = out.rearrange("b (t p) c -> b p t c", p=128)
            placed = place_tokens(S)
            AT = [XR[:, 2 * m:2 * m + 2, :].rearrange("p a c -> p (a c)") for m in range(4)]
            VF = VA[:, :, :, :].rearrange("p t h d -> p (t h d)")
            WF = W[:, 2:6, :, :].rearrange("p a k n -> p (a k n)")
            PF = PH[:, :, :, :].rearrange("p a b n -> p (a b n)").bitcast(F32)
            NW, NX = 5, 6
            EW = [(VF[:, 768 * i:768 * i + 512].rearrange("p (k n) -> p k n", k=2),
                   VF[:, 768 * i + 512:768 * i + 768]) for i in range(NW)]
            XE = [WF[:, 320 * i:320 * i + 320] for i in range(NX)]
            YO = [PF[:, 1536 + 256 * i:1792 + 256 * i] for i in range(3)]
            XTe = [PF[:, 256 * i:256 * i + 256] for i in range(4)]
            ATe = [PF[:, 1024 + 128 * i:1152 + 128 * i] for i in range(4)]

            def sh(t):
                return PB[t // 4][:, 256 * (t % 4):256 * (t % 4) + 256]

            st = {"gu": [None, None], "xn": None, "xt": None, "at": None, "down": None, "gate": None}
            sh_done = {}

            def batch_head(b):
                l3 = [S.dma("sp", lambda e, v, h=h: e.dma_start(
                    PB[2 * b + h][:, :].rearrange("p (t c) -> p t c", c=C), x3_b[b, :, 4 * h:4 * h + 4, :]))
                    for h in range(2)]
                ln = S.dma("sp", lambda e, v: e.dma_start(XN[:, :, :], xw_b[b]), st["xn"])
                txt = transposes(S, XN, [ln] * NT, NT, st["gu"], st["down"])
                st["xn"] = txt
                for t in range(NT):
                    for k in range(2):
                        mm = S.op("pe", lambda e, v, t=t, k=k: e.matmul(
                            BANKS[4][:, t:t + 1], XT[:, k, 128 * t:128 * t + 128], rw[:, k, 0:1],
                            start=(k == 0), stop=(k == 1)), txt, lw, st["down"],
                            sig=(k == 1 and t == NT - 1))
                st["gate"] = S.op("act", lambda e, v: e.activation(rstd[:, :], BANKS[4][:, 0:NT], ACT.Sigmoid),
                                  mm, st["down"])
                st["l3"] = l3
                st["txt"] = txt

            def gate_up(b, c, m):
                pg, pu = BANKS[2 * (m % 2)], BANKS[2 * (m % 2) + 1]
                for dst, off in ((pg, 128 * m), (pu, IS + 128 * m)):
                    for k in range(2):
                        mm = S.op("pe", lambda e, v, dst=dst, off=off, k=k: e.matmul(
                            dst, wgu[:, k, off:off + 128], XT[:, k, 512 * c:512 * c + 512],
                            start=(k == 0), stop=(k == 1)), st["gu"][m % 2], st["txt"], lw,
                            sig=(k == 1 and dst is pu))
                s1 = S.op("act", lambda e, v: e.activation(AT[m], pg, ACT.Sigmoid), mm, st["at"])
                s2 = S.op("dve", lambda e, v: e.tensor_tensor(AT[m], AT[m], pg, ALU.mult), s1)
                st["gu"][m % 2] = S.op("dve", lambda e, v: e.tensor_tensor(AT[m], AT[m], pu, ALU.mult), s2)

            def down(b, c, t):
                tile = NT * b + 4 * c + t
                for k in range(4):
                    mm = S.op("pe", lambda e, v, k=k: e.matmul(
                        BANKS[4][:, 0:C], AT[k][:, 128 * t:128 * t + 128], wsd[:, k, :],
                        start=(k == 0), stop=(k == 3)), st["gu"], st["down"], st["gate"], sig=(k == 3))
                st["down"] = S.op("dve", lambda e, v: e.scalar_tensor_tensor(
                    sh(tile), BANKS[4][:, 0:C], rstd[:, 4 * c + t:4 * c + t + 1], sh(tile),
                    ALU.mult, ALU.add), mm, st["gate"], st["l3"])
                if t == 3:
                    st["at"] = mm
                sh_done[b] = st["down"]

            def pieces(b):
                out_ = [lambda: batch_head(b)]
                for c in range(2):
                    out_ += [lambda c=c, m=m: gate_up(b, c, m) for m in range(4)]
                    out_ += [lambda c=c, t=t: down(b, c, t) for t in range(4)]
                return out_

            ex = {}
            ux = {"pt": None, "pg": None, "py": None, "acc": None}

            def weights(x):
                if x >= E1:
                    return
                gu, dn = EW[x % NW]
                old = ex.get(x - NW, {}).get("down")
                ex.setdefault(x, {})["w"] = [
                    S.dma("sp", lambda e, v: e.dma_start(
                        gu, d["L1_ffn_expert_gate_up_w"][x].rearrange("(k p) n -> p k n", p=128)), old),
                    S.dma("sp", lambda e, v: e.dma_start(dn, d["L1_ffn_expert_down_w"][x]), old)]

            def gather(x):
                if x >= E1:
                    return
                old = ex.get(x - NX, {})
                ex.setdefault(x, {})["g"] = S.dma("pool", lambda e, v: e.indirect_dma_start(
                    out=XE[x % NX], out_offset=None, in_=xw_d,
                    in_offset=bass.IndirectOffsetOnAxis(ap=lists[:, x:x + 1], axis=0)), ll,
                    old.get("y"))

            def turn(x):
                q = ex[x]
                for k in range(2):
                    mm = S.op("pe", lambda e, v, k=k: e.transpose(
                        BANKS[6][:, 128 * k:128 * k + 128], XE[x % NX][:, 128 * k:128 * k + 128], ident[:, :]),
                        q["g"], ux["pt"], sig=(k == 1))
                q["xt"] = ux["pt"] = S.op("act", lambda e, v: e.activation(
                    XTe[x % 4], BANKS[6][:, 0:256], ACT.Copy), mm)

            def up(x):
                q = ex[x]
                gu, dn = EW[x % NW]
                for m in range(2):
                    for k in range(2):
                        mm = S.op("pe", lambda e, v, k=k, m=m: e.matmul(
                            BANKS[7][:, 128 * m:128 * m + 128], gu[:, k, 128 * m:128 * m + 128],
                            XTe[x % 4][:, 128 * k:128 * k + 128], start=(k == 0), stop=(k == 1)),
                            q["xt"], q["w"], ux["pg"], sig=(k == 1 and m == 1))
                at = ATe[x % 4]
                s1 = S.op("act", lambda e, v: e.activation(at, BANKS[7][:, 0:128], ACT.Sigmoid), mm)
                s2 = S.op("dve", lambda e, v: e.tensor_tensor(at, at, BANKS[7][:, 0:128], ALU.mult), s1)
                q["at"] = ux["pg"] = S.op("dve", lambda e, v: e.tensor_tensor(
                    at, at, BANKS[7][:, 128:256], ALU.mult), s2)

            def down_x(x):
                q = ex[x]
                gu, dn = EW[x % NW]
                mm = S.op("pe", lambda e, v: e.matmul(
                    BANKS[5][:, 0:C], ATe[x % 4], dn, start=True, stop=True), q["at"], q["w"], ux["py"])
                q["down"] = mm
                q["y"] = ux["py"] = S.op("dve", lambda e, v: e.tensor_scalar(
                    YO[x % 3], BANKS[5][:, 0:C], XE[x % NX][:, C + x:C + x + 1], None, ALU.mult), mm,
                    ex.get(x - 3, {}).get("acc"))

            def add(x):
                ux["acc"] = ex[x]["acc"] = S.dma("pool", lambda e, v: e.indirect_dma_start(
                    out=ye_d, out_offset=bass.IndirectOffsetOnAxis(ap=lists[:, x:x + 1], axis=0),
                    in_=YO[x % 3], in_offset=None, compute_op=ALU.add), ex[x]["y"], ux["acc"])

            for x in range(NW - 1):
                weights(x)
            first = pieces(0) + pieces(1)
            for f in first[:len(first) // 2]:
                f()
            ll = S.dma("sp", lambda e, v: e.dma_start(
                lists[:, :], list_d.rearrange("(s e) o -> s (e o)", e=E1)), placed)
            for x in range(2):
                gather(x)
            for f in first[len(first) // 2:]:
                f()
            rest = pieces(2) + pieces(3)
            n_rest = len(rest)
            for i in range(E1 + 3):
                if i < E1:
                    turn(i)
                    gather(i + 2)
                if 0 <= i - 1 < E1:
                    up(i - 1)
                if 0 <= i - 2 < E1:
                    down_x(i - 2)
                    weights(i - 2 + NW)
                if 0 <= i - 2 < E1:
                    add(i - 2)
                if i == 0:
                    weights(NW - 1)
                while rest and (n_rest - len(rest)) < n_rest * (i + 1) / E1:
                    rest.pop(0)()
            buf = [XN, XR] + [x[:, :, :].rearrange("p a n -> p (a n)").rearrange("p (t c) -> p t c", c=C)
                              for x in (QF, XT)]
            free = [st["xn"], st["at"], st["gu"], st["gu"]]
            ly = {}
            for b in range(B):
                for h in range(2):
                    ly[b, h] = S.dma("sp", lambda e, v, b=b, h=h: e.dma_start(
                        buf[b][:, 4 * h:4 * h + 4, :], ye_b[b, :, 4 * h:4 * h + 4, :]), ux["acc"], free[b])
            for b in range(B):
                for h in range(2):
                    tk = S.op("dve", lambda e, v, b=b, h=h: e.tensor_tensor(
                        PB[2 * b + h][:, :], PB[2 * b + h][:, :],
                        buf[b][:, 4 * h:4 * h + 4, :].rearrange("p t c -> p (t c)"), ALU.add), ly[b, h], sh_done[b])
                    S.dma("sp", lambda e, v, b=b, h=h: e.dma_start(
                        out_b[b, :, 4 * h:4 * h + 4, :], PB[2 * b + h][:, :].rearrange("p (t c) -> p t c", c=C)), tk)
            return S.close()


        fronts = {nt: front(nt) for nt in range(1, NT + 1)}
        secs = {"constants": constants(), "l0_attn": l0_attn(), "pre_ffn": pre_ffn(),
                "pre_l1": pre_l1(), "l1_attn": l1_attn(), "last_layer": last_layer()}
        for nt in range(1, NT + 1):
            secs[f"ffn{nt}"] = ffn_unit(nt)
        secs["first_front"] = first_front()

        def emit(key, e):
            def barrier(raised=attn_sems):
                if key == "sp":
                    e.wait_ge(A1, 4)
                    for s in raised:
                        e.sem_clear(s)
                    e.sem_clear(A1)
                    e.sem_clear(B2)
                    e.sem_inc(A2, 1)
                    e.wait_ge(B1, 4)
                    e.sem_clear(A2)
                    e.sem_clear(B1)
                    e.sem_inc(B2, 1)
                else:
                    if key == "pool":
                        e.dma_reset()
                    e.drain().then_inc(A1, 1)
                    e.wait_ge(A2, 1)
                    e.drain().then_inc(B1, 1)
                    e.wait_ge(B2, 1)

            def run(name, env):
                for f in secs[name].q[key]:
                    f(e, env)

            run("constants", {})
            barrier()
            with e.Fori(0, B) as b:
                run("l0_attn", {"b": b})
                barrier()
            run("pre_ffn", {})
            barrier()
            run("first_front", {"nu": 0, "nex": 0, "next": e.value_load(cnt[0:1, 0:1], min_val=0, max_val=NT)})
            barrier(unit_sems)
            with e.Fori(0, B) as b:
                with e.Fori(0, E0) as ex:
                    u = b * E0 + ex
                    nex = (ex + 1) % E0
                    tiles = e.value_load(cnt[0:1, bass.ds(u, 1)], min_val=0, max_val=NT)
                    after = e.value_load(cnt[0:1, bass.ds(u + 1, 1)], min_val=0, max_val=NT)
                    env = {"b": b, "ex": ex, "u": u, "nu": u + 1, "nex": nex, "next": after}
                    for nt in range(1, NT + 1):
                        with e.If(tiles == nt):
                            run(f"ffn{nt}", env)
                    with e.If(tiles == 0):
                        run("first_front", env)
                    barrier(unit_sems)
            run("pre_l1", {})
            barrier()
            with e.Fori(0, B) as b:
                run("l1_attn", {"b": b})
                barrier()
            run("last_layer", {})
            barrier()

        block = ctx.enter_context(nc.Block())

        @block.sync
        def _(e):
            emit("sp", e)

        @block.tensor
        def _(e):
            emit("pe", e)

        @block.scalar
        def _(e):
            emit("act", e)

        @block.vector
        def _(e):
            emit("dve", e)

        @block.gpsimd
        def _(e):
            emit("pool", e)


def shape_constants():
    bf = mybir.dt.np(BF16)
    f = np.float32
    k = {}
    k["c_ident"] = np.eye(128, dtype=f)
    k["c_identb"] = np.eye(128, dtype=f).astype(bf)
    k["c_ones"] = np.ones((128, 128), f)
    k["c_upper"] = np.triu(np.ones((128, 128), f), 1)
    k["c_iota"] = np.arange(T, dtype=f)[None, :]
    mask = np.where(np.triu(np.ones((128, 128)), 1) > 0, f(NEG), f(0)).astype(f)
    k["c_maskA"] = mask.astype(bf)
    k["c_maskB"] = np.ascontiguousarray(mask.T).astype(bf)
    k["c_e4"] = np.tile(np.arange(E0, 0, -1, dtype=f), (128, NT))
    k["c_eoff"] = np.tile(np.arange(E0, dtype=f) * UROWS, (128, NT))
    k["c_eoff1"] = np.tile(f(16384) - np.arange(E1, dtype=f), (128, NT))
    k["c_tokid"] = (np.arange(NT)[None, :] * 128 + np.arange(128)[:, None]).astype(f)
    k["c_list"] = (NTOK + np.arange(E1 * CAP) // E1).astype(np.int32)[:, None]
    slopes = (f(2.0) ** (f(-0.5) * np.arange(1, H + 1, dtype=f))).astype(f)
    al = (slopes[:, None] * np.arange(T, dtype=f)[None, :]).astype(f) * f(4.0)
    parts = []
    r = al
    for _ in range(3):
        p = r.astype(bf)
        parts.append(p)
        r = (r - p.astype(f)).astype(f)
    k["c_alibi"] = np.stack(parts)
    k["c_rows"] = np.ones((KB - 96, H * T), dtype=bf)
    half = D // 2
    inv = (f(10000.0) ** (-np.arange(0, half, dtype=f) * f(2.0) / f(D))).astype(f)
    ang = np.arange(T, dtype=f)[:, None] * inv[None, :]
    cos, sin = np.cos(ang).astype(f), np.sin(ang).astype(f)
    ct = np.repeat(cos.T, 2, axis=0)
    sn = np.repeat(sin.T, 2, axis=0)
    sn[0::2] *= f(-1)
    k["c_cos"] = np.ascontiguousarray(np.tile(ct, (8, 1)))
    k["c_sin"] = np.ascontiguousarray(np.tile(sn, (8, 1)))
    return k


def kernel(**inputs):
    import concourse.bacc as bacc
    from concourse.bass_utils import run_bass_kernel_spmd

    nc = bacc.Bacc("TRN2", target_bir_lowering=False, num_devices=1)
    a = {n: np.ascontiguousarray(inputs[n]) for n in inputs}
    a["L0_attn_x"] = a["L0_attn_x"].reshape(NTOK, C)
    swap = np.arange(C).reshape(-1, 2)[:, ::-1].reshape(-1)
    for nm, src in (("q", "Wq"), ("k", "Wk"), ("v", "Wv"), ("o", "Wo")):
        a["w1_" + nm] = np.ascontiguousarray(a.pop("L1_attn_" + src).T)
    for nm in ("q", "k"):
        a[f"w1_{nm}s"] = np.ascontiguousarray(a["w1_" + nm][:, swap])
    a.update(shape_constants())
    arrays, d = {}, {}
    for n, x in a.items():
        arrays["in_" + n] = x
        d[n] = nc.dram_tensor("in_" + n, x.shape, mybir.dt.from_np(x.dtype), kind="ExternalInput").ap()
    out = nc.dram_tensor("out_0", (B, T, C), F32, kind="ExternalOutput").ap()
    build(nc, d, out)
    r = run_bass_kernel_spmd(nc, [arrays], core_ids=[0])
    return r.results[0]["out_0"]
```
